# Optimizing a Trainium2 kernel written in Bass

```python
import numpy as np
import jax
import jax.numpy as jnp

def _softmax(x, axis=-1):
    return jax.nn.softmax(x, axis=axis)

def _gelu(x):
    return jax.nn.gelu(x, approximate=True)

def _silu(x):
    return jax.nn.silu(x)

def _sigmoid(x):
    return jax.nn.sigmoid(x)

def _layernorm(x, axis=-1, eps=1e-05):
    m = jnp.mean(x, axis=axis, keepdims=True)
    v = jnp.var(x, axis=axis, keepdims=True)
    return (x - m) / jnp.sqrt(v + eps)

def _scatter_add(tgt, idx, src, axis=0):
    return tgt.at[idx].add(src)

def _segment_sum(src, seg, n):
    return jax.ops.segment_sum(src, seg, n)
kernel_name = 'mk_hybrid_d1_jaxref_r4_75da8e'

def setup_inputs(seed: int=0):
    np.random.seed(seed)
    _w = jnp.asarray

    def _L0_attn_a_setup():
        import jax, jax.numpy as jnp
        import numpy as np
        D_MODEL = 256
        N_HEAD = 16
        HEAD_DIM = D_MODEL // N_HEAD
        EPS = 1e-06
        B, T = (4, 256)

        def _eml(x, agg, eps=EPS):
            return jnp.log(jnp.abs(x) + eps) - jnp.log(agg + eps)

        def _split_heads(t):
            b, s, _ = t.shape
            return t.reshape(b, s, N_HEAD, HEAD_DIM).transpose(0, 2, 1, 3)
        key = jax.random.key(seed)
        k0, k1, k2, k3 = jax.random.split(key, 4)
        x = jax.random.normal(k0, (B, T, D_MODEL), dtype=jnp.float32)
        bound = 0.1 / np.sqrt(D_MODEL)
        w_qkv = jax.random.uniform(k1, (3 * D_MODEL, D_MODEL), jnp.float32, -bound, bound)
        w_ky = jax.random.uniform(k2, (D_MODEL, D_MODEL), jnp.float32, -bound, bound)
        w_proj = jax.random.uniform(k3, (D_MODEL, D_MODEL), jnp.float32, -bound, bound)
        return {'x': x, 'w_qkv': w_qkv, 'w_ky': w_ky, 'w_proj': w_proj}
    _L0_attn_a_in = _L0_attn_a_setup()

    def _L0_attn_b_setup():
        import jax, jax.numpy as jnp
        import numpy as np
        D_MODEL = 256
        EXP = 2
        D_IN = D_MODEL * EXP
        D_STATE = 16
        CONV_D = 4
        BATCH = 4
        SEQ = 512

        def _rmsnorm(x, w, eps=1e-06):
            return x * jax.lax.rsqrt(jnp.mean(x * x, axis=-1, keepdims=True) + eps) * w
        key = jax.random.key(seed)
        ks = jax.random.split(key, 8)
        sd = 1.0 / np.sqrt(D_MODEL)
        sdi = 1.0 / np.sqrt(D_IN)
        return {'x': jax.random.normal(ks[0], (BATCH, SEQ, D_MODEL), jnp.float32), 'norm_w': jnp.ones((D_MODEL,), jnp.float32), 'Win': jax.random.normal(ks[1], (D_MODEL, D_IN), jnp.float32) * sd, 'b_in': jnp.zeros((D_IN,), jnp.float32), 'conv_w': jax.random.normal(ks[2], (D_IN, 1, CONV_D), jnp.float32) * 0.5, 'conv_b': jnp.zeros((D_IN,), jnp.float32), 'A': jax.random.normal(ks[3], (D_IN, D_STATE, D_STATE), jnp.float32) * 0.1, 'Bm': jax.random.normal(ks[4], (D_IN, D_STATE, 1), jnp.float32), 'Cm': jax.random.normal(ks[5], (D_IN, 1, D_STATE), jnp.float32), 'Wout': jax.random.normal(ks[6], (D_IN, D_MODEL), jnp.float32) * sdi, 'b_out': jnp.zeros((D_MODEL,), jnp.float32)}
    _L0_attn_b_in = _L0_attn_b_setup()

    def _L0_ffn_setup():
        import jax, jax.numpy as jnp
        import numpy as np
        B, S, D, H, E = (8, 512, 256, 1024, 16)
        key = jax.random.key(seed)
        ks = jax.random.split(key, 4)
        sd = 1.0 / np.sqrt(D).astype(np.float32)
        sh = 1.0 / np.sqrt(H).astype(np.float32)
        return {'x': jax.random.normal(ks[0], (B, S, D), jnp.float32), 'Wg': jax.random.normal(ks[1], (D, E), jnp.float32) * sd, 'bg': jnp.zeros((E,), jnp.float32), 'W1': jax.random.normal(ks[2], (E, D, H), jnp.float32) * sd, 'b1': jnp.zeros((E, H), jnp.float32), 'W2': jax.random.normal(ks[3], (E, H, D), jnp.float32) * sh, 'b2': jnp.zeros((E, D), jnp.float32)}
    _L0_ffn_in = _L0_ffn_setup()
    _d = {'L0_attn_a_x': _L0_attn_a_in['x'], 'L0_attn_a_w_qkv': _L0_attn_a_in['w_qkv'], 'L0_attn_a_w_ky': _L0_attn_a_in['w_ky'], 'L0_attn_a_w_proj': _L0_attn_a_in['w_proj'], 'L0_attn_b_norm_w': _L0_attn_b_in['norm_w'], 'L0_attn_b_Win': _L0_attn_b_in['Win'], 'L0_attn_b_b_in': _L0_attn_b_in['b_in'], 'L0_attn_b_conv_w': _L0_attn_b_in['conv_w'], 'L0_attn_b_conv_b': _L0_attn_b_in['conv_b'], 'L0_attn_b_A': _L0_attn_b_in['A'], 'L0_attn_b_Bm': _L0_attn_b_in['Bm'], 'L0_attn_b_Cm': _L0_attn_b_in['Cm'], 'L0_attn_b_Wout': _L0_attn_b_in['Wout'], 'L0_attn_b_b_out': _L0_attn_b_in['b_out'], 'L0_ffn_Wg': _L0_ffn_in['Wg'], 'L0_ffn_bg': _L0_ffn_in['bg'], 'L0_ffn_W1': _L0_ffn_in['W1'], 'L0_ffn_b1': _L0_ffn_in['b1'], 'L0_ffn_W2': _L0_ffn_in['W2'], 'L0_ffn_b2': _L0_ffn_in['b2']}
    _x0 = _d['L0_attn_a_x']
    _d['L0_attn_a_x'] = jax.random.normal(jax.random.fold_in(jax.random.key(seed), 1), (16, 512, 256), dtype=_x0.dtype)
    del _x0
    return _d

def reference(L0_attn_a_x, L0_attn_a_w_qkv, L0_attn_a_w_ky, L0_attn_a_w_proj, L0_attn_b_norm_w, L0_attn_b_Win, L0_attn_b_b_in, L0_attn_b_conv_w, L0_attn_b_conv_b, L0_attn_b_A, L0_attn_b_Bm, L0_attn_b_Cm, L0_attn_b_Wout, L0_attn_b_b_out, L0_ffn_Wg, L0_ffn_bg, L0_ffn_W1, L0_ffn_b1, L0_ffn_W2, L0_ffn_b2):

    def _L0_attn_a_ref(x, w_qkv, w_ky, w_proj):
        import jax, jax.numpy as jnp
        import numpy as np
        D_MODEL = 256
        N_HEAD = 16
        HEAD_DIM = D_MODEL // N_HEAD
        EPS = 1e-06
        B, T = (4, 256)

        def _eml(x, agg, eps=EPS):
            return jnp.log(jnp.abs(x) + eps) - jnp.log(agg + eps)

        def _split_heads(t):
            b, s, _ = t.shape
            return t.reshape(b, s, N_HEAD, HEAD_DIM).transpose(0, 2, 1, 3)
        b, t, _ = x.shape
        qkv = x @ w_qkv.T
        q, k, v = jnp.split(qkv, 3, axis=-1)
        q, k, v = (_split_heads(q), _split_heads(k), _split_heads(v))
        scale = 1.0 / np.sqrt(HEAD_DIM)
        L = jnp.einsum('bhqd,bhkd->bhqk', q, k) * scale
        mask = jnp.tril(jnp.ones((t, t), dtype=L.dtype))[None, None]
        k_y = _split_heads(x @ w_ky.T)
        L_y = jnp.einsum('bhqd,bhkd->bhqk', q, k_y) * scale
        agg = jnp.sum(jnp.exp(jnp.clip(L_y, -15.0, 15.0)) * mask, axis=-1, keepdims=True) + EPS
        r = _eml(L, agg)
        w = jax.nn.softplus(r) * mask
        A = w / (jnp.sum(w, axis=-1, keepdims=True) + EPS)
        out = jnp.einsum('bhqk,bhkd->bhqd', A, v)
        out = out.transpose(0, 2, 1, 3).reshape(b, t, D_MODEL)
        return out @ w_proj.T

    def _L0_attn_b_ref(x, norm_w, Win, b_in, conv_w, conv_b, A, Bm, Cm, Wout, b_out):
        import jax, jax.numpy as jnp
        import numpy as np
        D_MODEL = 256
        EXP = 2
        D_IN = D_MODEL * EXP
        D_STATE = 16
        CONV_D = 4
        BATCH = 4
        SEQ = 512

        def _rmsnorm(x, w, eps=1e-06):
            return x * jax.lax.rsqrt(jnp.mean(x * x, axis=-1, keepdims=True) + eps) * w
        res = x
        h = _rmsnorm(x, norm_w)
        u = h @ Win + b_in
        u = u.transpose(0, 2, 1)
        u = jax.lax.conv_general_dilated(u, conv_w, window_strides=(1,), padding=[(CONV_D - 1, 0)], feature_group_count=D_IN, dimension_numbers=('NCH', 'OIH', 'NCH')) + conv_b[None, :, None]
        u = u.transpose(0, 2, 1)
        Bv = Bm[:, :, 0]
        Cv = Cm[:, 0, :]

        def step(hc, u_t):
            hc = jnp.einsum('bdr,drs->bds', hc, A) + u_t[:, :, None] * Bv[None]
            y = jnp.einsum('bds,ds->bd', hc, Cv)
            return (hc, y)
        h0 = jnp.zeros((x.shape[0], D_IN, D_STATE), u.dtype)
        _, ys = jax.lax.scan(step, h0, u.transpose(1, 0, 2))
        y = ys.transpose(1, 0, 2)
        return y @ Wout + b_out + res

    def _L0_ffn_ref(x, Wg, bg, W1, b1, W2, b2):
        import jax, jax.numpy as jnp
        import numpy as np
        B, S, D, H, E = (8, 512, 256, 1024, 16)
        d = x.shape[-1]
        xf = x.reshape(-1, d)
        n_tok = xf.shape[0]
        n_exp = Wg.shape[1]
        cap = -(-n_tok // n_exp)
        score = jax.nn.softmax(xf @ Wg + bg, axis=-1)
        gate = jnp.max(score, axis=-1)
        idx = jnp.argmax(score, axis=-1)
        onehot = jax.nn.one_hot(idx, n_exp, dtype=jnp.int32)
        pos = jnp.sum((jnp.cumsum(onehot, axis=0) - 1) * onehot, axis=-1)
        keep = pos < cap
        safe_pos = jnp.where(keep, pos, cap - 1)
        buf = jnp.zeros((n_exp, cap, d), x.dtype).at[idx, safe_pos].add(jnp.where(keep[:, None], xf, 0.0))
        h = jax.nn.relu(jnp.einsum('ecd,edh->ech', buf, W1) + b1[:, None, :])
        y = jnp.einsum('ech,ehd->ecd', h, W2) + b2[:, None, :]
        out = y[idx, safe_pos] * gate[:, None]
        out = jnp.where(keep[:, None], out, 0.0)
        return out.reshape(x.shape)
    x = L0_attn_a_x
    x = x + _L0_attn_a_ref(_layernorm(x, axis=-1), L0_attn_a_w_qkv, L0_attn_a_w_ky, L0_attn_a_w_proj)
    x = x + _L0_ffn_ref(_layernorm(x, axis=-1), L0_ffn_Wg, L0_ffn_bg, L0_ffn_W1, L0_ffn_b1, L0_ffn_W2, L0_ffn_b2)
    x = x + _L0_attn_b_ref(_layernorm(x, axis=-1), L0_attn_b_norm_w, L0_attn_b_Win, L0_attn_b_b_in, L0_attn_b_conv_w, L0_attn_b_conv_b, L0_attn_b_A, L0_attn_b_Bm, L0_attn_b_Cm, L0_attn_b_Wout, L0_attn_b_b_out)
    x = x + _L0_ffn_ref(_layernorm(x, axis=-1), L0_ffn_Wg, L0_ffn_bg, L0_ffn_W1, L0_ffn_b1, L0_ffn_W2, L0_ffn_b2)
    return x

_drawn_inputs = setup_inputs


def setup_inputs(seed=0):
    import zlib

    import numpy as np

    out = dict(_drawn_inputs(seed))
    spreads = {'L0_attn_b_norm_w': (1.0, 0.2),
     'L0_attn_b_b_in': (0.0, 0.1),
     'L0_attn_b_conv_b': (0.0, 0.1),
     'L0_attn_b_b_out': (0.0, 0.381),
     'L0_ffn_bg': (0.0, 0.1),
     'L0_ffn_b1': (0.0, 0.421),
     'L0_ffn_b2': (0.0, 0.294)}
    factors = {'L0_attn_a_w_qkv': 8.0, 'L0_attn_a_w_ky': 8.0, 'L0_attn_a_w_proj': 8.0}
    for name, (base, spread) in spreads.items():
        noise = np.random.default_rng([zlib.crc32(name.encode()), seed]).standard_normal(out[name].shape)
        drawn = base * np.exp(spread * noise) if base else spread * noise
        out[name] = jnp.asarray(drawn.astype(out[name].dtype))
    for name, factor in factors.items():
        out[name] = (out[name] * factor).astype(out[name].dtype)
    return out
```

```python
import concourse.bass as bass
from concourse import mybir
from contextlib import ExitStack

P = 128
F32 = mybir.dt.float32
U32 = mybir.dt.uint32
I32 = mybir.dt.int32
ALU = mybir.AluOpType
ACT = mybir.ActivationFunctionType
AX = mybir.AxisListType

BATCH, SEQ, D = 16, 512, 256
NTOK = BATCH * SEQ
TILES = SEQ // P
DC = D // P
HEADS, HD = 16, 16
HPC = P // HD
VW = 32
EXPERTS, HID = 16, 1024
CAP = NTOK // EXPERTS
HC = HID // P
DIN = 512
NST = 16
CHUNK = 32
NCH = SEQ // CHUNK
QC = DIN // P
GRP = P // CHUNK
NPAIR = CHUNK // 2
KW = 4
COLS = TILES * (TILES + 1) // 2 * P
PLACE = {512: 0, 384: 512, 128: 896, 256: 1024}
LN_EPS = 1e-5
EPS = 1e-6
LIMIT = 60.0


def constants(nc, sb):
    c = {
        "ident": sb("ident", [P, P], F32),
        "cap": sb("cap", [P, COLS], F32),
        "causal": sb("causal", [P, COLS], F32),
        "magnitude": sb("magnitude", [P, COLS], I32),
        "head_of": sb("head_of", [P, HPC], F32),
        "group_of": sb("group_of", [P, GRP], F32),
        "experts": sb("experts", [P, EXPERTS], F32),
        "experts_i": sb("experts_i", [P, EXPERTS], I32),
        "spare": sb("spare", [P, 2], F32),
        "power": sb("power", [P, TILES], F32),
    }
    with nc.semaphore("made") as made, nc.semaphore("bits") as bits, nc.Block() as block:
        @block.gpsimd
        def _(pool):
            pool.memset(c["ident"][:, :], 0.0)
            pool.memset(c["cap"][:, :], LIMIT)
            pool.memset(c["causal"][:, :], 1.0)
            pool.memset(c["head_of"][:, :], 1.0)
            pool.memset(c["group_of"][:, :], 1.0)
            pool.memset(c["power"][:, :], -0.5)
            pool.iota(c["experts_i"][:, :], [[1, EXPERTS]], base=0, channel_multiplier=0).then_inc(made, 1)
            pool.wait_ge(made, 1)
            pool.tensor_copy(c["experts"][:, :], c["experts_i"][:, :])
            pool.affine_select(out=c["ident"][:, :], in_=c["ident"][:, :], compare_op=ALU.not_equal, fill=1.0,
                               base=0, pattern=[[-1, P]], channel_multiplier=1)
            for t in range(TILES):
                n = (t + 1) * P
                v = c["cap"][:, PLACE[n]:PLACE[n] + n]
                pool.affine_select(out=v, in_=v, compare_op=ALU.is_ge, fill=-4e4, base=t * P,
                                   pattern=[[-1, n]], channel_multiplier=1)
                v = c["causal"][:, PLACE[n]:PLACE[n] + n]
                pool.affine_select(out=v, in_=v, compare_op=ALU.is_ge, fill=0.0, base=0,
                                   pattern=[[1, n]], channel_multiplier=-1)
            for name, width, n in (("head_of", HD, HPC), ("group_of", CHUNK, GRP)):
                m = c[name][:, :]
                pool.affine_select(out=m, in_=m, compare_op=ALU.is_ge, fill=0.0, base=0,
                                   pattern=[[-width, n]], channel_multiplier=1).then_inc(made, 1)
            pool.wait_ge(made, 3)
            for name, width, n in (("head_of", HD, HPC), ("group_of", CHUNK, GRP)):
                m = c[name][:, :]
                last = pool.affine_select(out=m, in_=m, compare_op=ALU.is_ge, fill=0.0, base=width - 1,
                                          pattern=[[width, n]], channel_multiplier=-1)
            last.then_inc(made, 1)
            pool.wait_ge(made, 4)

        @block.vector
        def _(dve):
            m = c["magnitude"][:, :]
            dve.wait_ge(made, 4)
            dve.tensor_copy(m, c["causal"][:, :]).then_inc(bits, 1)
            dve.wait_ge(bits, 1)
            dve.tensor_scalar(m, m, 31, 31, ALU.logical_shift_left, ALU.arith_shift_right).then_inc(bits, 1)
            dve.wait_ge(bits, 2)
            dve.tensor_scalar(m, m, 0x7FFFFFFF, None, ALU.bitwise_and).then_inc(bits, 1)
            dve.wait_ge(bits, 3)
    return c


def apart(eng, c):
    if eng.engine == mybir.EngineType.DVE:
        return eng.memset(c["spare"][:, 0:1], 0.0)
    return eng.tensor_tensor(c["spare"][:, 1:2], c["power"][:, 0:1], c["power"][:, 0:1], ALU.mult)


def attention(nc, c, x, wqkv, wky, wproj, x1):
    ident, cap, causal, head_of = c["ident"], c["cap"], c["causal"], c["head_of"]
    ones = causal[:, P:2 * P]
    upper = causal[:, 0:P]
    with ExitStack() as ctx:
        def sb(name, shape, dt=F32):
            return ctx.enter_context(nc.sbuf_tensor(name, shape, dt))

        def sem(name):
            return ctx.enter_context(nc.semaphore(name))

        w_sb = sb("a_w", [P, DC, 3 * D])
        wky_sb = sb("a_wky", [P, DC, D])
        wp_sb = sb("a_wp", [P, DC, D])
        x_in = sb("a_x", [P, TILES, D])
        x_res = sb("a_xres", [P, TILES, D])
        stats = sb("a_stats", [P, TILES, 6])
        mv = sb("a_mv", [P, TILES, 2])
        veps = sb("a_veps", [P, TILES])
        rstd = sb("a_rstd", [P, TILES])
        xn = sb("a_xn", [P, TILES, D])
        xnT = sb("a_xnT", [P, DC, SEQ])
        qT = sb("a_qT", [P, DC, SEQ])
        kT = sb("a_kT", [P, DC, SEQ])
        kyT = sb("a_kyT", [P, DC, SEQ])
        q2T = sb("a_q2T", [P, DC, SEQ])
        v = sb("a_v", [P, TILES, HEADS, VW])
        qm = sb("a_qm", [P, 4, SEQ])
        q2m = sb("a_q2m", [P, 4, SEQ])
        clipped = sb("a_clipped", [P, 2, COLS])
        agg = sb("a_agg", [P, TILES, HEADS])
        agg1 = sb("a_agg1", [P, TILES, HEADS])
        agg2 = sb("a_agg2", [P, TILES, HEADS])
        inv1 = sb("a_inv1", [P, TILES, HEADS])
        inv2 = sb("a_inv2", [P, TILES, HEADS])
        rx = sb("a_rx", [P, TILES, HEADS, HD])
        shift = sb("a_shift", [P, TILES, HEADS])
        ratio = sb("a_ratio", [P, 2, COLS])
        weight = sb("a_weight", [P, 2, COLS])
        headT = sb("a_headT", [P, SEQ])
        av = sb("a_av", [P, TILES, HEADS, VW])
        t1 = sb("a_t1", [P, HEADS, HD + 1])
        t2 = sb("a_t2", [P, HEADS, HD + 1])
        den = sb("a_den", [P, HEADS])
        rden = sb("a_rden", [P, HEADS])
        o = sb("a_o", [P, TILES, D])
        oT = sb("a_oT", [P, DC, SEQ])
        x1_sb = sb("a_x1", [P, TILES, D])
        ps = ctx.enter_context(nc.psum_tensor("a_ps", [P, 8, 512], F32))
        flat = ps[:, :, :].rearrange("p b n -> p (b n)")

        weights_in = sem("weights_in")
        x_loaded = sem("x_loaded")
        xres_loaded = sem("xres_loaded")
        x1_stored = sem("x1_stored")
        v_ones = sem("v_ones")
        ln_step = sem("ln_step")
        veps_ready = sem("veps_ready")
        rstd_ready = sem("rstd_ready")
        xn_ready = sem("xn_ready")
        misc_full = sem("misc_full")
        misc_read = sem("misc_read")
        qm_ready = sem("qm_ready")
        e_scores = sem("e_scores")
        clip_done = sem("clip_done")
        exp_done = sem("exp_done")
        agg_step = sem("agg_step")
        rx_ready = sem("rx_ready")
        shift_ready = sem("shift_ready")
        rT_full = sem("rT_full")
        q2_done = sem("q2_done")
        q2m_ready = sem("q2m_ready")
        w_scores = sem("w_scores")
        abs_done = sem("abs_done")
        ln_done = sem("ln_done")
        av_done = sem("av_done")
        headT_ready = sem("headT_ready")
        ot_full = sem("ot_full")
        av_read = sem("av_read")
        cv_full = sem("cv_full")
        norm_step = sem("norm_step")
        o_ready = sem("o_ready")
        oT_full = sem("oT_full")
        oT_ready = sem("oT_ready")
        proj_full = sem("proj_full")
        x1_ready = sem("x1_ready")
        block = ctx.enter_context(nc.Block())

        x_t = x.rearrange("b (t p) d -> b p t d", p=P)
        x1_t = x1.rearrange("(b t p) d -> b p t d", p=P, t=TILES)

        def score_place(n):
            return slice(PLACE[n], PLACE[n] + n)

        @block.sync
        def _(sp):
            sp.dma_start(x_in[:, :, :], x_t[0]).then_inc(x_loaded, 16)
            sp.dma_start(w_sb[:, :, :], wqkv.rearrange("(c p) n -> p c n", p=P)).then_inc(weights_in, 16)
            sp.dma_start(wky_sb[:, :, :], wky.rearrange("(c p) n -> p c n", p=P)).then_inc(weights_in, 16)
            sp.dma_start(wp_sb[:, :, :], wproj.rearrange("(c p) n -> p c n", p=P)).then_inc(weights_in, 16)

            def turn(b, last):
                sp.wait_ge(x1_ready, 2 * b)
                sp.dma_start(x_res[:, :, :], x_t[bass.ds(b, 1)].rearrange("a p t d -> p (a t) d")
                             if not last else x_t[BATCH - 1]).then_inc(xres_loaded, 16)
                if not last:
                    sp.wait_ge(xn_ready, b + 1)
                    sp.dma_start(x_in[:, :, :], x_t[bass.ds(b + 1, 1)].rearrange("a p t d -> p (a t) d"))\
                      .then_inc(x_loaded, 16)
                sp.wait_ge(x1_ready, 2 * b + 2)
                sp.dma_start(x1_t[bass.ds(b, 1)].rearrange("a p t d -> p (a t) d") if not last
                             else x1_t[BATCH - 1], x1_sb[:, :, :]).then_inc(x1_stored, 16)

            with sp.Fori(0, BATCH - 1) as b:
                turn(b, False)
            turn(BATCH - 1, True)
            sp.wait_ge(x1_stored, 16 * BATCH)

        @block.gpsimd
        def _(pool):
            pool.memset(v[:, :, :, HD:VW], 0.0).then_inc(v_ones, 1)
            pool.wait_ge(v_ones, 1)
            pool.memset(v[:, :, :, HD:HD + 1], 1.0).then_inc(v_ones, 1)
            with pool.Fori(0, BATCH) as b:
                pool.wait_ge(veps_ready, b + 1)
                pool.tensor_tensor(rstd[:, :], veps[:, :], c["power"][:, :], ALU.pow).then_inc(rstd_ready, 1)
                pool.wait_ge(misc_read, 10 * b + 4)
                for h in range(HEADS):
                    if h >= 4:
                        pool.wait_ge(e_scores, HEADS * b + h - 3)
                    pool.tensor_tensor(qm[:, h % 4, :], qT[:, h // HPC, :],
                                       head_of[:, h % HPC:h % HPC + 1].broadcast_to([P, SEQ]), ALU.mult).then_inc(qm_ready, 1)
                for h in range(HEADS):
                    if h % HPC == 0:
                        pool.wait_ge(q2_done, 2 * b + 1 + h // HPC)
                    if h >= 4:
                        pool.wait_ge(w_scores, HEADS * b + h - 3)
                    pool.tensor_tensor(q2m[:, h % 4, :], q2T[:, h // HPC, :],
                                       head_of[:, h % HPC:h % HPC + 1].broadcast_to([P, SEQ]), ALU.mult).then_inc(q2m_ready, 1)

        @block.tensor
        def _(pe):
            pe.wait_ge(weights_in, 48)
            pe.wait_ge(v_ones, 2)
            with pe.Fori(0, BATCH) as b:
                pe.wait_ge(xn_ready, b + 1)
                pe.wait_ge(x1_ready, 2 * b)
                for k in range(DC):
                    for t in range(TILES):
                        last = pe.transpose(ps[:, 6 + k, t * P:(t + 1) * P], xn[:, t, k * P:(k + 1) * P],
                                            ident[:, :])
                    last.then_inc(misc_full, 1)
                for m in range(2, 10):
                    pe.wait_ge(misc_read, 10 * b + (2 if m == 2 else m - 1))
                    bank = 6 + m % 2
                    if m < 8:
                        which, half = (m - 2) // 2, m % 2
                        w = wky_sb if which == 2 else w_sb
                        col = (D if which == 1 else 0) + half * P
                        for k in range(DC):
                            last = pe.matmul(ps[:, bank, :], w[:, k, col:col + P], xnT[:, k, :],
                                             start=(k == 0), stop=(k == DC - 1))
                    else:
                        for i in range(2):
                            t = 2 * (m - 8) + i
                            for k in range(DC):
                                last = pe.matmul(ps[:, bank, i * D:(i + 1) * D], xnT[:, k, t * P:(t + 1) * P],
                                                 w_sb[:, k, 2 * D:3 * D], start=(k == 0), stop=(k == DC - 1))
                    last.then_inc(misc_full, 1)
                pe.wait_ge(misc_read, 10 * b + 8)
                for h in range(HEADS):
                    pe.wait_ge(qm_ready, HEADS * b + h + 1)
                    if h >= 2:
                        pe.wait_ge(clip_done, HEADS * b + h - 1)
                    base = 3 * 512 * (h % 2)
                    for t in range(TILES):
                        n = (t + 1) * P
                        last = pe.matmul(flat[:, base + PLACE[n]:base + PLACE[n] + n],
                                         qm[:, h % 4, t * P:(t + 1) * P], kyT[:, h // HPC, 0:n],
                                         start=True, stop=True)
                    last.then_inc(e_scores, 1)
                pe.wait_ge(rx_ready, b + 1)
                pe.wait_ge(misc_read, 10 * b + 10)
                for k in range(DC):
                    for t in range(TILES):
                        last = pe.transpose(ps[:, 6 + k, t * P:(t + 1) * P],
                                            rx[:, t, k * HPC:(k + 1) * HPC, :].rearrange("p h d -> p (h d)"),
                                            ident[:, :])
                    last.then_inc(rT_full, 1)

                def scores(h):
                    if h < 2:
                        pe.wait_ge(clip_done, HEADS * b + HEADS - 1 + h)
                    else:
                        pe.wait_ge(abs_done, HEADS * b + h - 1)
                    pe.wait_ge(q2m_ready, HEADS * b + h + 1)
                    base = 3 * 512 * (h % 2)
                    for t in range(TILES):
                        n = SEQ - t * P
                        last = pe.matmul(flat[:, base + PLACE[n]:base + PLACE[n] + n],
                                         kT[:, h // HPC, t * P:(t + 1) * P], q2m[:, h % 4, t * P:SEQ],
                                         start=True, stop=True)
                    last.then_inc(w_scores, 1)

                def values(h):
                    pe.wait_ge(ln_done, HEADS * b + h + 1)
                    if h == 0:
                        pe.wait_ge(q2_done, 2 * b + 2)
                    elif h % 4 == 0:
                        pe.wait_ge(headT_ready, 4 * b + h // 4)
                    r = 32 * (h % 4)
                    for t in range(TILES):
                        last = pe.matmul(ps[r:r + VW, 6, t * P:SEQ], v[:, t, h, :],
                                         weight[:, h % 2, score_place(SEQ - t * P)],
                                         start=(t == 0), stop=(t == TILES - 1))
                    last.then_inc(av_done, 1)

                def turn_back(g):
                    pe.wait_ge(headT_ready, 4 * b + g + 1)
                    if g:
                        pe.wait_ge(av_read, 4 * b + g)
                    for t in range(TILES):
                        last = pe.transpose(ps[:, 7, t * P:(t + 1) * P], headT[:, t * P:(t + 1) * P], ident[:, :])
                    last.then_inc(ot_full, 1)

                for h in range(HEADS + 2):
                    if h < HEADS:
                        scores(h)
                    if h >= 2:
                        values(h - 2)
                    if h >= 6 and (h - 6) % 4 == 0:
                        turn_back((h - 6) // 4)
                turn_back(3)
                pe.wait_ge(abs_done, HEADS * b + HEADS)
                for t in range(TILES):
                    for s in range(t + 1):
                        last = pe.matmul(ps[:, t, 0:HEADS * (HD + 1)], upper if s == t else ones,
                                         v[:, s, :, 0:HD + 1], start=(s == 0), stop=(s == t))
                    last.then_inc(cv_full, 1)
                for t in range(TILES):
                    pe.wait_ge(o_ready, TILES * b + t + 1)
                    for k in range(DC):
                        last = pe.transpose(ps[:, 4 + k, t * P:(t + 1) * P], o[:, t, k * P:(k + 1) * P],
                                            ident[:, :])
                last.then_inc(oT_full, 1)
                pe.wait_ge(oT_ready, 2 * b + 2)
                pe.wait_ge(av_read, 4 * b + 4)
                for t in range(TILES):
                    for k in range(DC):
                        last = pe.matmul(ps[:, 6 + t // 2, (t % 2) * D:(t % 2 + 1) * D],
                                         oT[:, k, t * P:(t + 1) * P], wp_sb[:, k, :],
                                         start=(k == 0), stop=(k == DC - 1))
                    if t % 2:
                        last.then_inc(proj_full, 1)

        @block.scalar
        def _(act):
            with act.Fori(0, BATCH) as b:
                for m in range(10):
                    act.wait_ge(misc_full, 10 * b + m + 1)
                    src = ps[:, 6 + m % 2, :]
                    if m == 2:
                        act.wait_ge(qm_ready, HEADS * b)
                        act.wait_ge(q2_done, 2 * b)
                    if m < 8:
                        dst = (xnT, qT, kT, kyT)[m // 2][:, m % 2, :]
                    else:
                        t = 2 * (m - 8)
                        dst = v[:, t:t + 2, :, 0:HD].rearrange("p t h d -> p (t h) d")
                        src = src.rearrange("p (t d) -> p t d", d=HD)
                    act.activation(dst, src, ACT.Copy).then_inc(misc_read, 1)
                for h in range(HEADS):
                    act.wait_ge(clip_done, HEADS * b + h + 1)
                    if h == 0:
                        act.wait_ge(rx_ready, b)
                    for t in range(TILES):
                        n = (t + 1) * P
                        last = act.activation(clipped[:, h % 2, score_place(n)], clipped[:, h % 2, score_place(n)], ACT.Exp, scale=0.25,
                                              accum_out=agg[:, t, h:h + 1])
                    last.then_inc(exp_done, 1)
                act.wait_ge(rx_ready, b + 1)
                act.activation(shift[:, :, :], inv1[:, :, :], ACT.Ln, scale=EPS, bias=1.0).then_inc(shift_ready, 1)

                def head_rows(g):
                    act.wait_ge(av_done, HEADS * b + 4 * g + 4)
                    if g:
                        act.wait_ge(ot_full, 4 * b + g)
                    act.activation(headT[:, :], ps[:, 6, :], ACT.Copy).then_inc(headT_ready, 1)

                for h in range(HEADS):
                    act.wait_ge(abs_done, HEADS * b + h + 1)
                    if h >= 2:
                        act.wait_ge(av_done, HEADS * b + h - 1)
                    act.activation(weight[:, h % 2, :], ratio[:, h % 2, :], ACT.Ln, bias=1.0).then_inc(ln_done, 1)
                    if h % 4 == 0 and h:
                        head_rows(h // 4 - 1)
                head_rows(3)
                act.wait_ge(oT_full, b + 1)
                for k in range(DC):
                    act.activation(oT[:, k, :], ps[:, 4 + k, :], ACT.Copy).then_inc(oT_ready, 1)

        @block.vector
        def _(dve):
            with dve.Fori(0, BATCH) as b:
                dve.wait_ge(x_loaded, 16 * b + 16)
                for t in range(TILES):
                    last = dve.bn_stats(stats[:, t, :], x_in[:, t, :])
                last.then_inc(ln_step, 1)
                dve.wait_ge(ln_step, 2 * b + 1)
                apart(dve, c)
                for t in range(TILES):
                    last = dve.bn_aggr(mv[:, t, :], stats[:, t, :])
                last.then_inc(ln_step, 1)
                dve.wait_ge(ln_step, 2 * b + 2)
                dve.tensor_scalar(veps[:, :], mv[:, :, 1], LN_EPS, None, ALU.add).then_inc(veps_ready, 1)
                dve.wait_ge(rstd_ready, b + 1)
                for t in range(TILES):
                    last = dve.tensor_scalar(xn[:, t, :], x_in[:, t, :], mv[:, t, 0:1], rstd[:, t:t + 1],
                                             ALU.subtract, ALU.mult)
                last.then_inc(xn_ready, 1)
                for h in range(HEADS):
                    dve.wait_ge(e_scores, HEADS * b + h + 1)
                    if h >= 2:
                        dve.wait_ge(exp_done, HEADS * b + h - 1)
                    elif h == 0:
                        dve.wait_ge(exp_done, HEADS * b)
                    base = 3 * 512 * (h % 2)
                    dve.scalar_tensor_tensor(out=clipped[:, h % 2, :], in0=flat[:, base:base + COLS], scalar=-LIMIT,
                                             in1=cap[:, :], op0=ALU.max, op1=ALU.min).then_inc(clip_done, 1)
                dve.wait_ge(exp_done, HEADS * b + HEADS)
                dve.wait_ge(shift_ready, b)
                dve.tensor_scalar(agg1[:, :, :], agg[:, :, :], EPS, None, ALU.add).then_inc(agg_step, 1)
                dve.wait_ge(agg_step, 3 * b + 1)
                dve.tensor_scalar(agg2[:, :, :], agg1[:, :, :], EPS, None, ALU.add).then_inc(agg_step, 1)
                dve.reciprocal(inv1[:, :, :], agg1[:, :, :])
                dve.wait_ge(agg_step, 3 * b + 2)
                dve.reciprocal(inv2[:, :, :], agg2[:, :, :]).then_inc(agg_step, 1)
                dve.wait_ge(agg_step, 3 * b + 3)
                dve.tensor_scalar(rx[:, :, :, :].rearrange("p t h d -> p (t h) d"),
                                  inv2[:, :, :].rearrange("p t h -> p (t h)").unsqueeze(2)
                                  .broadcast_to([P, TILES * HEADS, HD]),
                                  0.25, None, ALU.mult).then_inc(rx_ready, 1)
                dve.wait_ge(q2m_ready, HEADS * b)
                for k in range(DC):
                    dve.wait_ge(rT_full, 2 * b + k + 1)
                    dve.tensor_tensor(q2T[:, k, :], ps[:, 6 + k, :], qT[:, k, :], ALU.mult).then_inc(q2_done, 1)

                def sums(g):
                    dve.wait_ge(ot_full, 4 * b + g + 1)
                    dve.tensor_copy(av[:, :, 4 * g:4 * g + 4, :].rearrange("p t h d -> p t (h d)"),
                                    ps[:, 7, :].rearrange("p (t n) -> p t n", t=TILES)).then_inc(av_read, 1)

                for h in range(HEADS):
                    dve.wait_ge(w_scores, HEADS * b + h + 1)
                    if h >= 2:
                        dve.wait_ge(ln_done, HEADS * b + h - 1)
                    base = 3 * 512 * (h % 2)
                    dve.tensor_tensor(ratio[:, h % 2, :].bitcast(I32), flat[:, base:base + COLS].bitcast(I32),
                                      c["magnitude"][:, :], ALU.bitwise_and).then_inc(abs_done, 1)
                    if h >= 7 and (h - 7) % 4 == 0:
                        sums((h - 7) // 4)
                sums(3)
                dve.wait_ge(shift_ready, b + 1)
                for t in range(TILES):
                    n = 4 * (TILES * b + t)
                    dve.wait_ge(cv_full, TILES * b + t + 1)
                    dve.tensor_tensor(t1[:, :, :], ps[:, t, 0:HEADS * (HD + 1)].rearrange("p (h d) -> p h d", h=HEADS),
                                      shift[:, t, :].unsqueeze(2).broadcast_to([P, HEADS, HD + 1]),
                                      ALU.mult).then_inc(norm_step, 1)
                    dve.wait_ge(norm_step, n + 1)
                    dve.tensor_tensor(t2[:, :, :], t1[:, :, :], av[:, t, :, 0:HD + 1], ALU.add).then_inc(norm_step, 1)
                    dve.wait_ge(norm_step, n + 2)
                    dve.tensor_scalar(den[:, :], t2[:, :, HD], EPS, None, ALU.add).then_inc(norm_step, 1)
                    dve.wait_ge(norm_step, n + 3)
                    dve.reciprocal(rden[:, :], den[:, :]).then_inc(norm_step, 1)
                    dve.wait_ge(norm_step, n + 4)
                    dve.tensor_tensor(o[:, t, :].rearrange("p (h d) -> p h d", h=HEADS), t2[:, :, 0:HD],
                                      rden[:, :].unsqueeze(2).broadcast_to([P, HEADS, HD]),
                                      ALU.mult).then_inc(o_ready, 1)
                dve.wait_ge(xres_loaded, 16 * b + 16)
                dve.wait_ge(x1_stored, 16 * b)
                for k in range(2):
                    dve.wait_ge(proj_full, 2 * b + k + 1)
                    dve.tensor_tensor(x1_sb[:, 2 * k:2 * k + 2, :].rearrange("p t d -> p (t d)"), ps[:, 6 + k, :],
                                      x_res[:, 2 * k:2 * k + 2, :].rearrange("p t d -> p (t d)"),
                                      ALU.add).then_inc(x1_ready, 1)


def route(nc, c, tag, x_rows, wg, bg, buf, gates, slots):
    ident, causal = c["ident"], c["causal"]
    ones, upper = causal[:, P:2 * P], causal[:, 0:P]
    groups = NTOK // (TILES * P)
    with ExitStack() as ctx:
        def sb(name, shape, dt=F32):
            return ctx.enter_context(nc.sbuf_tensor(f"{tag}_{name}", shape, dt))

        def sem(name):
            return ctx.enter_context(nc.semaphore(f"{tag}_{name}"))

        wg_sb = sb("wg", [P, DC, EXPERTS])
        bg_sb = sb("bg", [P, EXPERTS])
        x = sb("x", [P, TILES, D])
        stats = sb("stats", [P, TILES, 6])
        mv = sb("mv", [P, TILES, 2])
        veps = sb("veps", [P, TILES])
        rstd = sb("rstd", [P, TILES])
        z = sb("z", [P, TILES, D])
        zT = sb("zT", [P, DC, SEQ])
        logit = sb("logit", [P, TILES, EXPERTS])
        best = sb("best", [P, TILES, 8])
        which = sb("which", [P, TILES, 8], U32)
        expert = sb("expert", [P, TILES])
        below = sb("below", [P, TILES, EXPERTS])
        expd = sb("expd", [P, TILES, EXPERTS])
        total = sb("total", [P, TILES])
        gate = sb("gate", [P, TILES])
        onehot = sb("onehot", [P, TILES, EXPERTS])
        before = sb("before", [P, TILES + 1, EXPERTS])
        place = sb("place", [P, TILES, EXPERTS])
        count = sb("count", [P, TILES])
        kept = sb("kept", [P, TILES])
        safe = sb("safe", [P, TILES])
        slot = sb("slot", [P, TILES])
        away = sb("away", [P, TILES])
        target = sb("target", [P, TILES])
        target_u = sb("target_u", [P, TILES], U32)
        ps = ctx.enter_context(nc.psum_tensor(f"{tag}_ps", [P, 4, 512], F32))

        weights_in = sem("weights_in")
        x_loaded = sem("x_loaded")
        dve_step = sem("dve_step")
        veps_ready = sem("veps_ready")
        rstd_ready = sem("rstd_ready")
        z_ready = sem("z_ready")
        zT_full = sem("zT_full")
        zT_ready = sem("zT_ready")
        logits_full = sem("logits_full")
        below_ready = sem("below_ready")
        exp_ready = sem("exp_ready")
        onehot_ready = sem("onehot_ready")
        place_full = sem("place_full")
        target_ready = sem("target_ready")
        scattered = sem("scattered")
        block = ctx.enter_context(nc.Block())
        x_t = x_rows.rearrange("(g t p) d -> g p t d", p=P, t=TILES)

        @block.sync
        def _(sp):
            sp.dma_start(wg_sb[:, :, :], wg.rearrange("(c p) e -> p c e", p=P)).then_inc(weights_in, 16)
            sp.dma_start(bg_sb[:, :], bg.rearrange("(a e) -> a e", a=1).broadcast_to([P, EXPERTS])).then_inc(weights_in, 16)
            with sp.Fori(0, groups) as g:
                sp.wait_ge(z_ready, g)
                sp.dma_start(x[:, :, :], x_t[bass.ds(g, 1)].rearrange("a p t d -> p (a t) d")).then_inc(x_loaded, 16)

        @block.gpsimd
        def _(pool):
            with pool.Fori(0, groups) as g:
                pool.wait_ge(veps_ready, g + 1)
                pool.tensor_tensor(rstd[:, :], veps[:, :], c["power"][:, :], ALU.pow).then_inc(rstd_ready, 1)
                pool.wait_ge(target_ready, g + 1)
                apart(pool, c)
                for t in range(TILES):
                    pool.indirect_dma_start(buf, bass.IndirectOffsetOnAxis(target_u[:, t:t + 1], 0), z[:, t, :], None,
                                            bounds_check=NTOK - 1, oob_is_err=False).then_inc(scattered, 16)
            pool.wait_ge(scattered, 16 * TILES * groups)

        @block.tensor
        def _(pe):
            pe.wait_ge(weights_in, 32)
            with pe.Fori(0, groups) as g:
                pe.wait_ge(z_ready, g + 1)
                pe.wait_ge(zT_ready, 2 * g)
                for k in range(DC):
                    for t in range(TILES):
                        last = pe.transpose(ps[:, k, t * P:(t + 1) * P], z[:, t, k * P:(k + 1) * P], ident[:, :])
                last.then_inc(zT_full, 1)
                pe.wait_ge(zT_ready, 2 * g + 2)
                pe.wait_ge(below_ready, g)
                for t in range(TILES):
                    for k in range(DC):
                        last = pe.matmul(ps[:, 2, t * EXPERTS:(t + 1) * EXPERTS], zT[:, k, t * P:(t + 1) * P],
                                         wg_sb[:, k, :], start=(k == 0), stop=(k == DC - 1))
                last.then_inc(logits_full, 1)
                pe.wait_ge(onehot_ready, g + 1)
                for t in range(TILES):
                    pe.matmul(ps[:, 3, t * EXPERTS:(t + 1) * EXPERTS], upper, onehot[:, t, :], start=True, stop=False)
                    last = pe.matmul(ps[:, 3, t * EXPERTS:(t + 1) * EXPERTS], ones, before[:, t, :],
                                     start=False, stop=True)
                last.then_inc(place_full, 1)

        @block.scalar
        def _(act):
            with act.Fori(0, groups) as g:
                act.wait_ge(zT_full, g + 1)
                for k in range(DC):
                    act.activation(zT[:, k, :], ps[:, k, :], ACT.Copy).then_inc(zT_ready, 1)
                act.wait_ge(below_ready, g + 1)
                act.activation(expd[:, :, :], below[:, :, :], ACT.Exp).then_inc(exp_ready, 1)

        @block.vector
        def _(dve):
            dve.memset(before[:, TILES, :], 0.0).then_inc(dve_step, 1)
            dve.wait_ge(weights_in, 32)
            steps = 18
            with dve.Fori(0, groups) as g:
                done = [1]

                def link(ins, alone=False):
                    done[0] += 1
                    ins.then_inc(dve_step, 1)
                    dve.wait_ge(dve_step, steps * g + done[0])
                    if alone:
                        apart(dve, c)

                dve.wait_ge(x_loaded, 16 * g + 16)
                for t in range(TILES):
                    last = dve.bn_stats(stats[:, t, :], x[:, t, :])
                link(last, alone=True)
                for t in range(TILES):
                    last = dve.bn_aggr(mv[:, t, :], stats[:, t, :])
                link(last)
                dve.tensor_scalar(veps[:, :], mv[:, :, 1], LN_EPS, None, ALU.add).then_inc(veps_ready, 1)
                dve.wait_ge(rstd_ready, g + 1)
                dve.wait_ge(scattered, 16 * TILES * g)
                for t in range(TILES):
                    last = dve.tensor_scalar(z[:, t, :], x[:, t, :], mv[:, t, 0:1], rstd[:, t:t + 1],
                                             ALU.subtract, ALU.mult)
                last.then_inc(z_ready, 1)
                dve.wait_ge(logits_full, g + 1)
                link(dve.tensor_tensor(logit[:, :, :], ps[:, 2, 0:TILES * EXPERTS].rearrange("p (t e) -> p t e", t=TILES),
                                       bg_sb[:, :].unsqueeze(1).broadcast_to([P, TILES, EXPERTS]), ALU.add), alone=True)
                for t in range(TILES):
                    last = dve.max(best[:, t, :], logit[:, t, :])
                link(last, alone=True)
                for t in range(TILES):
                    last = dve.max_index(which[:, t, :], best[:, t, :], logit[:, t, :])
                link(last)
                dve.tensor_tensor(below[:, :, :], logit[:, :, :], best[:, :, 0:1].broadcast_to([P, TILES, EXPERTS]),
                                  ALU.subtract).then_inc(below_ready, 1)
                link(dve.tensor_copy(expert[:, :], which[:, :, 0]))
                link(dve.tensor_tensor(onehot[:, :, :], c["experts"][:, :].unsqueeze(1).broadcast_to([P, TILES, EXPERTS]),
                                       expert[:, :].unsqueeze(2).broadcast_to([P, TILES, EXPERTS]), ALU.is_equal))
                link(dve.tensor_copy(before[:, 0, :], before[:, TILES, :]))
                for t in range(TILES):
                    ins = dve.tensor_tensor(before[:, t + 1, :], before[:, t, :], onehot[:, t, :], ALU.add)
                    if t < TILES - 1:
                        link(ins)
                ins.then_inc(onehot_ready, 1)
                dve.wait_ge(exp_ready, g + 1)
                link(dve.tensor_reduce(total[:, :], expd[:, :, :], AX.X, ALU.add))
                link(dve.reciprocal(gate[:, :], total[:, :]))
                dve.wait_ge(place_full, g + 1)
                link(dve.tensor_tensor(place[:, :, :], ps[:, 3, 0:TILES * EXPERTS].rearrange("p (t e) -> p t e", t=TILES),
                                       onehot[:, :, :], ALU.mult))
                link(dve.tensor_reduce(count[:, :], place[:, :, :], AX.X, ALU.add))
                dve.tensor_scalar(kept[:, :], count[:, :], float(CAP), None, ALU.is_le)
                dve.tensor_scalar(away[:, :], count[:, :], float(CAP), float(2 * NTOK), ALU.is_gt, ALU.mult)
                link(dve.tensor_scalar(safe[:, :], count[:, :], float(CAP), -1.0, ALU.min, ALU.add))
                dve.tensor_tensor(gates[:, bass.ds(g * TILES, TILES)], gate[:, :], kept[:, :], ALU.mult)
                link(dve.scalar_tensor_tensor(out=slot[:, :], in0=expert[:, :], scalar=float(CAP), in1=safe[:, :],
                                              op0=ALU.mult, op1=ALU.add))
                dve.tensor_copy(slots[:, bass.ds(g * TILES, TILES)], slot[:, :])
                link(dve.tensor_tensor(target[:, :], slot[:, :], away[:, :], ALU.add))
                dve.tensor_copy(target_u[:, :], target[:, :]).then_inc(target_ready, 1)
                assert done[0] == steps + 1, done


def experts(nc, c, tag, buf, w1, b1, w2, b2, y_rows):
    ident = c["ident"]
    with ExitStack() as ctx:
        def sb(name, shape, dt=F32):
            return ctx.enter_context(nc.sbuf_tensor(f"{tag}_{name}", shape, dt))

        def sem(name):
            return ctx.enter_context(nc.semaphore(f"{tag}_{name}"))

        w1_sb = sb("w1", [P, 2, DC, HID])
        w2_sb = sb("w2", [P, 2, HC, D])
        b1_sb = sb("b1", [P, 2, HC])
        b2_sb = sb("b2", [P, 2, D])
        rows = sb("rows", [P, 2, TILES, D])
        rowsT = sb("rowsT", [P, 2, DC, CAP])
        hT = sb("hT", [P, 2, HC, CAP])
        y = sb("y", [P, 2, TILES, D])
        ps = ctx.enter_context(nc.psum_tensor(f"{tag}_ps", [P, 8, 512], F32))
        loaded = [sem(f"loaded{u}") for u in range(2)]
        rowsT_full = sem("rowsT_full")
        rowsT_ready = sem("rowsT_ready")
        h_full = sem("h_full")
        h_ready = sem("h_ready")
        y_full = sem("y_full")
        y_ready = sem("y_ready")
        y_stored = [sem(f"y_stored{u}") for u in range(2)]
        block = ctx.enter_context(nc.Block())
        buf_t = buf.rearrange("(e t p) d -> e p t d", p=P, t=TILES)
        y_t = y_rows.rearrange("(e t p) d -> e p t d", p=P, t=TILES)
        w1_t = w1.rearrange("e (c p) h -> e p c h", p=P)
        w2_t = w2.rearrange("e (j p) d -> e p j d", p=P)
        LOADS = 5

        @block.sync
        def _(sp):
            def load(e, u, used):
                if used is not None:
                    sp.wait_ge(y_ready, used)
                for dst, src in ((rows[:, u], buf_t[bass.ds(e, 1)].rearrange("a p t d -> p (a t) d")),
                                 (w1_sb[:, u], w1_t[bass.ds(e, 1)].rearrange("a p c h -> p (a c) h")),
                                 (b1_sb[:, u], b1[bass.ds(e, 1)].rearrange("a p j -> p (a j)")),
                                 (w2_sb[:, u], w2_t[bass.ds(e, 1)].rearrange("a p j d -> p (a j) d")),
                                 (b2_sb[:, u], b2[bass.ds(e, 1), :].broadcast_to([P, D]))):
                    sp.dma_start(dst, src).then_inc(loaded[u], 16)

            with sp.Fori(0, EXPERTS // 2) as i:
                for u in range(2):
                    load(2 * i + u, u, (2 * i + u) * TILES if u == 0 else None)
                    if u == 0:
                        sp.wait_ge(y_ready, 2 * i * TILES)

        @block.gpsimd
        def _(pool):
            with pool.Fori(0, EXPERTS // 2) as i:
                for u in range(2):
                    pool.wait_ge(y_ready, TILES * (2 * i + u + 1))
                    pool.dma_start(y_t[bass.ds(2 * i + u, 1)].rearrange("a p t d -> p (a t) d"), y[:, u])\
                        .then_inc(y_stored[u], 16)
            for u in range(2):
                pool.wait_ge(y_stored[u], 16 * EXPERTS // 2)

        @block.tensor
        def _(pe):
            with pe.Fori(0, EXPERTS // 2) as i:
                for u in range(2):
                    pe.wait_ge(loaded[u], 16 * LOADS * (i + 1))
                    pe.wait_ge(rowsT_ready, 2 * (2 * i + u))
                    for k in range(DC):
                        for t in range(TILES):
                            last = pe.transpose(ps[:, k, t * P:(t + 1) * P], rows[:, u, t, k * P:(k + 1) * P],
                                                ident[:, :])
                    last.then_inc(rowsT_full, 1)
                    pe.wait_ge(rowsT_ready, 2 * (2 * i + u) + 2)
                    for j in range(HC):
                        if j < 4:
                            pe.wait_ge(h_ready, HC * (2 * i + u))
                        else:
                            pe.wait_ge(h_ready, HC * (2 * i + u) + j - 3)
                        for k in range(DC):
                            last = pe.matmul(ps[:, 2 + j % 4, :], w1_sb[:, u, k, j * P:(j + 1) * P], rowsT[:, u, k, :],
                                             start=(k == 0), stop=(k == DC - 1))
                        last.then_inc(h_full, 1)
                    pe.wait_ge(h_ready, HC * (2 * i + u + 1))
                    for t in range(TILES):
                        if t < 2:
                            pe.wait_ge(y_ready, TILES * (2 * i + u))
                        else:
                            pe.wait_ge(y_ready, TILES * (2 * i + u) + t - 1)
                        for j in range(HC):
                            last = pe.matmul(ps[:, 6 + t % 2, 0:D], hT[:, u, j, t * P:(t + 1) * P], w2_sb[:, u, j, :],
                                             start=(j == 0), stop=(j == HC - 1))
                        last.then_inc(y_full, 1)

        @block.scalar
        def _(act):
            with act.Fori(0, EXPERTS // 2) as i:
                for u in range(2):
                    act.wait_ge(rowsT_full, 2 * i + u + 1)
                    for k in range(DC):
                        act.activation(rowsT[:, u, k, :], ps[:, k, :], ACT.Copy).then_inc(rowsT_ready, 1)
                    for j in range(HC):
                        act.wait_ge(h_full, HC * (2 * i + u) + j + 1)
                        if j == 0:
                            act.wait_ge(loaded[u], 16 * LOADS * (i + 1))
                        act.activation(hT[:, u, j, :], ps[:, 2 + j % 4, :], ACT.Relu, bias=b1_sb[:, u, j:j + 1])\
                           .then_inc(h_ready, 1)

        @block.vector
        def _(dve):
            with dve.Fori(0, EXPERTS // 2) as i:
                for u in range(2):
                    dve.wait_ge(loaded[u], 16 * LOADS * (i + 1))
                    dve.wait_ge(y_stored[u], 16 * i)
                    for t in range(TILES):
                        dve.wait_ge(y_full, TILES * (2 * i + u) + t + 1)
                        dve.tensor_tensor(y[:, u, t, :], ps[:, 6 + t % 2, 0:D], b2_sb[:, u, :], ALU.add)\
                           .then_inc(y_ready, 1)


def combine_out(nc, c, x_rows, y_rows, gates, slots, out):
    groups = NTOK // (TILES * P)
    with ExitStack() as ctx:
        def sb(name, shape, dt=F32):
            return ctx.enter_context(nc.sbuf_tensor(f"c_{name}", shape, dt))

        def sem(name):
            return ctx.enter_context(nc.semaphore(f"c_{name}"))

        x = sb("x", [P, 2, TILES, D])
        y = sb("y", [P, 2, TILES, D])
        s = sb("s", [P, 2, TILES, D])
        slot = sb("slot", [P, 2, TILES], U32)
        loaded = [sem(f"loaded{u}") for u in range(2)]
        gathered = [sem(f"gathered{u}") for u in range(2)]
        stored = [sem(f"stored{u}") for u in range(2)]
        slot_ready = sem("slot_ready")
        summed = sem("summed")
        spared = sem("spared")
        block = ctx.enter_context(nc.Block())
        x_t = x_rows.rearrange("(g t p) d -> g p t d", p=P, t=TILES)
        out_t = out.rearrange("g (t p) d -> g p t d", p=P)

        @block.sync
        def _(sp):
            with sp.Fori(0, groups // 2) as i:
                for u in range(2):
                    sp.wait_ge(summed, 2 * i)
                    sp.dma_start(x[:, u], x_t[bass.ds(2 * i + u, 1)].rearrange("a p t d -> p (a t) d"))\
                      .then_inc(loaded[u], 16)

        @block.scalar
        def _(act):
            with act.Fori(0, groups // 2) as i:
                for u in range(2):
                    act.wait_ge(summed, 2 * i + u + 1)
                    act.dma_start(out_t[bass.ds(2 * i + u, 1)].rearrange("a p t d -> p (a t) d"), s[:, u])\
                       .then_inc(stored[u], 16)
            for u in range(2):
                act.wait_ge(stored[u], 16 * (groups // 2))

        @block.gpsimd
        def _(pool):
            with pool.Fori(0, groups // 2) as i:
                for u in range(2):
                    pool.wait_ge(summed, 2 * i)
                    pool.wait_ge(slot_ready, 2 * i + u + 1)
                    pool.wait_ge(spared, 2 * i + u)
                    apart(pool, c).then_inc(spared, 1)
                    for t in range(TILES):
                        pool.indirect_dma_start(y[:, u, t, :], None, y_rows,
                                                bass.IndirectOffsetOnAxis(slot[:, u, t:t + 1], 0),
                                                bounds_check=NTOK - 1, oob_is_err=False).then_inc(gathered[u], 16)

        @block.vector
        def _(dve):
            with dve.Fori(0, groups // 2) as i:
                for u in range(2):
                    dve.wait_ge(gathered[u], 16 * TILES * i)
                    dve.tensor_copy(slot[:, u, :], slots[:, bass.ds((2 * i + u) * TILES, TILES)]).then_inc(slot_ready, 1)
                for u in range(2):
                    dve.wait_ge(loaded[u], 16 * (i + 1))
                    dve.wait_ge(gathered[u], 16 * TILES * (i + 1))
                    dve.wait_ge(stored[u], 16 * i)
                    for t in range(TILES):
                        last = dve.scalar_tensor_tensor(out=s[:, u, t, :], in0=y[:, u, t, :],
                                                        scalar=gates[:, bass.ds((2 * i + u) * TILES + t, 1)],
                                                        in1=x[:, u, t, :], op0=ALU.mult, op1=ALU.add)
                    last.then_inc(summed, 1)


def settle(nc, c, x_rows, y_rows, gates, slots, norm_w, b_out, xr_rows, hT_d):
    ident = c["ident"]
    groups = NTOK // SEQ
    with ExitStack() as ctx:
        def sb(name, shape, dt=F32):
            return ctx.enter_context(nc.sbuf_tensor(f"n_{name}", shape, dt))

        def sem(name):
            return ctx.enter_context(nc.semaphore(f"n_{name}"))

        x = sb("x", [P, TILES, D])
        y = sb("y", [P, TILES, D])
        x2 = sb("x2", [P, TILES, D])
        res = sb("res", [P, TILES, D])
        h = sb("h", [P, TILES, D])
        hT = sb("hT", [P, DC, SEQ])
        xr = sb("xr", [P, TILES, D])
        xb = sb("xb", [P, TILES, D])
        nw = sb("nw", [P, DC])
        bo = sb("bo", [P, D])
        slot = sb("slot", [P, TILES], U32)
        stats = sb("stats", [P, 2, TILES, 6])
        mv = sb("mv", [P, 2, TILES, 2])
        veps = sb("veps", [P, 2, TILES])
        square = sb("square", [P, TILES])
        meansq = sb("meansq", [P, TILES])
        rstd = sb("rstd", [P, 2, TILES])
        ps = ctx.enter_context(nc.psum_tensor("n_ps", [P, 2, 512], F32))
        weights_in = sem("weights_in")
        x_loaded = sem("x_loaded")
        slot_ready = sem("slot_ready")
        gathered = sem("gathered")
        dve_step = sem("dve_step")
        x2_ready = sem("x2_ready")
        veps_ready = sem("veps_ready")
        rstd_ready = sem("rstd_ready")
        h_ready = sem("h_ready")
        hT_full = sem("hT_full")
        hT_ready = sem("hT_ready")
        xr_ready = sem("xr_ready")
        xb_ready = sem("xb_ready")
        xb_stored = sem("xb_stored")
        hT_stored = sem("hT_stored")
        block = ctx.enter_context(nc.Block())
        x_t = x_rows.rearrange("(g t p) d -> g p t d", p=P, t=TILES)
        xr_t = xr_rows.rearrange("(g t p) d -> g p t d", p=P, t=TILES)

        @block.sync
        def _(sp):
            sp.dma_start(nw[:, :], norm_w).then_inc(weights_in, 16)
            sp.dma_start(bo[:, :], b_out.rearrange("(a e) -> a e", a=1).broadcast_to([P, D])).then_inc(weights_in, 16)
            with sp.Fori(0, groups) as g:
                sp.wait_ge(x2_ready, g)
                sp.dma_start(x[:, :, :], x_t[bass.ds(g, 1)].rearrange("a p t d -> p (a t) d")).then_inc(x_loaded, 16)
                sp.wait_ge(xb_ready, g + 1)
                sp.dma_start(xr_t[bass.ds(g, 1)].rearrange("a p t d -> p (a t) d"), xb[:, :, :]).then_inc(xb_stored, 16)
            sp.wait_ge(xb_stored, 16 * groups)

        @block.gpsimd
        def _(pool):
            pool.wait_ge(weights_in, 32)
            with pool.Fori(0, groups) as g:
                pool.wait_ge(x2_ready, g)
                pool.wait_ge(slot_ready, g + 1)
                apart(pool, c)
                for t in range(TILES):
                    pool.indirect_dma_start(y[:, t, :], None, y_rows, bass.IndirectOffsetOnAxis(slot[:, t:t + 1], 0),
                                            bounds_check=NTOK - 1, oob_is_err=False).then_inc(gathered, 16)
                for k in range(2):
                    pool.wait_ge(veps_ready, 2 * g + k + 1)
                    pool.tensor_tensor(rstd[:, k, :], veps[:, k, :], c["power"][:, :], ALU.pow).then_inc(rstd_ready, 1)
                pool.wait_ge(xr_ready, g + 1)
                pool.wait_ge(xb_stored, 16 * g)
                pool.tensor_tensor(xb[:, :, :], xr[:, :, :], bo[:, :].unsqueeze(1).broadcast_to([P, TILES, D]),
                                   ALU.add).then_inc(xb_ready, 1)

        @block.tensor
        def _(pe):
            with pe.Fori(0, groups) as g:
                pe.wait_ge(h_ready, g + 1)
                pe.wait_ge(hT_ready, 2 * g)
                for k in range(DC):
                    for t in range(TILES):
                        last = pe.transpose(ps[:, k, t * P:(t + 1) * P], h[:, t, k * P:(k + 1) * P], ident[:, :])
                last.then_inc(hT_full, 1)

        @block.scalar
        def _(act):
            act.wait_ge(weights_in, 32)
            with act.Fori(0, groups) as g:
                act.wait_ge(hT_full, g + 1)
                act.wait_ge(hT_stored, 16 * g)
                for k in range(DC):
                    act.activation(hT[:, k, :], ps[:, k, :], ACT.Copy, scale=nw[:, k:k + 1]).then_inc(hT_ready, 1)
                act.wait_ge(hT_ready, 2 * g + 2)
                act.dma_start(hT_d[:, :, bass.ds(g * SEQ, SEQ)], hT[:, :, :]).then_inc(hT_stored, 16)
            act.wait_ge(hT_stored, 16 * groups)

        @block.vector
        def _(dve):
            steps = 6
            with dve.Fori(0, groups) as g:
                done = [0]

                def link(ins, alone=False):
                    done[0] += 1
                    ins.then_inc(dve_step, 1)
                    dve.wait_ge(dve_step, steps * g + done[0])
                    if alone:
                        apart(dve, c)

                dve.wait_ge(gathered, 16 * TILES * g)
                dve.tensor_copy(slot[:, :], slots[:, bass.ds(g * TILES, TILES)]).then_inc(slot_ready, 1)
                dve.wait_ge(x_loaded, 16 * g + 16)
                dve.wait_ge(gathered, 16 * TILES * (g + 1))
                for t in range(TILES):
                    last = dve.scalar_tensor_tensor(out=x2[:, t, :], in0=y[:, t, :], scalar=gates[:, bass.ds(g * TILES + t, 1)],
                                                    in1=x[:, t, :], op0=ALU.mult, op1=ALU.add)
                last.then_inc(x2_ready, 1)
                dve.wait_ge(x2_ready, g + 1)
                for t in range(TILES):
                    last = dve.bn_stats(stats[:, 0, t, :], x2[:, t, :])
                link(last, alone=True)
                for t in range(TILES):
                    last = dve.bn_aggr(mv[:, 0, t, :], stats[:, 0, t, :])
                link(last)
                dve.tensor_scalar(veps[:, 0, :], mv[:, 0, :, 1], LN_EPS, None, ALU.add).then_inc(veps_ready, 1)
                dve.wait_ge(rstd_ready, 2 * g + 1)
                for t in range(TILES):
                    last = dve.tensor_scalar(res[:, t, :], x2[:, t, :], mv[:, 0, t, 0:1], rstd[:, 0, t:t + 1],
                                             ALU.subtract, ALU.mult)
                link(last)
                for t in range(TILES):
                    last = dve.bn_stats(stats[:, 1, t, :], res[:, t, :])
                link(last, alone=True)
                for t in range(TILES):
                    last = dve.bn_aggr(mv[:, 1, t, :], stats[:, 1, t, :])
                link(last)
                link(dve.tensor_tensor(square[:, :], mv[:, 1, :, 0], mv[:, 1, :, 0], ALU.mult))
                dve.scalar_tensor_tensor(out=veps[:, 1, :], in0=mv[:, 1, :, 1], scalar=EPS, in1=square[:, :],
                                         op0=ALU.add, op1=ALU.add).then_inc(veps_ready, 1)
                dve.wait_ge(xb_ready, g)
                dve.tensor_tensor(xr[:, :, :], x2[:, :, :], res[:, :, :], ALU.add).then_inc(xr_ready, 1)
                dve.wait_ge(rstd_ready, 2 * g + 2)
                dve.wait_ge(hT_full, g)
                for t in range(TILES):
                    last = dve.tensor_scalar(h[:, t, :], res[:, t, :], rstd[:, 1, t:t + 1], None, ALU.mult)
                last.then_inc(h_ready, 1)
                assert done[0] == steps, done


def state_space(nc, c, hT_d, win, b_in, conv_w, conv_b, a_bd, at_bd, b_bd, b_col, c_col, yT_d):
    ident, head_of, group_of = c["ident"], c["head_of"], c["group_of"]
    with ExitStack() as ctx:
        def sb(name, shape, dt=F32):
            return ctx.enter_context(nc.sbuf_tensor(f"s_{name}", shape, dt))

        def sem(name):
            return ctx.enter_context(nc.semaphore(f"s_{name}"))

        win_sb = sb("win", [P, DC, P])
        bias = sb("bias", [P, 2])
        taps = sb("taps", [P, KW])
        pw = sb("pw", [P, NPAIR, P + CHUNK])
        qv = sb("qv", [P, NPAIR, CHUNK + P])
        cb = sb("cb", [P, 2, NPAIR])
        at = sb("at", [P, NPAIR, P])
        bb = sb("bb", [P, NPAIR, 8])
        wo = sb("wo", [P, NPAIR, CHUNK])
        k_sb = sb("k", [8, NPAIR, CHUNK])
        zero = sb("zero", [P, CHUNK])
        tc_rev = sb("tc_rev", [P, CHUNK, CHUNK])
        tc_sb = sb("tc", [P, CHUNK, CHUNK])
        tbd = sb("tbd", [P, CHUNK, P])
        obd = sb("obd", [P, CHUNK, P])
        rbd = sb("rbd", [P, CHUNK, P])
        hb = sb("hb", [P, 2, DC, SEQ])
        upad = sb("upad", [P, 2, KW - 1 + SEQ])
        acc = sb("acc", [P, SEQ])
        ut = sb("ut", [P, CHUNK, NCH, BATCH])
        xs = sb("xs", [P, NPAIR, NCH, BATCH])
        yts = sb("yts", [P, 2, SEQ])
        ps = ctx.enter_context(nc.psum_tensor("s_ps", [P, 8, 512], F32))
        kpad = nc.dram_tensor("s_kpad", (GRP, NPAIR, 2, 2 * CHUNK), F32, kind="Internal").ap()

        zeroed = sem("zeroed")
        kpad_zero = sem("kpad_zero")
        loaded = sem("loaded")
        hb_loaded = [sem(f"hb_loaded{u}") for u in range(2)]
        first_ready = sem("first_ready")
        proj_full = sem("proj_full")
        u_ready = sem("u_ready")
        conv_step = sem("conv_step")
        ut_ready = sem("ut_ready")
        ring_full = sem("ring_full")
        act_read = sem("act_read")
        dve_read = sem("dve_read")
        k_stored = sem("k_stored")
        tc_loaded = sem("tc_loaded")
        tc_turned = sem("tc_turned")
        v_spread = sem("v_spread")
        o_spread = sem("o_spread")
        t_spread = sem("t_spread")
        yt_ready = sem("yt_ready")
        y_stored = [sem(f"y_stored{u}") for u in range(2)]
        block = ctx.enter_context(nc.Block())

        groups = [range(3 * g, min(3 * g + 3, NPAIR)) for g in range((NPAIR + 2) // 3)]
        uses, reader = [], []

        def plan(key, who):
            uses.append(key)
            reader.append(who)

        for level in range(5):
            for g in range(len(groups)):
                plan(("P", level, g), "act")
                plan(("Q", level, g), "act")
        plan(("O",), "act")
        plan(("K",), "act")
        for n in range(8):
            plan(("R", n), "act")
        for n in range(8):
            plan(("S", n), "act")
        for s in range(4):
            for n in range(8):
                plan(("X", s, n), "dve")
            if s < 3:
                for g in range(len(groups)):
                    plan(("P", 5 + s, g), "act")
                    if s < 2:
                        plan(("Q", 5 + s, g), "act")
        for n in range(NPAIR):
            plan(("Y", n), "act" if n % 2 else "dve")
        NU = len(uses)
        number = {key: n for n, key in enumerate(uses)}
        read_by = [reader[:n + 1].count(reader[n]) for n in range(NU)]
        NA, ND = reader.count("act"), reader.count("dve")
        reads = {"act": (act_read, NA), "dve": (dve_read, ND)}

        def bank(key):
            return 2 + number[key] % 6

        def wait_read(eng, q, key):
            n = number[key]
            s, per = reads[reader[n]]
            eng.wait_ge(s, per * q + read_by[n])

        @block.sync
        def _(sp):
            sp.wait_ge(zeroed, 2)
            rows = kpad.rearrange("g p j n -> (g p j) n")
            sp.dma_start(rows[:, 0:CHUNK], zero[:, :]).then_inc(kpad_zero, 16)
            sp.wait_ge(kpad_zero, 16)
            with sp.Fori(0, QC) as q:
                sp.wait_ge(ring_full, NU * q)
                sp.dma_start(hb[:, 0], hT_d[:, :, 0:SEQ]).then_inc(hb_loaded[0], 16)
                one = bass.ds(q, 1)
                for dst, src in ((pw[:, :, 0:P], a_bd[one].rearrange("a p i n -> p (a i) n")),
                                 (qv[:, :, CHUNK:], at_bd[one].rearrange("a p i n -> p (a i) n")),
                                 (at[:, :, :], at_bd[one].rearrange("a p i n -> p (a i) n")),
                                 (cb[:, 0, :], c_col[one].rearrange("a p i -> p (a i)")),
                                 (cb[:, 1, :], b_col[one].rearrange("a p i -> p (a i)")),
                                 (bb[:, :, :], b_bd[one].rearrange("a p i n -> p (a i) n")),
                                 (win_sb[:, :, :], win[one].rearrange("a p c n -> p (a c) n")),
                                 (bias[:, 0:1], b_in[one].rearrange("a p n -> p (a n)")),
                                 (bias[:, 1:2], conv_b[one].rearrange("a p n -> p (a n)")),
                                 (taps[:, :], conv_w[one].rearrange("a p n -> p (a n)"))):
                    sp.dma_start(dst, src).then_inc(loaded, 16)
                for b in range(1, BATCH):
                    if b >= 2:
                        sp.wait_ge(proj_full, BATCH * q + b - 1)
                    sp.dma_start(hb[:, b % 2], hT_d[:, :, b * SEQ:(b + 1) * SEQ]).then_inc(hb_loaded[b % 2], 16)
                wait_read(sp, q, ("K",))
                for j in range(2):
                    sp.dma_start(kpad[:, :, j, CHUNK:], k_sb[GRP * j:GRP * (j + 1)]).then_inc(k_stored, 16)
                sp.wait_ge(k_stored, 32 * q + 32)
                sp.wait_ge(tc_turned, q)
                for g in range(GRP):
                    src = bass.AP(kpad.tensor, g * CHUNK * 2 * CHUNK + 1,
                                  [[1, CHUNK], [2 * CHUNK, CHUNK], [1, CHUNK]])
                    sp.dma_start(tc_rev[CHUNK * g:CHUNK * (g + 1)], src).then_inc(tc_loaded, 16)
                for b in range(BATCH):
                    sp.wait_ge(yt_ready, BATCH * q + b + 1)
                    sp.dma_start(yT_d[bass.ds(q, 1), :, b * SEQ:(b + 1) * SEQ].rearrange("a p n -> p (a n)"),
                                 yts[:, b % 2, :]).then_inc(y_stored[b % 2], 16)
            for u in range(2):
                sp.wait_ge(y_stored[u], 16 * QC * BATCH // 2)

        @block.gpsimd
        def _(pool):
            pool.memset(zero[:, :], 0.0).then_inc(zeroed, 1)
            pool.memset(upad[:, :, 0:KW - 1], 0.0).then_inc(zeroed, 1)

            def spread(out, src, mask):
                return pool.tensor_tensor(out.rearrange("p i (g t) -> p i g t", g=GRP),
                                          src.unsqueeze(2).broadcast_to([P, src.shape[1], GRP, CHUNK]),
                                          mask.unsqueeze(1).unsqueeze(3).broadcast_to([P, src.shape[1], GRP, CHUNK]),
                                          ALU.mult)

            with pool.Fori(0, QC) as q:
                wait_read(pool, q, ("Q", 4, len(groups) - 1))
                for j in range(2):
                    last = spread(tbd[:, j::2, :], qv[:, :, 0:CHUNK], head_of[:, GRP * j:GRP * (j + 1)])
                last.then_inc(v_spread, 1)
                wait_read(pool, q, ("O",))
                for j in range(2):
                    last = spread(obd[:, j::2, :], wo[:, :, :], head_of[:, GRP * j:GRP * (j + 1)])
                last.then_inc(o_spread, 1)
                wait_read(pool, q, ("R", 7))
                pool.wait_ge(tc_turned, q + 1)
                spread(tbd[:, :, :], tc_sb[:, :, :], group_of[:, :]).then_inc(t_spread, 1)

        @block.tensor
        def _(pe):
            pe.wait_ge(zeroed, 2)
            with pe.Fori(0, QC) as q:
                pe.wait_ge(loaded, 160 * q + 160)
                pe.wait_ge(first_ready, 2 * q + 2)
                pe.wait_ge(act_read, NA * q)
                pe.wait_ge(dve_read, ND * q)

                def begin(key):
                    n = number[key]
                    if n >= 6:
                        wait_read(pe, q, uses[n - 6])
                    return bank(key)

                def project(b):
                    pe.wait_ge(hb_loaded[b % 2], 16 * (BATCH // 2) * q + 16 * (b // 2 + 1))
                    if b >= 2:
                        pe.wait_ge(u_ready, BATCH * q + b - 1)
                    else:
                        pe.wait_ge(u_ready, BATCH * q)
                    for k in range(DC):
                        last = pe.matmul(ps[:, b % 2, :], win_sb[:, k, :], hb[:, b % 2, k, :],
                                         start=(k == 0), stop=(k == DC - 1))
                    last.then_inc(proj_full, 1)

                def square(level, g):
                    w = 2 ** level if level < 5 else 0
                    if level:
                        wait_read(pe, q, ("Q", level - 1, g))
                    for side in "PQ":
                        key = (side, level, g)
                        if key not in number:
                            continue
                        bk = begin(key)
                        for n, p in enumerate(groups[g]):
                            if side == "P":
                                stay, move = qv[:, p, CHUNK:], pw[:, p, 0:P + w]
                            else:
                                stay, move = pw[:, p, 0:P], qv[:, p, CHUNK - w:]
                            last = pe.matmul(ps[:, bk, n * (P + w):(n + 1) * (P + w)], stay, move,
                                             start=True, stop=True)
                        last.then_inc(ring_full, 1)

                steps = [(level, g) for level in range(5) for g in range(len(groups))]
                for b in range(BATCH):
                    project(b)
                    for level, g in steps[2 * b:2 * b + 2]:
                        square(level, g)
                wait_read(pe, q, ("Q", 4, len(groups) - 1))
                bk = begin(("O",))
                for p in range(NPAIR):
                    last = pe.matmul(ps[:, bk, p * CHUNK:(p + 1) * CHUNK], at[:, p, :], pw[:, p, P:],
                                     start=True, stop=True)
                last.then_inc(ring_full, 1)
                bk = begin(("K",))
                for p in range(NPAIR):
                    last = pe.matmul(ps[0:8, bk, p * CHUNK:(p + 1) * CHUNK], bb[:, p, :], pw[:, p, P:],
                                     start=True, stop=True)
                last.then_inc(ring_full, 1)
                pe.wait_ge(v_spread, q + 1)
                for n in range(8):
                    bk = begin(("R", n))
                    for i in range(4):
                        last = pe.transpose(ps[:, bk, i * P:(i + 1) * P], tbd[:, 4 * n + i, :], ident[:, :])
                    last.then_inc(ring_full, 1)
                pe.wait_ge(ut_ready, BATCH * (q + 1))
                per = NCH * BATCH
                for n in range(8):
                    if n == 0:
                        wait_read(pe, q, ("R", 7))
                    bk = begin(("S", n))
                    for m in range(2):
                        for j in range(2):
                            i = 2 * (2 * n + m) + j
                            last = pe.matmul(ps[:, bk, m * per:(m + 1) * per], rbd[:, i, :],
                                             ut[:, i, :, :].rearrange("p c b -> p (c b)"), start=(j == 0), stop=(j == 1))
                    last.then_inc(ring_full, 1)
                for s in range(4):
                    far = 2 ** s
                    for n in range(8):
                        wait_read(pe, q, ("X", s - 1, n) if s else ("S", n))
                        bk = begin(("X", s, n))
                        for m in range(2):
                            last = pe.matmul(ps[:, bk, m * per:m * per + (NCH - far) * BATCH], pw[:, 2 * n + m, 0:P],
                                             xs[:, 2 * n + m, 0:NCH - far, :].rearrange("p c b -> p (c b)"),
                                             start=True, stop=True)
                        last.then_inc(ring_full, 1)
                    if s < 3:
                        for g in range(len(groups)):
                            square(5 + s, g)
                        wait_read(pe, q, ("P", 5 + s, len(groups) - 1))
                pe.wait_ge(t_spread, q + 1)
                pe.wait_ge(o_spread, q + 1)
                wait_read(pe, q, ("X", 3, 7))
                for n in range(NPAIR):
                    bk = begin(("Y", n))
                    for j in range(2):
                        i = 2 * n + j
                        pe.matmul(ps[:, bk, j * per:(j + 1) * per], tbd[:, i, :],
                                  ut[:, i, :, :].rearrange("p c b -> p (c b)"), start=True, stop=False)
                        last = pe.matmul(ps[:, bk, j * per + BATCH:(j + 1) * per], obd[:, i, :],
                                         xs[:, n, 0:NCH - 1, :].rearrange("p c b -> p (c b)"), start=False, stop=True)
                    last.then_inc(ring_full, 1)

        def full(eng, q, key):
            eng.wait_ge(ring_full, NU * q + number[key] + 1)

        @block.scalar
        def _(act):
            with act.Fori(0, QC) as q:
                act.wait_ge(loaded, 160 * q + 160)
                act.wait_ge(o_spread, q)
                act.activation(pw[:, :, P], cb[:, 0, :], ACT.Copy).then_inc(first_ready, 1)
                act.activation(qv[:, :, CHUNK - 1], cb[:, 1, :], ACT.Copy).then_inc(first_ready, 1)
                act.wait_ge(k_stored, 32 * q)

                def take(b):
                    act.wait_ge(proj_full, BATCH * q + b + 1)
                    if b >= 2:
                        act.wait_ge(ut_ready, BATCH * q + b - 1)
                    act.activation(upad[:, b % 2, KW - 1:], ps[:, b % 2, :], ACT.Identity, bias=bias[:, 0:1])\
                       .then_inc(u_ready, 1)

                def squared(level, g):
                    w = 2 ** level if level < 5 else 0
                    a, z = groups[g][0], groups[g][-1] + 1
                    full(act, q, ("Q", level, g) if ("Q", level, g) in number else ("P", level, g))
                    for side in "PQ":
                        key = (side, level, g)
                        if key not in number:
                            continue
                        src = ps[:, bank(key), 0:(z - a) * (P + w)].rearrange("p (i n) -> p i n", n=P + w)
                        if side == "P":
                            if w:
                                act.activation(pw[:, a:z, P + w:P + 2 * w], src[:, :, P:], ACT.Copy)
                            last = act.activation(pw[:, a:z, 0:P], src[:, :, 0:P], ACT.Copy)
                        else:
                            if w:
                                act.activation(qv[:, a:z, CHUNK - 2 * w:CHUNK - w], src[:, :, 0:w], ACT.Copy)
                            last = act.activation(qv[:, a:z, CHUNK:], src[:, :, w:], ACT.Copy)
                        last.then_inc(act_read, 1)

                steps = [(level, g) for level in range(5) for g in range(len(groups))]
                for b in range(BATCH):
                    take(b)
                    for level, g in steps[2 * b:2 * b + 2]:
                        squared(level, g)
                full(act, q, ("O",))
                act.activation(wo[:, :, :].rearrange("p i n -> p (i n)"), ps[:, bank(("O",)), :], ACT.Copy)\
                   .then_inc(act_read, 1)
                full(act, q, ("K",))
                act.activation(k_sb[:, :, :].rearrange("p i n -> p (i n)"), ps[0:8, bank(("K",)), :], ACT.Copy)\
                   .then_inc(act_read, 1)
                for n in range(8):
                    full(act, q, ("R", n))
                    act.activation(rbd[:, 4 * n:4 * n + 4, :].rearrange("p i n -> p (i n)"), ps[:, bank(("R", n)), :],
                                   ACT.Copy).then_inc(act_read, 1)
                for n in range(8):
                    full(act, q, ("S", n))
                    act.activation(xs[:, 2 * n:2 * n + 2, :, :].rearrange("p i c b -> p (i c b)"),
                                   ps[:, bank(("S", n)), :], ACT.Copy).then_inc(act_read, 1)
                for s in range(3):
                    for g in range(len(groups)):
                        squared(5 + s, g)
                for n in range(1, NPAIR, 2):
                    full(act, q, ("Y", n))
                    act.activation(ut[:, 2 * n:2 * n + 2, :, :].rearrange("p i c b -> p (i c b)"),
                                   ps[:, bank(("Y", n)), :], ACT.Copy).then_inc(act_read, 1)

        @block.vector
        def _(dve):
            dve.wait_ge(zeroed, 2)
            with dve.Fori(0, QC) as q:
                dve.wait_ge(loaded, 160 * q + 160)
                for b in range(BATCH):
                    dve.wait_ge(u_ready, BATCH * q + b + 1)
                    dve.wait_ge(ut_ready, BATCH * q + b)
                    u = upad[:, b % 2, :]
                    dve.tensor_scalar(acc[:, :], u[:, KW - 1:], taps[:, KW - 1:KW], bias[:, 1:2], ALU.mult, ALU.add)\
                       .then_inc(conv_step, 1)
                    for k in range(1, KW):
                        dve.wait_ge(conv_step, KW * (BATCH * q + b) + k)
                        dve.scalar_tensor_tensor(out=acc[:, :], in0=u[:, KW - 1 - k:KW - 1 - k + SEQ],
                                                 scalar=taps[:, KW - 1 - k:KW - k], in1=acc[:, :],
                                                 op0=ALU.mult, op1=ALU.add).then_inc(conv_step, 1)
                    dve.wait_ge(conv_step, KW * (BATCH * q + b) + KW)
                    dve.transpose(ut[:, :, :, b].rearrange("p i c -> p c i"),
                                  acc[:, :].rearrange("p (c t) -> p c t", t=CHUNK)).then_inc(ut_ready, 1)
                dve.wait_ge(tc_loaded, 16 * GRP * (q + 1))
                dve.wait_ge(t_spread, q)
                apart(dve, c)
                dve.stream_shuffle(tc_sb[:, :, :].rearrange("p i t -> p (i t)"),
                                   tc_rev[:, :, :].rearrange("p i t -> p (i t)"),
                                   mask=[CHUNK - 1 - k for k in range(CHUNK)]).then_inc(tc_turned, 1)
                for s in range(4):
                    far = 2 ** s
                    n_cols = (NCH - far) * BATCH
                    for n in range(8):
                        full(dve, q, ("X", s, n))
                        src = ps[:, bank(("X", s, n)), :].rearrange("p (i n) -> p i n", i=2)[:, :, 0:n_cols]
                        dst = xs[:, 2 * n:2 * n + 2, far:, :].rearrange("p i c b -> p i (c b)")
                        dve.tensor_tensor(dst, src, dst, ALU.add).then_inc(dve_read, 1)
                for n in range(0, NPAIR, 2):
                    full(dve, q, ("Y", n))
                    dve.tensor_copy(ut[:, 2 * n:2 * n + 2, :, :].rearrange("p i c b -> p (i c b)"),
                                    ps[:, bank(("Y", n)), :]).then_inc(dve_read, 1)
                wait_read(dve, q, ("Y", NPAIR - 1))
                wait_read(dve, q, ("Y", NPAIR - 2))
                for b in range(BATCH):
                    if b >= 2:
                        dve.wait_ge(y_stored[b % 2], 16 * (BATCH // 2) * q + 16 * (b // 2))
                    else:
                        dve.wait_ge(y_stored[b % 2], 16 * (BATCH // 2) * q)
                    dve.transpose(yts[:, b % 2, :].rearrange("p (c t) -> p c t", t=CHUNK),
                                  ut[:, :, :, b].rearrange("p i c -> p c i")).then_inc(yt_ready, 1)
                dve.wait_ge(yt_ready, BATCH * (q + 1))


def project_out(nc, yT_d, wout, xr_rows, x3_rows):
    with ExitStack() as ctx:
        def sb(name, shape, dt=F32):
            return ctx.enter_context(nc.sbuf_tensor(f"o_{name}", shape, dt))

        def sem(name):
            return ctx.enter_context(nc.semaphore(f"o_{name}"))

        w = sb("w", [P, QC, D])
        yT = sb("yT", [P, 2, QC, SEQ])
        xr = sb("xr", [P, 2, TILES, D])
        x3 = sb("x3", [P, 2, TILES, D])
        ps = ctx.enter_context(nc.psum_tensor("o_ps", [P, 8, 512], F32))
        weights_in = sem("weights_in")
        loaded = [sem(f"loaded{u}") for u in range(2)]
        stored = [sem(f"stored{u}") for u in range(2)]
        full = sem("full")
        summed = sem("summed")
        block = ctx.enter_context(nc.Block())
        xr_t = xr_rows.rearrange("(g t p) d -> g p t d", p=P, t=TILES)
        x3_t = x3_rows.rearrange("(g t p) d -> g p t d", p=P, t=TILES)
        y_t = yT_d.rearrange("q p (g n) -> g p q n", n=SEQ)

        @block.sync
        def _(sp):
            sp.dma_start(w[:, :, :], wout.rearrange("(q p) d -> p q d", p=P)).then_inc(weights_in, 16)
            with sp.Fori(0, BATCH // 2) as i:
                for u in range(2):
                    sp.wait_ge(summed, TILES * 2 * i)
                    one = bass.ds(2 * i + u, 1)
                    sp.dma_start(yT[:, u], y_t[one].rearrange("a p q n -> p (a q) n")).then_inc(loaded[u], 16)
                    sp.dma_start(xr[:, u], xr_t[one].rearrange("a p t d -> p (a t) d")).then_inc(loaded[u], 16)

        @block.gpsimd
        def _(pool):
            with pool.Fori(0, BATCH // 2) as i:
                for u in range(2):
                    pool.wait_ge(summed, TILES * (2 * i + u + 1))
                    pool.dma_start(x3_t[bass.ds(2 * i + u, 1)].rearrange("a p t d -> p (a t) d"), x3[:, u])\
                        .then_inc(stored[u], 16)
            for u in range(2):
                pool.wait_ge(stored[u], 16 * BATCH // 2)

        @block.tensor
        def _(pe):
            pe.wait_ge(weights_in, 16)
            with pe.Fori(0, BATCH // 2) as i:
                for u in range(2):
                    pe.wait_ge(loaded[u], 32 * (i + 1))
                    pe.wait_ge(summed, TILES * 2 * i)
                    for t in range(TILES):
                        for k in range(QC):
                            last = pe.matmul(ps[:, TILES * u + t, 0:D], yT[:, u, k, t * P:(t + 1) * P], w[:, k, :],
                                             start=(k == 0), stop=(k == QC - 1))
                        last.then_inc(full, 1)

        @block.vector
        def _(dve):
            with dve.Fori(0, BATCH // 2) as i:
                for u in range(2):
                    dve.wait_ge(loaded[u], 32 * (i + 1))
                    dve.wait_ge(stored[u], 16 * i)
                    for t in range(TILES):
                        dve.wait_ge(full, TILES * (2 * i + u) + t + 1)
                        dve.tensor_tensor(x3[:, u, t, :], ps[:, TILES * u + t, 0:D], xr[:, u, t, :], ALU.add)\
                           .then_inc(summed, 1)


def copy_rows(nc, src, dst):
    with nc.semaphore("filled") as filled, nc.Block() as block:
        @block.sync
        def _(sp):
            sp.dma_start(dst, src).then_inc(filled, 16)
            sp.wait_ge(filled, 16)


def hybrid_block(nc, x, w_qkv, w_ky, w_proj, norm_w, win, b_in, conv_w, conv_b, a_bd, at_bd, b_bd, b_col, c_col,
                 wout, b_out, wg, bg, w1, b1, w2, b2, out):
    def dram(name, shape):
        return nc.dram_tensor(name, shape, F32, kind="Internal").ap()

    x1 = dram("x1", (NTOK, D))
    xr = dram("xr", (NTOK, D))
    x3 = dram("x3", (NTOK, D))
    rows = dram("rows", (NTOK, D))
    y = dram("y", (NTOK, D))
    hT = dram("hT", (P, DC, NTOK))
    yT = dram("yT", (QC, P, NTOK))
    with ExitStack() as ctx:
        def sb(name, shape, dt):
            return ctx.enter_context(nc.sbuf_tensor(name, shape, dt))

        c = constants(nc, sb)
        gates = sb("gates", [P, NTOK // P], F32)
        slots = sb("slots", [P, NTOK // P], U32)
        copy_rows(nc, x.rearrange("b s d -> (b s) d"), rows)
        attention(nc, c, x, w_qkv, w_ky, w_proj, x1)
        route(nc, c, "r1", x1, wg, bg, rows, gates, slots)
        experts(nc, c, "e1", rows, w1, b1, w2, b2, y)
        settle(nc, c, x1, y, gates, slots, norm_w, b_out, xr, hT)
        state_space(nc, c, hT, win, b_in, conv_w, conv_b, a_bd, at_bd, b_bd, b_col, c_col, yT)
        project_out(nc, yT, wout, xr, x3)
        route(nc, c, "r2", x3, wg, bg, rows, gates, slots)
        experts(nc, c, "e2", rows, w1, b1, w2, b2, y)
        combine_out(nc, c, x3, y, gates, slots, out)


def layouts(i):
    import numpy as np

    def groups(a):
        a = a.reshape(QC, GRP, NPAIR, 2, *a.shape[1:])
        return a.transpose(0, 2, 3, 1, *range(4, a.ndim)).reshape(QC, NPAIR, 8, *a.shape[4:])

    def diagonal(a):
        q, p, e, n, m = a.shape
        out = np.zeros((q, e, n, p, e, m), a.dtype)
        for k in range(e):
            out[:, k, :, :, k, :] = a[:, :, k].transpose(0, 2, 1, 3)
        return out.reshape(q, e * n, p, e * m)

    A = groups(i["L0_attn_b_A"])
    B = groups(i["L0_attn_b_Bm"])
    C = groups(i["L0_attn_b_Cm"].transpose(0, 2, 1))

    def column(a):
        return a.reshape(QC, NPAIR, P).transpose(0, 2, 1)

    return {
        "x": i["L0_attn_a_x"],
        "w_qkv": i["L0_attn_a_w_qkv"].T,
        "w_ky": i["L0_attn_a_w_ky"].T,
        "w_proj": i["L0_attn_a_w_proj"].T,
        "norm_w": i["L0_attn_b_norm_w"].reshape(DC, P).T,
        "win": i["L0_attn_b_Win"].reshape(DC, P, QC, P).transpose(2, 1, 0, 3),
        "b_in": i["L0_attn_b_b_in"].reshape(QC, P, 1),
        "conv_w": i["L0_attn_b_conv_w"].reshape(QC, P, KW),
        "conv_b": i["L0_attn_b_conv_b"].reshape(QC, P, 1),
        "a_bd": diagonal(A),
        "at_bd": diagonal(A.transpose(0, 1, 2, 4, 3)),
        "b_bd": diagonal(B),
        "b_col": column(B),
        "c_col": column(C),
        "wout": i["L0_attn_b_Wout"],
        "b_out": i["L0_attn_b_b_out"],
        "wg": i["L0_ffn_Wg"],
        "bg": i["L0_ffn_bg"],
        "w1": i["L0_ffn_W1"],
        "b1": i["L0_ffn_b1"].reshape(EXPERTS, HC, P).transpose(0, 2, 1),
        "w2": i["L0_ffn_W2"],
        "b2": i["L0_ffn_b2"],
    }


def kernel(**inputs):
    import numpy as np
    import concourse.bacc as bacc
    from concourse.bass_utils import run_bass_kernel_spmd

    nc = bacc.Bacc("TRN2", target_bir_lowering=False, num_devices=1)
    arrays, args = {}, {}
    for name, a in layouts({k: np.asarray(v) for k, v in inputs.items()}).items():
        a = np.ascontiguousarray(a)
        arrays[f"in_{name}"] = a
        args[name] = nc.dram_tensor(f"in_{name}", a.shape, mybir.dt.from_np(a.dtype), kind="ExternalInput").ap()
    out = nc.dram_tensor("out", (BATCH, SEQ, D), F32, kind="ExternalOutput").ap()
    hybrid_block(nc, out=out, **args)
    r = run_bass_kernel_spmd(nc, [arrays], core_ids=[0])
    return r.results[0]["out"]
```

```python
import concourse.bass as bass
from concourse import mybir
from contextlib import ExitStack

P = 128
F32 = mybir.dt.float32
F32R = mybir.dt.float32r
U32 = mybir.dt.uint32
I32 = mybir.dt.int32
ALU = mybir.AluOpType
ACT = mybir.ActivationFunctionType
AX = mybir.AxisListType

BATCH, SEQ, D = 16, 512, 256
NTOK = BATCH * SEQ
TILES = SEQ // P
DC = D // P
HEADS, HD = 16, 16
HPC = P // HD
PAIRS = HEADS // 2
VW = 32
EXPERTS, HID = 16, 1024
CAP = NTOK // EXPERTS
HC = HID // P
DIN = 512
NST = 16
CHUNK = 32
NCH = SEQ // CHUNK
QC = DIN // P
GRP = P // CHUNK
NPAIR = CHUNK // 2
KW = 4
COLS = TILES * (TILES + 1) // 2 * P
PLACE = {512: 0, 384: 512, 128: 896, 256: 1024}
START = 1
LN_EPS = 1e-5
EPS = 1e-6
LIMIT = 60.0


def constants(nc, sb):
    c = {
        "ident": sb("ident", [P, P], F32),
        "cap": sb("cap", [P, COLS], F32),
        "causal": sb("causal", [P, COLS], F32),
        "magnitude": sb("magnitude", [P, COLS], I32),
        "head_of": sb("head_of", [P, HPC], F32),
        "group_of": sb("group_of", [P, GRP], F32),
        "experts": sb("experts", [P, EXPERTS], F32),
        "experts_i": sb("experts_i", [P, EXPERTS], I32),
        "spare": sb("spare", [P, 2], F32),
        "power": sb("power", [P, TILES], F32),
    }
    with nc.semaphore("made") as made, nc.semaphore("bits") as bits, nc.Block() as block:
        @block.gpsimd
        def _(pool):
            pool.memset(c["ident"][:, :], 0.0)
            pool.memset(c["cap"][:, :], LIMIT)
            pool.memset(c["causal"][:, :], 1.0)
            pool.memset(c["head_of"][:, :], 1.0)
            pool.memset(c["group_of"][:, :], 1.0)
            pool.memset(c["power"][:, :], -0.5)
            pool.iota(c["experts_i"][:, :], [[1, EXPERTS]], base=0, channel_multiplier=0).then_inc(made, 1)
            pool.wait_ge(made, 1)
            pool.tensor_copy(c["experts"][:, :], c["experts_i"][:, :])
            pool.affine_select(out=c["ident"][:, :], in_=c["ident"][:, :], compare_op=ALU.not_equal, fill=1.0,
                               base=0, pattern=[[-1, P]], channel_multiplier=1)
            for t in range(TILES):
                n = (t + 1) * P
                v = c["cap"][:, PLACE[n]:PLACE[n] + n]
                pool.affine_select(out=v, in_=v, compare_op=ALU.is_ge, fill=-4e4, base=t * P,
                                   pattern=[[-1, n]], channel_multiplier=1)
                v = c["causal"][:, PLACE[n]:PLACE[n] + n]
                pool.affine_select(out=v, in_=v, compare_op=ALU.is_ge, fill=0.0, base=0,
                                   pattern=[[1, n]], channel_multiplier=-1)
            for name, width, n in (("head_of", HD, HPC), ("group_of", CHUNK, GRP)):
                m = c[name][:, :]
                pool.affine_select(out=m, in_=m, compare_op=ALU.is_ge, fill=0.0, base=0,
                                   pattern=[[-width, n]], channel_multiplier=1).then_inc(made, 1)
            pool.wait_ge(made, 3)
            for name, width, n in (("head_of", HD, HPC), ("group_of", CHUNK, GRP)):
                m = c[name][:, :]
                last = pool.affine_select(out=m, in_=m, compare_op=ALU.is_ge, fill=0.0, base=width - 1,
                                          pattern=[[width, n]], channel_multiplier=-1)
            last.then_inc(made, 1)
            pool.wait_ge(made, 4)

        @block.vector
        def _(dve):
            m = c["magnitude"][:, :]
            dve.wait_ge(made, 4)
            dve.tensor_copy(m, c["causal"][:, :]).then_inc(bits, 1)
            dve.wait_ge(bits, 1)
            dve.tensor_scalar(m, m, 31, 31, ALU.logical_shift_left, ALU.arith_shift_right).then_inc(bits, 1)
            dve.wait_ge(bits, 2)
            dve.tensor_scalar(m, m, 0x7FFFFFFF, None, ALU.bitwise_and).then_inc(bits, 1)
            dve.wait_ge(bits, 3)
    return c


def apart(eng, c):
    if eng.engine == mybir.EngineType.DVE:
        return eng.memset(c["spare"][:, 0:1], 0.0)
    return eng.tensor_tensor(c["spare"][:, 1:2], c["power"][:, 0:1], c["power"][:, 0:1], ALU.mult)


def prime(nc, semaphores):
    with nc.Block() as block:
        @block.sync
        def _(sp):
            for s, software in semaphores:
                sp.sem_clear(s)
                if not software:
                    sp.sem_inc(s, START)


def selections(nc, c, made_in, sel):
    with nc.semaphore("a_zeroed") as zeroed, nc.semaphore("a_chosen") as chosen, nc.semaphore("a_sel") as moved, \
            nc.Block() as block:
        @block.gpsimd
        def _(pool):
            pool.memset(made_in[:, :, :], 0.0).then_inc(zeroed, 1)
            pool.wait_ge(zeroed, 1)
            for p in range(HPC // 2):
                for side in range(2):
                    for half in range(2):
                        m = made_in[:, 4 * p + 2 * side + half, :].rearrange("k (j a d) -> k j a d", j=2, a=4)
                        m = m[:, :, half::2, :] if side == 0 else m[:, :, 2 * half:2 * half + 2, :]
                        last = pool.affine_select(out=m, in_=m, compare_op=ALU.not_equal, fill=1.0, base=-2 * HD * p,
                                                  pattern=[[-HD, 2], [0, 2], [-1, HD]], channel_multiplier=1)
            last.then_inc(chosen, 1)

        @block.vector
        def _(dve):
            dve.wait_ge(chosen, 1)
            dve.tensor_copy(sel[:, :, :], made_in[:, :, :]).then_inc(moved, 1)
            dve.wait_ge(moved, 1)


def attention(nc, c, x, wqkv, wky, wproj, x1):
    ident, cap, causal = c["ident"], c["cap"], c["causal"]
    ones = causal[:, P:2 * P]
    upper = causal[:, 0:P]
    primed = []
    STATS_AT, NORM_AT = 5, 9
    with ExitStack() as ctx:
        def sb(name, shape, dt=F32):
            return ctx.enter_context(nc.sbuf_tensor(name, shape, dt))

        def sem(name, software=False):
            s = ctx.enter_context(nc.semaphore(name))
            primed.append((s, software))
            return s

        sel = sb("a_sel", [P, 2 * HPC, P], F32R)
        with nc.sbuf_tensor("a_made_in", [P, 2 * HPC, P], F32) as made_in:
            selections(nc, c, made_in, sel)
        w_sb = sb("a_w", [P, DC, 3 * D])
        wky_sb = sb("a_wky", [P, DC, D])
        wp_sb = sb("a_wp", [P, DC, D])
        x_in = sb("a_x", [P, TILES, D])
        x_res = sb("a_xres", [P, TILES, D])
        stats = sb("a_stats", [P, TILES, 6])
        mv = sb("a_mv", [P, TILES, 2])
        veps = sb("a_veps", [P, TILES])
        rstd = sb("a_rstd", [P, TILES])
        xn = sb("a_xn", [P, TILES, D])
        xnT = sb("a_xnT", [P, DC, SEQ])
        qT = sb("a_qT", [P, DC, SEQ])
        q2T = sb("a_q2T", [P, DC, SEQ])
        halves = sb("a_halves", [P, 3, 2, DC, SEQ], F32R)
        q_stack = sb("a_q_stack", [P, PAIRS, SEQ], F32R)
        k_stack = sb("a_k_stack", [P, PAIRS, SEQ], F32R)
        ky_stack = sb("a_ky_stack", [P, PAIRS, SEQ], F32R)
        v = sb("a_v", [P, TILES, HEADS, VW])
        clipped = sb("a_clipped", [P, 2, COLS])
        agg = sb("a_agg", [P, TILES, HEADS])
        agg1 = sb("a_agg1", [P, TILES, HEADS])
        agg2 = sb("a_agg2", [P, TILES, HEADS])
        inv1 = sb("a_inv1", [P, TILES, HEADS])
        inv2 = sb("a_inv2", [P, TILES, HEADS])
        rx = sb("a_rx", [P, TILES, HEADS, HD])
        shift = sb("a_shift", [P, TILES, HEADS])
        ratio = sb("a_ratio", [P, 2, COLS])
        weight = sb("a_weight", [P, 3, COLS])
        headT = sb("a_headT", [P, SEQ])
        av = sb("a_av", [P, TILES, HEADS, VW])
        t1 = sb("a_t1", [P, HEADS, HD + 1])
        t2 = sb("a_t2", [P, HEADS, HD + 1])
        den = sb("a_den", [P, HEADS])
        rden = sb("a_rden", [P, HEADS])
        o = sb("a_o", [P, TILES, D])
        oT = sb("a_oT", [P, DC, SEQ])
        x1_sb = sb("a_x1", [P, TILES, D])
        ps = ctx.enter_context(nc.psum_tensor("a_ps", [P, 8, 512], F32))
        flat = ps[:, :, :].rearrange("p b n -> p (b n)")

        weights_in = sem("weights_in")
        x_loaded = sem("x_loaded")
        xres_loaded = sem("xres_loaded")
        x1_stored = sem("x1_stored")
        v_ones = sem("v_ones")
        ln_step = sem("ln_step")
        veps_ready = sem("veps_ready")
        rstd_ready = sem("rstd_ready")
        xn_ready = sem("xn_ready")
        misc_full = sem("misc_full")
        misc_read = sem("misc_read")
        lo_ready = sem("lo_ready")
        q_stacked = sem("q_stacked")
        ky_stacked = sem("ky_stacked")
        k_stacked = sem("k_stacked")
        q_stack_ready = sem("q_stack_ready")
        ky_stack_ready = sem("ky_stack_ready")
        k_stack_ready = sem("k_stack_ready")
        e_scores = sem("e_scores")
        clip_done = sem("clip_done")
        exp_done = sem("exp_done")
        agg_step = sem("agg_step")
        rx_ready = sem("rx_ready")
        shift_ready = sem("shift_ready")
        rT_full = sem("rT_full")
        q2_step = sem("q2_step")
        q2_stacked = sem("q2_stacked")
        q2_even_ready = sem("q2_even_ready")
        q2_odd_ready = sem("q2_odd_ready")
        w_scores = sem("w_scores")
        abs_done = sem("abs_done")
        ln_done = sem("ln_done")
        av_done = sem("av_done")
        headT_ready = sem("headT_ready")
        ot_full = sem("ot_full")
        av_read = sem("av_read")
        cv_full = sem("cv_full")
        norm_step = sem("norm_step")
        o_ready = sem("o_ready")
        oT_full = sem("oT_full")
        oT_ready = sem("oT_ready")
        proj_full = sem("proj_full")
        x1_ready = sem("x1_ready")
        prime(nc, primed)
        block = ctx.enter_context(nc.Block())

        x_t = x.rearrange("b (t p) d -> b p t d", p=P)
        x1_t = x1.rearrange("(b t p) d -> b p t d", p=P, t=TILES)

        def score_place(n):
            return slice(PLACE[n], PLACE[n] + n)

        @block.sync
        def _(sp):
            sp.dma_start(x_in[:, :, :], x_t[0]).then_inc(x_loaded, 16)
            sp.dma_start(w_sb[:, :, :], wqkv.rearrange("(c p) n -> p c n", p=P)).then_inc(weights_in, 16)
            sp.dma_start(wky_sb[:, :, :], wky.rearrange("(c p) n -> p c n", p=P)).then_inc(weights_in, 16)
            sp.dma_start(wp_sb[:, :, :], wproj.rearrange("(c p) n -> p c n", p=P)).then_inc(weights_in, 16)

            def turn(b, last):
                sp.wait_ge(x1_ready, START + 2 * b)
                sp.dma_start(x_res[:, :, :], x_t[bass.ds(b, 1)].rearrange("a p t d -> p (a t) d")
                             if not last else x_t[BATCH - 1]).then_inc(xres_loaded, 16)
                if not last:
                    sp.wait_ge(xn_ready, START + b + 1)
                    sp.dma_start(x_in[:, :, :], x_t[bass.ds(b + 1, 1)].rearrange("a p t d -> p (a t) d"))\
                      .then_inc(x_loaded, 16)
                sp.wait_ge(x1_ready, START + 2 * b + 2)
                sp.dma_start(x1_t[bass.ds(b, 1)].rearrange("a p t d -> p (a t) d") if not last
                             else x1_t[BATCH - 1], x1_sb[:, :, :]).then_inc(x1_stored, 16)

            with sp.Fori(0, BATCH - 1) as b:
                turn(b, False)
            turn(BATCH - 1, True)
            sp.wait_ge(x1_stored, START + 16 * BATCH)

        @block.gpsimd
        def _(pool):
            pool.memset(v[:, :, :, HD:VW], 0.0).then_inc(v_ones, 1)
            pool.wait_ge(v_ones, START + 1)
            pool.memset(v[:, :, :, HD:HD + 1], 1.0).then_inc(v_ones, 1)

            def rms(b):
                pool.wait_ge(veps_ready, START + b + 1)
                pool.tensor_tensor(rstd[:, :], veps[:, :], c["power"][:, :], ALU.pow).then_inc(rstd_ready, 1)

            with pool.Fori(0, BATCH) as b:
                rms(b)

        @block.tensor
        def _(pe):
            pe.wait_ge(weights_in, START + 48)
            pe.wait_ge(v_ones, START + 2)
            def stack(bank, which, p):
                side = min(which, 1)
                for half in range(2):
                    last = pe.matmul(ps[:, bank, :], sel[:, 4 * (p % (HPC // 2)) + 2 * side + half, :],
                                     halves[:, which, half, 2 * p // HPC, :], start=(half == 0), stop=(half == 1))
                return last

            def project(b, first):
                pe.wait_ge(xn_ready, START + b + 1)
                if not first:
                    pe.wait_ge(headT_ready, START + 4 * b)
                    pe.wait_ge(av_read, START + 4 * b)
                for k in range(DC):
                    for t in range(TILES):
                        last = pe.transpose(ps[:, 6 + k, t * P:(t + 1) * P], xn[:, t, k * P:(k + 1) * P],
                                            ident[:, :])
                    last.then_inc(misc_full, 1)
                for m in range(2, 10):
                    if m < 4:
                        pe.wait_ge(misc_read, START + 10 * b + 2)
                    else:
                        pe.wait_ge(lo_ready, START + 6 * b + m - 3)
                    bank = 6 + m % 2
                    if m < 8:
                        which, half = (m - 2) // 2, m % 2
                        w = wky_sb if which == 2 else w_sb
                        col = (D if which == 1 else 0) + half * P
                        for k in range(DC):
                            last = pe.matmul(ps[:, bank, :], w[:, k, col:col + P], xnT[:, k, :],
                                             start=(k == 0), stop=(k == DC - 1))
                    else:
                        for i in range(2):
                            t = 2 * (m - 8) + i
                            for k in range(DC):
                                last = pe.matmul(ps[:, bank, i * D:(i + 1) * D], xnT[:, k, t * P:(t + 1) * P],
                                                 w_sb[:, k, 2 * D:3 * D], start=(k == 0), stop=(k == DC - 1))
                    last.then_inc(misc_full, 1)

                pe.wait_ge(lo_ready, START + 6 * b + 6)
                for p in range(PAIRS):
                    if p == 1:
                        pe.wait_ge(misc_read, START + 10 * b + 10)
                    elif p:
                        pe.wait_ge(q_stack_ready, START + PAIRS * b + p - 1)
                    stack(4 + 2 * (p % 2), 0, p).then_inc(q_stacked, 1)
                    if p >= 2:
                        pe.wait_ge(ky_stack_ready, START + PAIRS * b + p - 1)
                    stack(5 + 2 * (p % 2), 2, p).then_inc(ky_stacked, 1)

            def turn(b, last_turn):
                pe.wait_ge(q_stack_ready, START + PAIRS * b + PAIRS)
                pe.wait_ge(ky_stack_ready, START + PAIRS * b + PAIRS)
                for h in range(HEADS):
                    if h >= 2:
                        pe.wait_ge(clip_done, START + HEADS * b + h - 1)
                    base = 3 * 512 * (h % 2)
                    r = P // 2 * (h % 2)
                    for t in range(TILES):
                        n = (t + 1) * P
                        last = pe.matmul(flat[:, base + PLACE[n]:base + PLACE[n] + n],
                                         q_stack[r:r + P // 2, h // 2, t * P:(t + 1) * P],
                                         ky_stack[r:r + P // 2, h // 2, 0:n], start=True, stop=True)
                    last.then_inc(e_scores, 1)
                    if h % 2:
                        p = h // 2
                        if p == 0:
                            pe.wait_ge(x1_ready, START + 2 * b)
                        elif p >= 2:
                            pe.wait_ge(k_stack_ready, START + PAIRS * b + p - 1)
                        stack(6 + p % 2, 1, p).then_inc(k_stacked, 1)
                pe.wait_ge(rx_ready, START + b + 1)
                pe.wait_ge(k_stack_ready, START + PAIRS * b + PAIRS)
                for k in range(DC):
                    for t in range(TILES):
                        last = pe.transpose(ps[:, 6 + k, t * P:(t + 1) * P],
                                            rx[:, t, k * HPC:(k + 1) * HPC, :].rearrange("p h d -> p (h d)"),
                                            ident[:, :])
                    last.then_inc(rT_full, 1)
                pe.wait_ge(q2_step, START + 6 * b + 6)
                for p in range(PAIRS):
                    stack((p + 6) % 8, 0, p).then_inc(q2_stacked, 1)
                pe.wait_ge(q2_even_ready, START + PAIRS // 2 * (b + 1))
                pe.wait_ge(q2_odd_ready, START + PAIRS // 2 * (b + 1))

                def scores(h):
                    if h >= 2:
                        pe.wait_ge(abs_done, START + HEADS * b + h - 1)
                    base = 3 * 512 * (h % 2)
                    r = P // 2 * (h % 2)
                    for t in range(TILES):
                        n = SEQ - t * P
                        last = pe.matmul(flat[:, base + PLACE[n]:base + PLACE[n] + n],
                                         k_stack[r:r + P // 2, h // 2, t * P:(t + 1) * P],
                                         q_stack[r:r + P // 2, h // 2, t * P:SEQ],
                                         start=True, stop=True)
                    last.then_inc(w_scores, 1)

                def values(h):
                    pe.wait_ge(ln_done, START + HEADS * b + h + 1)
                    if h % 4 == 0 and h:
                        pe.wait_ge(headT_ready, START + 4 * b + h // 4)
                    r = 32 * (h % 4)
                    for t in range(TILES):
                        last = pe.matmul(ps[r:r + VW, 6, t * P:SEQ], v[:, t, h, :],
                                         weight[:, h % 3, score_place(SEQ - t * P)],
                                         start=(t == 0), stop=(t == TILES - 1))
                    last.then_inc(av_done, 1)

                def turn_back(g):
                    pe.wait_ge(headT_ready, START + 4 * b + g + 1)
                    if g:
                        pe.wait_ge(av_read, START + 4 * b + g)
                    for t in range(TILES):
                        last = pe.transpose(ps[:, 7, t * P:(t + 1) * P], headT[:, t * P:(t + 1) * P], ident[:, :])
                    last.then_inc(ot_full, 1)

                for h in range(HEADS + 3):
                    if h < HEADS:
                        scores(h)
                    if h >= 3:
                        values(h - 3)
                    if h >= 7 and h % 4 == 3:
                        turn_back((h - 7) // 4)
                turn_back(3)
                pe.wait_ge(abs_done, START + HEADS * b + HEADS)
                for t in range(TILES):
                    for s in range(t + 1):
                        last = pe.matmul(ps[:, t, 0:HEADS * (HD + 1)], upper if s == t else ones,
                                         v[:, s, :, 0:HD + 1], start=(s == 0), stop=(s == t))
                    last.then_inc(cv_full, 1)
                if not last_turn:
                    project(b + 1, False)
                if not last_turn:
                    pe.wait_ge(q_stack_ready, START + PAIRS * (b + 2))
                    pe.wait_ge(ky_stack_ready, START + PAIRS * (b + 2))
                for t in range(TILES):
                    pe.wait_ge(o_ready, START + TILES * b + t + 1)
                    for k in range(DC):
                        last = pe.transpose(ps[:, 4 + k, t * P:(t + 1) * P], o[:, t, k * P:(k + 1) * P],
                                            ident[:, :])
                last.then_inc(oT_full, 1)
                pe.wait_ge(oT_ready, START + 2 * b + 2)
                if last_turn:
                    pe.wait_ge(av_read, START + 4 * b + 4)
                for t in range(TILES):
                    for k in range(DC):
                        last = pe.matmul(ps[:, 6 + t // 2, (t % 2) * D:(t % 2 + 1) * D],
                                         oT[:, k, t * P:(t + 1) * P], wp_sb[:, k, :],
                                         start=(k == 0), stop=(k == DC - 1))
                    if t % 2:
                        last.then_inc(proj_full, 1)

            project(0, True)
            with pe.Fori(0, BATCH - 1) as b:
                turn(b, False)
            turn(BATCH - 1, True)

        @block.scalar
        def _(act):
            def project(b):
                for m in range(10):
                    act.wait_ge(misc_full, START + 10 * b + m + 1)
                    src = ps[:, 6 + m % 2, :]
                    if m < 2:
                        dst = xnT[:, m, :]
                    elif m < 8:
                        if m < 4:
                            act.wait_ge(q2_step, START + 6 * b)
                            act.activation(qT[:, m % 2, :], src, ACT.Copy)
                        dst = halves[:, m // 2 - 1, 0, m % 2, :]
                    else:
                        t = 2 * (m - 8)
                        dst = v[:, t:t + 2, :, 0:HD].rearrange("p t h d -> p (t h) d")
                        src = src.rearrange("p (t d) -> p t d", d=HD)
                    act.activation(dst, src, ACT.Copy).then_inc(misc_read, 1)
                for p in range(PAIRS):
                    act.wait_ge(q_stacked, START + PAIRS * b + p + 1)
                    act.activation(q_stack[:, p, :], ps[:, 4 + 2 * (p % 2), :], ACT.Copy).then_inc(q_stack_ready, 1)

            def turn(b, last_turn):
                for h in range(HEADS):
                    act.wait_ge(clip_done, START + HEADS * b + h + 1)
                    if h == 0:
                        act.wait_ge(rx_ready, START + b)
                    for t in range(TILES):
                        n = (t + 1) * P
                        last = act.activation(clipped[:, h % 2, score_place(n)], clipped[:, h % 2, score_place(n)], ACT.Exp, scale=0.25,
                                              accum_out=agg[:, t, h:h + 1])
                    last.then_inc(exp_done, 1)
                act.wait_ge(rx_ready, START + b + 1)
                act.activation(shift[:, :, :], inv1[:, :, :], ACT.Ln, scale=EPS, bias=1.0).then_inc(shift_ready, 1)

                for p in range(0, PAIRS, 2):
                    act.wait_ge(q2_stacked, START + PAIRS * b + p + 1)
                    act.activation(q_stack[:, p, :], ps[:, (p + 6) % 8, :], ACT.Copy).then_inc(q2_even_ready, 1)

                def head_rows(g):
                    act.wait_ge(av_done, START + HEADS * b + 4 * g + 4)
                    if g:
                        act.wait_ge(ot_full, START + 4 * b + g)
                    act.activation(headT[:, :], ps[:, 6, :], ACT.Copy).then_inc(headT_ready, 1)

                for h in range(HEADS):
                    act.wait_ge(abs_done, START + HEADS * b + h + 1)
                    if h >= 3:
                        act.wait_ge(av_done, START + HEADS * b + h - 2)
                    act.activation(weight[:, h % 3, :], ratio[:, h % 2, :], ACT.Ln, bias=1.0).then_inc(ln_done, 1)
                    if h >= 5 and h % 4 == 1:
                        head_rows((h - 5) // 4)
                head_rows(3)
                if not last_turn:
                    project(b + 1)
                act.wait_ge(oT_full, START + b + 1)
                for k in range(DC):
                    act.activation(oT[:, k, :], ps[:, 4 + k, :], ACT.Copy).then_inc(oT_ready, 1)

            project(0)
            with act.Fori(0, BATCH - 1) as b:
                turn(b, False)
            turn(BATCH - 1, True)

        @block.vector
        def _(dve):
            def statistics(b):
                dve.wait_ge(x_loaded, START + 16 * b + 16)
                for t in range(TILES):
                    last = dve.bn_stats(stats[:, t, :], x_in[:, t, :])
                last.then_inc(ln_step, 1)
                dve.wait_ge(ln_step, START + 2 * b + 1)
                apart(dve, c)
                for t in range(TILES):
                    last = dve.bn_aggr(mv[:, t, :], stats[:, t, :])
                last.then_inc(ln_step, 1)
                dve.wait_ge(ln_step, START + 2 * b + 2)
                dve.tensor_scalar(veps[:, :], mv[:, :, 1], LN_EPS, None, ALU.add).then_inc(veps_ready, 1)

            def normalise(b, first):
                dve.wait_ge(rstd_ready, START + b + 1)
                if not first:
                    dve.wait_ge(misc_full, START + 10 * b - 8)
                for t in range(TILES):
                    last = dve.tensor_scalar(xn[:, t, :], x_in[:, t, :], mv[:, t, 0:1], rstd[:, t:t + 1],
                                             ALU.subtract, ALU.mult)
                last.then_inc(xn_ready, 1)

            def low(b, m):
                dve.wait_ge(misc_read, START + 10 * b + m + 1)
                high = halves[:, m // 2 - 1, 0, m % 2, :]
                dve.tensor_tensor(halves[:, m // 2 - 1, 1, m % 2, :], ps[:, 6 + m % 2, :], high, ALU.subtract)\
                   .then_inc(lo_ready, 1)

            def ky_stacks(b):
                for p in range(PAIRS):
                    dve.wait_ge(ky_stacked, START + PAIRS * b + p + 1)
                    dve.tensor_copy(ky_stack[:, p, :], ps[:, 5 + 2 * (p % 2), :]).then_inc(ky_stack_ready, 1)

            def turn(b, last_turn):
                for h in range(HEADS):
                    dve.wait_ge(e_scores, START + HEADS * b + h + 1)
                    if h >= 2:
                        dve.wait_ge(exp_done, START + HEADS * b + h - 1)
                    elif h == 0:
                        dve.wait_ge(exp_done, START + HEADS * b)
                    base = 3 * 512 * (h % 2)
                    dve.scalar_tensor_tensor(out=clipped[:, h % 2, :], in0=flat[:, base:base + COLS], scalar=-LIMIT,
                                             in1=cap[:, :], op0=ALU.max, op1=ALU.min).then_inc(clip_done, 1)
                    if h % 2:
                        p = h // 2
                        dve.wait_ge(k_stacked, START + PAIRS * b + p + 1)
                        dve.tensor_copy(k_stack[:, p, :], ps[:, 6 + p % 2, :]).then_inc(k_stack_ready, 1)
                dve.wait_ge(exp_done, START + HEADS * b + HEADS)
                dve.wait_ge(shift_ready, START + b)
                dve.tensor_scalar(agg1[:, :, :], agg[:, :, :], EPS, None, ALU.add).then_inc(agg_step, 1)
                dve.wait_ge(agg_step, START + 3 * b + 1)
                dve.tensor_scalar(agg2[:, :, :], agg1[:, :, :], EPS, None, ALU.add).then_inc(agg_step, 1)
                dve.reciprocal(inv1[:, :, :], agg1[:, :, :])
                dve.wait_ge(agg_step, START + 3 * b + 2)
                dve.reciprocal(inv2[:, :, :], agg2[:, :, :]).then_inc(agg_step, 1)
                dve.wait_ge(agg_step, START + 3 * b + 3)
                dve.tensor_scalar(rx[:, :, :, :].rearrange("p t h d -> p (t h) d"),
                                  inv2[:, :, :].rearrange("p t h -> p (t h)").unsqueeze(2)
                                  .broadcast_to([P, TILES * HEADS, HD]),
                                  0.25, None, ALU.mult).then_inc(rx_ready, 1)
                for k in range(DC):
                    dve.wait_ge(rT_full, START + 2 * b + k + 1)
                    dve.tensor_tensor(q2T[:, k, :], ps[:, 6 + k, :], qT[:, k, :], ALU.mult).then_inc(q2_step, 1)
                for k in range(DC):
                    dve.wait_ge(q2_step, START + 6 * b + k + 1)
                    dve.tensor_copy(halves[:, 0, 0, k, :], q2T[:, k, :]).then_inc(q2_step, 1)
                for k in range(DC):
                    dve.wait_ge(q2_step, START + 6 * b + k + 3)
                    dve.tensor_tensor(halves[:, 0, 1, k, :], q2T[:, k, :], halves[:, 0, 0, k, :],
                                      ALU.subtract).then_inc(q2_step, 1)
                for p in range(1, PAIRS, 2):
                    dve.wait_ge(q2_stacked, START + PAIRS * b + p + 1)
                    dve.tensor_copy(q_stack[:, p, :], ps[:, (p + 6) % 8, :]).then_inc(q2_odd_ready, 1)

                def sums(g):
                    dve.wait_ge(ot_full, START + 4 * b + g + 1)
                    dve.tensor_copy(av[:, :, 4 * g:4 * g + 4, :].rearrange("p t h d -> p t (h d)"),
                                    ps[:, 7, :].rearrange("p (t n) -> p t n", t=TILES)).then_inc(av_read, 1)

                for h in range(HEADS):
                    dve.wait_ge(w_scores, START + HEADS * b + h + 1)
                    if h >= 2:
                        dve.wait_ge(ln_done, START + HEADS * b + h - 1)
                    base = 3 * 512 * (h % 2)
                    dve.tensor_tensor(ratio[:, h % 2, :].bitcast(I32), flat[:, base:base + COLS].bitcast(I32),
                                      c["magnitude"][:, :], ALU.bitwise_and).then_inc(abs_done, 1)
                    if h >= 8 and h % 4 == 0:
                        sums((h - 8) // 4)
                    if h == STATS_AT and not last_turn:
                        statistics(b + 1)
                    if h == NORM_AT and not last_turn:
                        normalise(b + 1, False)
                sums(2)
                sums(3)
                dve.wait_ge(shift_ready, START + b + 1)
                def normed(t):
                    n = 4 * (TILES * b + t)
                    dve.wait_ge(cv_full, START + TILES * b + t + 1)
                    dve.tensor_tensor(t1[:, :, :], ps[:, t, 0:HEADS * (HD + 1)].rearrange("p (h d) -> p h d", h=HEADS),
                                      shift[:, t, :].unsqueeze(2).broadcast_to([P, HEADS, HD + 1]),
                                      ALU.mult).then_inc(norm_step, 1)
                    dve.wait_ge(norm_step, START + n + 1)
                    dve.tensor_tensor(t2[:, :, :], t1[:, :, :], av[:, t, :, 0:HD + 1], ALU.add).then_inc(norm_step, 1)
                    dve.wait_ge(norm_step, START + n + 2)
                    dve.tensor_scalar(den[:, :], t2[:, :, HD], EPS, None, ALU.add).then_inc(norm_step, 1)
                    dve.wait_ge(norm_step, START + n + 3)
                    dve.reciprocal(rden[:, :], den[:, :]).then_inc(norm_step, 1)
                    dve.wait_ge(norm_step, START + n + 4)
                    dve.tensor_tensor(o[:, t, :].rearrange("p (h d) -> p h d", h=HEADS), t2[:, :, 0:HD],
                                      rden[:, :].unsqueeze(2).broadcast_to([P, HEADS, HD]),
                                      ALU.mult).then_inc(o_ready, 1)

                for t in range(TILES):
                    normed(t)
                    if not last_turn and t:
                        low(b + 1, 2 * t)
                        low(b + 1, 2 * t + 1)
                if not last_turn:
                    ky_stacks(b + 1)
                dve.wait_ge(xres_loaded, START + 16 * b + 16)
                dve.wait_ge(x1_stored, START + 16 * b)
                for k in range(2):
                    dve.wait_ge(proj_full, START + 2 * b + k + 1)
                    dve.tensor_tensor(x1_sb[:, 2 * k:2 * k + 2, :].rearrange("p t d -> p (t d)"), ps[:, 6 + k, :],
                                      x_res[:, 2 * k:2 * k + 2, :].rearrange("p t d -> p (t d)"),
                                      ALU.add).then_inc(x1_ready, 1)

            statistics(0)
            normalise(0, True)
            for m in range(2, 8):
                low(0, m)
            ky_stacks(0)
            with dve.Fori(0, BATCH - 1) as b:
                turn(b, False)
            turn(BATCH - 1, True)


def route(nc, c, tag, x_rows, wg, bg, buf, gates, slots):
    ident, causal = c["ident"], c["causal"]
    ones, upper = causal[:, P:2 * P], causal[:, 0:P]
    groups = NTOK // (TILES * P)
    NT = NTOK // P
    half = NT // 2 * EXPERTS
    primed = []
    with ExitStack() as ctx:
        def sb(name, shape, dt=F32):
            return ctx.enter_context(nc.sbuf_tensor(f"{tag}_{name}", shape, dt))

        def sem(name, software=False):
            s = ctx.enter_context(nc.semaphore(f"{tag}_{name}"))
            primed.append((s, software))
            return s

        wg_sb = sb("wg", [P, DC, EXPERTS])
        bg_sb = sb("bg", [P, EXPERTS])
        x = sb("x", [P, 2, TILES, D])
        stats = sb("stats", [P, 2, TILES, 6])
        mv = sb("mv", [P, 2, TILES, 2])
        veps = sb("veps", [P, 2, TILES])
        rstd = sb("rstd", [P, 2, TILES])
        zg = sb("zg", [P, 2, TILES, D])
        z = sb("z", [P, NT, D])
        zT = sb("zT", [P, 2, DC, SEQ])
        logit = sb("logit", [P, NT, EXPERTS])
        best = sb("best", [P, NT])
        tied = sb("tied", [P, NT, EXPERTS])
        index = sb("index", [P, NT, EXPERTS])
        from_last = sb("from_last", [P, EXPERTS])
        expert = sb("expert", [P, NT])
        below = sb("below", [P, NT, EXPERTS])
        total = sb("total", [P, NT])
        gate = sb("gate", [P, NT])
        onehot = sb("onehot", [P, NT, EXPERTS])
        before = sb("before", [P, 2, NT + 1, EXPERTS])
        place = sb("place", [P, NT, EXPERTS])
        count = sb("count", [P, NT])
        kept = sb("kept", [P, NT])
        safe = sb("safe", [P, NT])
        slot = sb("slot", [P, NT])
        away = sb("away", [P, NT])
        target = sb("target", [P, NT])
        row = sb("row", [P, 2, TILES, D])
        row_target = sb("row_target", [P, 2, TILES], U32)
        ps = ctx.enter_context(nc.psum_tensor(f"{tag}_ps", [P, 8, 512], F32))

        weights_in = sem("weights_in")
        x_loaded = [sem(f"x_loaded{u}") for u in range(2)]
        ln_step = sem("ln_step")
        veps_ready = sem("veps_ready")
        rstd_ready = sem("rstd_ready")
        z_ready = sem("z_ready")
        z_kept = sem("z_kept")
        zT_full = sem("zT_full")
        zT_ready = sem("zT_ready")
        logits_full = sem("logits_full")
        logits_ready = sem("logits_ready")
        choice_step = sem("choice_step")
        below_ready = sem("below_ready")
        exp_ready = sem("exp_ready")
        onehot_ready = sem("onehot_ready")
        place_full = sem("place_full")
        row_ready = sem("row_ready")
        target_ready = sem("target_ready")
        row_free = sem("row_free")
        spared = sem("spared")
        scattered = [sem(f"scattered{u}", software=True) for u in range(2)]
        prime(nc, primed)
        block = ctx.enter_context(nc.Block())
        x_t = x_rows.rearrange("(g t p) d -> g p t d", p=P, t=TILES)

        @block.sync
        def _(sp):
            sp.dma_start(wg_sb[:, :, :], wg.rearrange("(c p) e -> p c e", p=P)).then_inc(weights_in, 16)
            sp.dma_start(bg_sb[:, :], bg.rearrange("(a e) -> a e", a=1).broadcast_to([P, EXPERTS])).then_inc(weights_in, 16)
            for u in range(2):
                sp.dma_start(x[:, u], x_t[u]).then_inc(x_loaded[u], 16)
            with sp.Fori(0, groups // 2 - 1) as i:
                for u in range(2):
                    sp.wait_ge(z_ready, START + 2 * i + u + 1)
                    sp.dma_start(x[:, u], x_t[bass.ds(2 * i + u + 2, 1)].rearrange("a p t d -> p (a t) d"))\
                      .then_inc(x_loaded[u], 16)

        @block.gpsimd
        def _(pool):
            with pool.Fori(0, groups // 2) as i:
                for u in range(2):
                    pool.wait_ge(veps_ready, START + 2 * i + u + 1)
                    pool.tensor_tensor(rstd[:, u, :], veps[:, u, :], c["power"][:, :], ALU.pow).then_inc(rstd_ready, 1)
                for u in range(2):
                    pool.wait_ge(z_ready, START + 2 * i + u + 1)
                    pool.tensor_copy(z[:, bass.ds((2 * i + u) * TILES, TILES), :].rearrange("p t d -> p (t d)"),
                                     zg[:, u, :, :].rearrange("p t d -> p (t d)")).then_inc(z_kept, 1)
            with pool.Fori(0, groups // 2) as i:
                for u in range(2):
                    pool.wait_ge(row_ready, START + 2 * i + u + 1)
                    pool.wait_ge(target_ready, START + 2 * i + u + 1)
                    pool.wait_ge(spared, START + 2 * i + u)
                    apart(pool, c).then_inc(spared, 1)
                    for t in range(TILES):
                        pool.indirect_dma_start(buf, bass.IndirectOffsetOnAxis(row_target[:, u, t:t + 1], 0),
                                                row[:, u, t, :], None,
                                                bounds_check=NTOK - 1, oob_is_err=False).then_inc(scattered[u], 16)
                for u in range(2):
                    pool.wait_ge(scattered[u], 16 * TILES * (i + 1))
                    pool.sem_inc(row_free, 1)

        @block.tensor
        def _(pe):
            pe.wait_ge(weights_in, START + 32)
            with pe.Fori(0, groups // 2) as i:
                for u in range(2):
                    pe.wait_ge(z_ready, START + 2 * i + u + 1)
                    pe.wait_ge(zT_ready, START + DC * (2 * i))
                    for k in range(DC):
                        for t in range(TILES):
                            last = pe.transpose(ps[:, DC * u + k, t * P:(t + 1) * P],
                                                zg[:, u, t, k * P:(k + 1) * P], ident[:, :])
                    last.then_inc(zT_full, 1)
                    pe.wait_ge(zT_ready, START + DC * (2 * i + u + 1))
                    pe.wait_ge(logits_ready, START + 2 * i)
                    for t in range(TILES):
                        for k in range(DC):
                            last = pe.matmul(ps[:, 4 + u, t * EXPERTS:(t + 1) * EXPERTS], zT[:, u, k, t * P:(t + 1) * P],
                                             wg_sb[:, k, :], start=(k == 0), stop=(k == DC - 1))
                    last.then_inc(logits_full, 1)
            pe.wait_ge(onehot_ready, START + 1)
            for j, matrix in enumerate((upper, ones)):
                for h in range(2):
                    last = pe.matmul(ps[:, 2 * j + h, :], matrix,
                                     onehot[:, h * NT // 2:(h + 1) * NT // 2, :].rearrange("p t e -> p (t e)"),
                                     start=True, stop=True)
            last.then_inc(place_full, 1)

        @block.scalar
        def _(act):
            with act.Fori(0, groups // 2) as i:
                for u in range(2):
                    act.wait_ge(zT_full, START + 2 * i + u + 1)
                    act.wait_ge(logits_full, START + 2 * i)
                    for k in range(DC):
                        act.activation(zT[:, u, k, :], ps[:, DC * u + k, :], ACT.Copy).then_inc(zT_ready, 1)
                    act.wait_ge(logits_full, START + 2 * i + u + 1)
                    act.activation(logit[:, bass.ds((2 * i + u) * TILES, TILES), :].rearrange("p t e -> p (t e)"),
                                   ps[:, 4 + u, 0:TILES * EXPERTS], ACT.Copy).then_inc(logits_ready, 1)
            act.wait_ge(below_ready, START + 1)
            act.activation(below[:, :, :], below[:, :, :], ACT.Exp).then_inc(exp_ready, 1)
            act.wait_ge(z_kept, START + groups)
            with act.Fori(0, groups // 2) as i:
                for u in range(2):
                    act.wait_ge(row_free, START + 2 * i)
                    act.activation(row[:, u, :, :].rearrange("p t d -> p (t d)"),
                                   z[:, bass.ds((2 * i + u) * TILES, TILES), :].rearrange("p t d -> p (t d)"), ACT.Copy)\
                       .then_inc(row_ready, 1)

        @block.vector
        def _(dve):
            with dve.Fori(0, groups // 2) as i:
                for u in range(2):
                    dve.wait_ge(x_loaded[u], START + 16 * (i + 1))
                    for t in range(TILES):
                        last = dve.bn_stats(stats[:, u, t, :], x[:, u, t, :])
                    last.then_inc(ln_step, 1)
                    dve.wait_ge(ln_step, START + 4 * i + 2 * u + 1)
                    apart(dve, c)
                    for t in range(TILES):
                        last = dve.bn_aggr(mv[:, u, t, :], stats[:, u, t, :])
                    last.then_inc(ln_step, 1)
                    dve.wait_ge(ln_step, START + 4 * i + 2 * u + 2)
                    dve.tensor_scalar(veps[:, u, :], mv[:, u, :, 1], LN_EPS, None, ALU.add).then_inc(veps_ready, 1)
                for u in range(2):
                    dve.wait_ge(z_kept, START + 2 * i)
                    dve.wait_ge(zT_full, START + 2 * i)
                    dve.wait_ge(rstd_ready, START + 2 * i + u + 1)
                    for t in range(TILES):
                        last = dve.tensor_scalar(zg[:, u, t, :], x[:, u, t, :], mv[:, u, t, 0:1],
                                                 rstd[:, u, t:t + 1], ALU.subtract, ALU.mult)
                    last.then_inc(z_ready, 1)
            done = [0]

            def link(ins):
                done[0] += 1
                ins.then_inc(choice_step, 1)
                dve.wait_ge(choice_step, START + done[0])

            def over_experts(a):
                return a.unsqueeze(2).broadcast_to([P, NT, EXPERTS])

            def over_tiles(a):
                return a.unsqueeze(1).broadcast_to([P, NT, EXPERTS])

            dve.wait_ge(weights_in, START + 32)
            dve.wait_ge(logits_ready, START + groups)
            dve.tensor_scalar(from_last[:, :], c["experts"][:, :], float(EXPERTS), None, ALU.subtract)
            dve.memset(before[:, :, 0, :], 0.0)
            link(dve.tensor_tensor(logit[:, :, :], logit[:, :, :], over_tiles(bg_sb[:, :]), ALU.add))
            link(dve.tensor_reduce(best[:, :], logit[:, :, :], AX.X, ALU.max))
            dve.tensor_tensor(below[:, :, :], logit[:, :, :], over_experts(best[:, :]), ALU.subtract).then_inc(below_ready, 1)
            link(dve.tensor_tensor(tied[:, :, :], logit[:, :, :], over_experts(best[:, :]), ALU.is_equal))
            link(dve.tensor_tensor(index[:, :, :], tied[:, :, :], over_tiles(from_last[:, :]), ALU.mult))
            link(dve.tensor_reduce(safe[:, :], index[:, :, :], AX.X, ALU.min))
            link(dve.tensor_scalar(expert[:, :], safe[:, :], float(EXPERTS), None, ALU.add))
            dve.tensor_tensor(onehot[:, :, :], over_tiles(c["experts"][:, :]), over_experts(expert[:, :]), ALU.is_equal)\
               .then_inc(onehot_ready, 1)
            dve.wait_ge(exp_ready, START + 1)
            link(dve.tensor_reduce(total[:, :], below[:, :, :], AX.X, ALU.add))
            link(dve.reciprocal(gate[:, :], total[:, :]))
            dve.wait_ge(place_full, START + 1)
            link(dve.tensor_copy(before[:, 0, 1:, :].rearrange("p (h t) e -> p h (t e)", h=2), ps[:, 2:4, :]))
            far, src = 1, 0
            while far < NT:
                dve.tensor_copy(before[:, 1 - src, 1:far + 1, :], before[:, src, 1:far + 1, :])
                link(dve.tensor_tensor(before[:, 1 - src, far + 1:, :], before[:, src, far + 1:, :],
                                       before[:, src, 1:NT + 1 - far, :], ALU.add))
                far, src = 2 * far, 1 - src
            link(dve.tensor_tensor(place[:, :, :].rearrange("p (h t) e -> p h (t e)", h=2), ps[:, 0:2, :],
                                   before[:, src, 0:NT, :].rearrange("p (h t) e -> p h (t e)", h=2), ALU.add))
            link(dve.tensor_tensor(tied[:, :, :], place[:, :, :], onehot[:, :, :], ALU.mult))
            link(dve.tensor_reduce(count[:, :], tied[:, :, :], AX.X, ALU.add))
            dve.tensor_scalar(kept[:, :], count[:, :], float(CAP), None, ALU.is_le)
            dve.tensor_scalar(away[:, :], count[:, :], float(CAP), float(2 * NTOK), ALU.is_gt, ALU.mult)
            link(dve.tensor_scalar(safe[:, :], count[:, :], float(CAP), -1.0, ALU.min, ALU.add))
            dve.tensor_tensor(gates[:, :], gate[:, :], kept[:, :], ALU.mult)
            link(dve.scalar_tensor_tensor(out=slot[:, :], in0=expert[:, :], scalar=float(CAP), in1=safe[:, :],
                                          op0=ALU.mult, op1=ALU.add))
            dve.tensor_copy(slots[:, :], slot[:, :])
            link(dve.tensor_tensor(target[:, :], slot[:, :], away[:, :], ALU.add))
            with dve.Fori(0, groups // 2) as i:
                for u in range(2):
                    dve.wait_ge(row_free, START + 2 * i)
                    dve.tensor_copy(row_target[:, u, :], target[:, bass.ds((2 * i + u) * TILES, TILES)])\
                       .then_inc(target_ready, 1)


def experts(nc, c, tag, buf, w1, b1, w2, b2, y_rows):
    ident = c["ident"]
    primed = []
    with ExitStack() as ctx:
        def sb(name, shape, dt=F32):
            return ctx.enter_context(nc.sbuf_tensor(f"{tag}_{name}", shape, dt))

        def sem(name, software=False):
            s = ctx.enter_context(nc.semaphore(f"{tag}_{name}"))
            primed.append((s, software))
            return s

        w1_sb = sb("w1", [P, 2, DC, HID])
        w2_sb = sb("w2", [P, 2, HC, D])
        b1_sb = sb("b1", [P, 2, HC])
        b2_sb = sb("b2", [P, 2, D])
        rows = sb("rows", [P, 2, TILES, D])
        rowsT = sb("rowsT", [P, 2, DC, CAP])
        hT = sb("hT", [P, 2, HC, CAP])
        y = sb("y", [P, 2, TILES, D])
        ps = ctx.enter_context(nc.psum_tensor(f"{tag}_ps", [P, 8, 512], F32))
        loaded = [sem(f"loaded{u}") for u in range(2)]
        rowsT_full = sem("rowsT_full")
        rowsT_ready = sem("rowsT_ready")
        h_full = sem("h_full")
        h_ready = sem("h_ready")
        y_full = sem("y_full")
        y_ready = sem("y_ready")
        y_stored = [sem(f"y_stored{u}") for u in range(2)]
        prime(nc, primed)
        block = ctx.enter_context(nc.Block())
        buf_t = buf.rearrange("(e t p) d -> e p t d", p=P, t=TILES)
        y_t = y_rows.rearrange("(e t p) d -> e p t d", p=P, t=TILES)
        w1_t = w1.rearrange("e (c p) h -> e p c h", p=P)
        w2_t = w2.rearrange("e (j p) d -> e p j d", p=P)
        LOADS = 5

        @block.sync
        def _(sp):
            def load(e, u):
                for dst, src in ((rows[:, u], buf_t[bass.ds(e, 1)].rearrange("a p t d -> p (a t) d")),
                                 (w1_sb[:, u], w1_t[bass.ds(e, 1)].rearrange("a p c h -> p (a c) h")),
                                 (b1_sb[:, u], b1[bass.ds(e, 1)].rearrange("a p j -> p (a j)")),
                                 (w2_sb[:, u], w2_t[bass.ds(e, 1)].rearrange("a p j d -> p (a j) d")),
                                 (b2_sb[:, u], b2[bass.ds(e, 1), :].broadcast_to([P, D]))):
                    sp.dma_start(dst, src).then_inc(loaded[u], 16)

            def store(e, u):
                sp.wait_ge(y_ready, START + TILES * (e + 1))
                sp.dma_start(y_t[bass.ds(e, 1)].rearrange("a p t d -> p (a t) d"), y[:, u]).then_inc(y_stored[u], 16)

            for u in range(2):
                load(u, u)
            with sp.Fori(0, EXPERTS // 2 - 1) as i:
                for u in range(2):
                    store(2 * i + u, u)
                    load(2 * i + u + 2, u)
            for u in range(2):
                store(EXPERTS - 2 + u, u)
            for u in range(2):
                sp.wait_ge(y_stored[u], START + 16 * EXPERTS // 2)

        @block.tensor
        def _(pe):
            with pe.Fori(0, EXPERTS // 2) as i:
                for u in range(2):
                    pe.wait_ge(loaded[u], START + 16 * LOADS * (i + 1))
                    pe.wait_ge(rowsT_ready, START + 2 * (2 * i + u))
                    for k in range(DC):
                        for t in range(TILES):
                            last = pe.transpose(ps[:, k, t * P:(t + 1) * P], rows[:, u, t, k * P:(k + 1) * P],
                                                ident[:, :])
                    last.then_inc(rowsT_full, 1)
                    pe.wait_ge(rowsT_ready, START + 2 * (2 * i + u) + 2)
                    for j in range(HC):
                        if j < 4:
                            pe.wait_ge(h_ready, START + HC * (2 * i + u))
                        else:
                            pe.wait_ge(h_ready, START + HC * (2 * i + u) + j - 3)
                        for k in range(DC):
                            last = pe.matmul(ps[:, 2 + j % 4, :], w1_sb[:, u, k, j * P:(j + 1) * P], rowsT[:, u, k, :],
                                             start=(k == 0), stop=(k == DC - 1))
                        last.then_inc(h_full, 1)
                    pe.wait_ge(h_ready, START + HC * (2 * i + u + 1))
                    for t in range(TILES):
                        if t < 2:
                            pe.wait_ge(y_ready, START + TILES * (2 * i + u))
                        else:
                            pe.wait_ge(y_ready, START + TILES * (2 * i + u) + t - 1)
                        for j in range(HC):
                            last = pe.matmul(ps[:, 6 + t % 2, 0:D], hT[:, u, j, t * P:(t + 1) * P], w2_sb[:, u, j, :],
                                             start=(j == 0), stop=(j == HC - 1))
                        last.then_inc(y_full, 1)

        @block.scalar
        def _(act):
            with act.Fori(0, EXPERTS // 2) as i:
                for u in range(2):
                    act.wait_ge(rowsT_full, START + 2 * i + u + 1)
                    for k in range(DC):
                        act.activation(rowsT[:, u, k, :], ps[:, k, :], ACT.Copy).then_inc(rowsT_ready, 1)
                    for j in range(HC):
                        act.wait_ge(h_full, START + HC * (2 * i + u) + j + 1)
                        if j == 0:
                            act.wait_ge(loaded[u], START + 16 * LOADS * (i + 1))
                        act.activation(hT[:, u, j, :], ps[:, 2 + j % 4, :], ACT.Relu, bias=b1_sb[:, u, j:j + 1])\
                           .then_inc(h_ready, 1)

        @block.vector
        def _(dve):
            with dve.Fori(0, EXPERTS // 2) as i:
                for u in range(2):
                    dve.wait_ge(loaded[u], START + 16 * LOADS * (i + 1))
                    dve.wait_ge(y_stored[u], START + 16 * i)
                    for t in range(TILES):
                        dve.wait_ge(y_full, START + TILES * (2 * i + u) + t + 1)
                        dve.tensor_tensor(y[:, u, t, :], ps[:, 6 + t % 2, 0:D], b2_sb[:, u, :], ALU.add)\
                           .then_inc(y_ready, 1)


def combine_out(nc, c, x_rows, y_rows, gates, slots, out):
    groups = NTOK // (TILES * P)
    primed = []
    with ExitStack() as ctx:
        def sb(name, shape, dt=F32):
            return ctx.enter_context(nc.sbuf_tensor(f"c_{name}", shape, dt))

        def sem(name, software=False):
            s = ctx.enter_context(nc.semaphore(f"c_{name}"))
            primed.append((s, software))
            return s

        x = sb("x", [P, 2, TILES, D])
        y = sb("y", [P, 2, TILES, D])
        s = sb("s", [P, 2, TILES, D])
        slot = sb("slot", [P, 2, TILES], U32)
        loaded = [sem(f"loaded{u}") for u in range(2)]
        gathered = [sem(f"gathered{u}", software=True) for u in range(2)]
        stored = [sem(f"stored{u}") for u in range(2)]
        slot_ready = sem("slot_ready")
        summed = sem("summed")
        spared = sem("spared")
        prime(nc, primed)
        block = ctx.enter_context(nc.Block())
        x_t = x_rows.rearrange("(g t p) d -> g p t d", p=P, t=TILES)
        out_t = out.rearrange("g (t p) d -> g p t d", p=P)

        @block.sync
        def _(sp):
            with sp.Fori(0, groups // 2) as i:
                for u in range(2):
                    sp.wait_ge(summed, START + 2 * i)
                    sp.dma_start(x[:, u], x_t[bass.ds(2 * i + u, 1)].rearrange("a p t d -> p (a t) d"))\
                      .then_inc(loaded[u], 16)

        @block.scalar
        def _(act):
            with act.Fori(0, groups // 2) as i:
                for u in range(2):
                    act.wait_ge(summed, START + 2 * i + u + 1)
                    act.dma_start(out_t[bass.ds(2 * i + u, 1)].rearrange("a p t d -> p (a t) d"), s[:, u])\
                       .then_inc(stored[u], 16)
            for u in range(2):
                act.wait_ge(stored[u], START + 16 * (groups // 2))

        @block.gpsimd
        def _(pool):
            with pool.Fori(0, groups // 2) as i:
                for u in range(2):
                    pool.wait_ge(summed, START + 2 * i)
                    pool.wait_ge(slot_ready, START + 2 * i + u + 1)
                    pool.wait_ge(spared, START + 2 * i + u)
                    apart(pool, c).then_inc(spared, 1)
                    for t in range(TILES):
                        pool.indirect_dma_start(y[:, u, t, :], None, y_rows,
                                                bass.IndirectOffsetOnAxis(slot[:, u, t:t + 1], 0),
                                                bounds_check=NTOK - 1, oob_is_err=False).then_inc(gathered[u], 16)

        @block.vector
        def _(dve):
            with dve.Fori(0, groups // 2) as i:
                for u in range(2):
                    dve.tensor_copy(slot[:, u, :], slots[:, bass.ds((2 * i + u) * TILES, TILES)]).then_inc(slot_ready, 1)
                for u in range(2):
                    dve.wait_ge(loaded[u], START + 16 * (i + 1))
                    dve.wait_ge(gathered[u], 16 * TILES * (i + 1))
                    dve.wait_ge(stored[u], START + 16 * i)
                    for t in range(TILES):
                        last = dve.scalar_tensor_tensor(out=s[:, u, t, :], in0=y[:, u, t, :],
                                                        scalar=gates[:, bass.ds((2 * i + u) * TILES + t, 1)],
                                                        in1=x[:, u, t, :], op0=ALU.mult, op1=ALU.add)
                    last.then_inc(summed, 1)


def settle(nc, c, x_rows, y_rows, gates, slots, norm_w, b_out, xr_rows, hT_d):
    ident = c["ident"]
    groups = NTOK // SEQ
    primed = []
    with ExitStack() as ctx:
        def sb(name, shape, dt=F32):
            return ctx.enter_context(nc.sbuf_tensor(f"n_{name}", shape, dt))

        def sem(name, software=False):
            s = ctx.enter_context(nc.semaphore(f"n_{name}"))
            primed.append((s, software))
            return s

        x = sb("x", [P, 2, TILES, D])
        y = sb("y", [P, 2, TILES, D])
        x2 = sb("x2", [P, TILES, D])
        res = sb("res", [P, TILES, D])
        h = sb("h", [P, TILES, D])
        hT = sb("hT", [P, DC, SEQ])
        xr = sb("xr", [P, TILES, D])
        xb = sb("xb", [P, TILES, D])
        nw = sb("nw", [P, DC])
        bo = sb("bo", [P, D])
        slot = sb("slot", [P, 2, TILES], U32)
        stats = sb("stats", [P, 2, TILES, 6])
        mv = sb("mv", [P, 2, TILES, 2])
        veps = sb("veps", [P, 2, TILES])
        square = sb("square", [P, TILES])
        meansq = sb("meansq", [P, TILES])
        rstd = sb("rstd", [P, 2, TILES])
        ps = ctx.enter_context(nc.psum_tensor("n_ps", [P, 2, 512], F32))
        weights_in = sem("weights_in")
        x_loaded = [sem(f"x_loaded{u}") for u in range(2)]
        slot_ready = sem("slot_ready")
        gathered = [sem(f"gathered{u}", software=True) for u in range(2)]
        dve_step = sem("dve_step")
        x2_ready = sem("x2_ready")
        veps_ready = sem("veps_ready")
        rstd_ready = sem("rstd_ready")
        h_ready = sem("h_ready")
        hT_full = sem("hT_full")
        hT_ready = sem("hT_ready")
        xr_ready = sem("xr_ready")
        xb_ready = sem("xb_ready")
        xb_stored = sem("xb_stored")
        hT_stored = sem("hT_stored")
        spared = sem("spared")
        prime(nc, primed)
        block = ctx.enter_context(nc.Block())
        x_t = x_rows.rearrange("(g t p) d -> g p t d", p=P, t=TILES)
        xr_t = xr_rows.rearrange("(g t p) d -> g p t d", p=P, t=TILES)

        @block.sync
        def _(sp):
            sp.dma_start(nw[:, :], norm_w).then_inc(weights_in, 16)
            sp.dma_start(bo[:, :], b_out.rearrange("(a e) -> a e", a=1).broadcast_to([P, D])).then_inc(weights_in, 16)

            def load(g, u):
                sp.dma_start(x[:, u], x_t[bass.ds(g, 1)].rearrange("a p t d -> p (a t) d")).then_inc(x_loaded[u], 16)

            def store(g):
                sp.wait_ge(xb_ready, START + g + 1)
                sp.dma_start(xr_t[bass.ds(g, 1)].rearrange("a p t d -> p (a t) d"), xb[:, :, :]).then_inc(xb_stored, 16)

            load(0, 0)
            load(1, 1)
            with sp.Fori(0, groups // 2 - 1) as i:
                for u in range(2):
                    sp.wait_ge(x2_ready, START + 2 * i + u + 1)
                    load(2 * i + u + 2, u)
                    store(2 * i + u)
            for u in range(2):
                store(groups - 2 + u)
            sp.wait_ge(xb_stored, START + 16 * groups)

        @block.gpsimd
        def _(pool):
            pool.wait_ge(weights_in, START + 32)

            def gather(g, u):
                pool.wait_ge(slot_ready, START + g + 1)
                pool.wait_ge(spared, START + g)
                apart(pool, c).then_inc(spared, 1)
                for t in range(TILES):
                    pool.indirect_dma_start(y[:, u, t, :], None, y_rows,
                                            bass.IndirectOffsetOnAxis(slot[:, u, t:t + 1], 0),
                                            bounds_check=NTOK - 1, oob_is_err=False).then_inc(gathered[u], 16)

            def turn(g, u, last):
                if not last:
                    gather(g + 1, 1 - u)
                for k in range(2):
                    pool.wait_ge(veps_ready, START + 2 * g + k + 1)
                    pool.tensor_tensor(rstd[:, k, :], veps[:, k, :], c["power"][:, :], ALU.pow).then_inc(rstd_ready, 1)
                pool.wait_ge(xr_ready, START + g + 1)
                pool.wait_ge(xb_stored, START + 16 * g)
                pool.tensor_tensor(xb[:, :, :], xr[:, :, :], bo[:, :].unsqueeze(1).broadcast_to([P, TILES, D]),
                                   ALU.add).then_inc(xb_ready, 1)

            gather(0, 0)
            with pool.Fori(0, groups // 2 - 1) as i:
                for u in range(2):
                    turn(2 * i + u, u, False)
            for u in range(2):
                turn(groups - 2 + u, u, u == 1)

        @block.tensor
        def _(pe):
            with pe.Fori(0, groups) as g:
                pe.wait_ge(h_ready, START + g + 1)
                pe.wait_ge(hT_ready, START + 2 * g)
                for k in range(DC):
                    for t in range(TILES):
                        last = pe.transpose(ps[:, k, t * P:(t + 1) * P], h[:, t, k * P:(k + 1) * P], ident[:, :])
                last.then_inc(hT_full, 1)

        @block.scalar
        def _(act):
            act.wait_ge(weights_in, START + 32)
            with act.Fori(0, groups) as g:
                act.wait_ge(hT_full, START + g + 1)
                act.wait_ge(hT_stored, START + 16 * g)
                for k in range(DC):
                    act.activation(hT[:, k, :], ps[:, k, :], ACT.Copy, scale=nw[:, k:k + 1]).then_inc(hT_ready, 1)
                act.wait_ge(hT_ready, START + 2 * g + 2)
                act.dma_start(hT_d[:, :, bass.ds(g * SEQ, SEQ)], hT[:, :, :]).then_inc(hT_stored, 16)
            act.wait_ge(hT_stored, START + 16 * groups)

        @block.vector
        def _(dve):
            steps = 6

            def take_slots(g, u):
                dve.tensor_copy(slot[:, u, :], slots[:, bass.ds(g * TILES, TILES)]).then_inc(slot_ready, 1)

            def turn(g, u, n, last_turn):
                done = [0]

                def link(ins, alone=False):
                    done[0] += 1
                    ins.then_inc(dve_step, 1)
                    dve.wait_ge(dve_step, START + steps * g + done[0])
                    if alone:
                        apart(dve, c)

                if not last_turn:
                    take_slots(g + 1, 1 - u)
                dve.wait_ge(h_ready, START + g)
                dve.wait_ge(x_loaded[u], START + 16 * n)
                dve.wait_ge(gathered[u], 16 * TILES * n)
                for t in range(TILES):
                    last = dve.scalar_tensor_tensor(out=x2[:, t, :], in0=y[:, u, t, :], scalar=gates[:, bass.ds(g * TILES + t, 1)],
                                                    in1=x[:, u, t, :], op0=ALU.mult, op1=ALU.add)
                last.then_inc(x2_ready, 1)
                dve.wait_ge(x2_ready, START + g + 1)
                for t in range(TILES):
                    last = dve.bn_stats(stats[:, 0, t, :], x2[:, t, :])
                link(last, alone=True)
                for t in range(TILES):
                    last = dve.bn_aggr(mv[:, 0, t, :], stats[:, 0, t, :])
                link(last)
                dve.tensor_scalar(veps[:, 0, :], mv[:, 0, :, 1], LN_EPS, None, ALU.add).then_inc(veps_ready, 1)
                dve.wait_ge(rstd_ready, START + 2 * g + 1)
                for t in range(TILES):
                    last = dve.tensor_scalar(res[:, t, :], x2[:, t, :], mv[:, 0, t, 0:1], rstd[:, 0, t:t + 1],
                                             ALU.subtract, ALU.mult)
                link(last)
                for t in range(TILES):
                    last = dve.bn_stats(stats[:, 1, t, :], res[:, t, :])
                link(last, alone=True)
                for t in range(TILES):
                    last = dve.bn_aggr(mv[:, 1, t, :], stats[:, 1, t, :])
                link(last)
                link(dve.tensor_tensor(square[:, :], mv[:, 1, :, 0], mv[:, 1, :, 0], ALU.mult))
                dve.scalar_tensor_tensor(out=veps[:, 1, :], in0=mv[:, 1, :, 1], scalar=EPS, in1=square[:, :],
                                         op0=ALU.add, op1=ALU.add).then_inc(veps_ready, 1)
                dve.wait_ge(xb_ready, START + g)
                dve.tensor_tensor(xr[:, :, :], x2[:, :, :], res[:, :, :], ALU.add).then_inc(xr_ready, 1)
                dve.wait_ge(rstd_ready, START + 2 * g + 2)
                dve.wait_ge(hT_full, START + g)
                for t in range(TILES):
                    last = dve.tensor_scalar(h[:, t, :], res[:, t, :], rstd[:, 1, t:t + 1], None, ALU.mult)
                last.then_inc(h_ready, 1)
                assert done[0] == steps, done

            take_slots(0, 0)
            with dve.Fori(0, groups // 2 - 1) as i:
                for u in range(2):
                    turn(2 * i + u, u, i + 1, False)
            for u in range(2):
                turn(groups - 2 + u, u, groups // 2, u == 1)


def state_space(nc, c, hT_d, win, b_in, conv_w, conv_b, a_bd, at_bd, b_bd, b_col, c_col, yT_d):
    ident, head_of, group_of = c["ident"], c["head_of"], c["group_of"]
    primed = []
    with ExitStack() as ctx:
        def sb(name, shape, dt=F32):
            return ctx.enter_context(nc.sbuf_tensor(f"s_{name}", shape, dt))

        def sem(name, software=False):
            s = ctx.enter_context(nc.semaphore(f"s_{name}"))
            primed.append((s, software))
            return s

        win_sb = sb("win", [P, DC, P])
        bias = sb("bias", [P, 2])
        taps = sb("taps", [P, KW])
        pw = sb("pw", [P, NPAIR, P + CHUNK])
        qv = sb("qv", [P, NPAIR, CHUNK + P])
        cb = sb("cb", [P, 2, NPAIR])
        at = sb("at", [P, NPAIR, P])
        bb = sb("bb", [P, NPAIR, 8])
        wo = sb("wo", [P, NPAIR, CHUNK])
        k_sb = sb("k", [8, NPAIR, CHUNK])
        zero = sb("zero", [P, CHUNK])
        tc_rev = sb("tc_rev", [P, CHUNK, CHUNK])
        tc_sb = sb("tc", [P, CHUNK, CHUNK])
        tbd = sb("tbd", [P, CHUNK, P])
        obd = sb("obd", [P, CHUNK, P])
        rbd = sb("rbd", [P, CHUNK, P])
        hb = sb("hb", [P, 2, DC, SEQ])
        upad = sb("upad", [P, 2, KW - 1 + SEQ])
        acc = sb("acc", [P, SEQ])
        ut = sb("ut", [P, CHUNK, NCH, BATCH])
        xs = sb("xs", [P, NPAIR, NCH, BATCH])
        yts = sb("yts", [P, 2, SEQ])
        ps = ctx.enter_context(nc.psum_tensor("s_ps", [P, 8, 512], F32))
        kpad = nc.dram_tensor("s_kpad", (GRP, NPAIR, 2, 2 * CHUNK), F32, kind="Internal").ap()

        zeroed = sem("zeroed")
        kpad_zero = sem("kpad_zero")
        loaded = sem("loaded")
        hb_loaded = [sem(f"hb_loaded{u}") for u in range(2)]
        first_ready = sem("first_ready")
        proj_full = sem("proj_full")
        u_ready = sem("u_ready")
        conv_step = sem("conv_step")
        ut_ready = sem("ut_ready")
        ring_full = sem("ring_full")
        act_read = sem("act_read")
        dve_read = sem("dve_read")
        k_stored = sem("k_stored")
        tc_loaded = sem("tc_loaded")
        tc_turned = sem("tc_turned")
        v_spread = sem("v_spread")
        o_spread = sem("o_spread")
        t_spread = sem("t_spread")
        yt_ready = sem("yt_ready")
        y_stored = [sem(f"y_stored{u}") for u in range(2)]
        prime(nc, primed)
        block = ctx.enter_context(nc.Block())

        groups = [range(3 * g, min(3 * g + 3, NPAIR)) for g in range((NPAIR + 2) // 3)]
        uses, reader = [], []

        def plan(key, who):
            uses.append(key)
            reader.append(who)

        for level in range(5):
            for g in range(len(groups)):
                plan(("P", level, g), "act")
                plan(("Q", level, g), "act")
        plan(("O",), "act")
        plan(("K",), "act")
        for n in range(8):
            plan(("R", n), "act")
        for n in range(8):
            plan(("S", n), "act")
        for s in range(4):
            for n in range(8):
                plan(("X", s, n), "dve")
            if s < 3:
                for g in range(len(groups)):
                    plan(("P", 5 + s, g), "act")
                    if s < 2:
                        plan(("Q", 5 + s, g), "act")
        for n in range(NPAIR):
            plan(("Y", n), "act" if n % 2 else "dve")
        NU = len(uses)
        number = {key: n for n, key in enumerate(uses)}
        read_by = [reader[:n + 1].count(reader[n]) for n in range(NU)]
        NA, ND = reader.count("act"), reader.count("dve")
        reads = {"act": (act_read, NA), "dve": (dve_read, ND)}

        def bank(key):
            return 2 + number[key] % 6

        def wait_read(eng, q, key):
            n = number[key]
            s, per = reads[reader[n]]
            eng.wait_ge(s, START + per * q + read_by[n])

        @block.sync
        def _(sp):
            sp.wait_ge(zeroed, START + 2)
            rows = kpad.rearrange("g p j n -> (g p j) n")
            sp.dma_start(rows[:, 0:CHUNK], zero[:, :]).then_inc(kpad_zero, 16)
            sp.wait_ge(kpad_zero, START + 16)

            def load(q):
                one = bass.ds(q, 1)
                for dst, src in ((pw[:, :, 0:P], a_bd[one].rearrange("a p i n -> p (a i) n")),
                                 (qv[:, :, CHUNK:], at_bd[one].rearrange("a p i n -> p (a i) n")),
                                 (at[:, :, :], at_bd[one].rearrange("a p i n -> p (a i) n")),
                                 (cb[:, 0, :], c_col[one].rearrange("a p i -> p (a i)")),
                                 (cb[:, 1, :], b_col[one].rearrange("a p i -> p (a i)")),
                                 (bb[:, :, :], b_bd[one].rearrange("a p i n -> p (a i) n")),
                                 (win_sb[:, :, :], win[one].rearrange("a p c n -> p (a c) n")),
                                 (bias[:, 0:1], b_in[one].rearrange("a p n -> p (a n)")),
                                 (bias[:, 1:2], conv_b[one].rearrange("a p n -> p (a n)")),
                                 (taps[:, :], conv_w[one].rearrange("a p n -> p (a n)"))):
                    sp.dma_start(dst, src).then_inc(loaded, 16)

            def rows_of(b):
                sp.dma_start(hb[:, b % 2], hT_d[:, :, b * SEQ:(b + 1) * SEQ]).then_inc(hb_loaded[b % 2], 16)

            def turn(q, last):
                for b in range(2, BATCH):
                    sp.wait_ge(proj_full, START + BATCH * q + b - 1)
                    rows_of(b)
                wait_read(sp, q, ("K",))
                for j in range(2):
                    sp.dma_start(kpad[:, :, j, CHUNK:], k_sb[GRP * j:GRP * (j + 1)]).then_inc(k_stored, 16)
                sp.wait_ge(k_stored, START + 32 * q + 32)
                for g in range(GRP):
                    src = bass.AP(kpad.tensor, g * CHUNK * 2 * CHUNK + 1,
                                  [[1, CHUNK], [2 * CHUNK, CHUNK], [1, CHUNK]])
                    sp.dma_start(tc_rev[CHUNK * g:CHUNK * (g + 1)], src).then_inc(tc_loaded, 16)
                if not last:
                    sp.wait_ge(ring_full, START + NU * q + number[("X", 3, 7)] + 1)
                    for b in range(2):
                        rows_of(b)
                    load(q + 1)
                for b in range(BATCH):
                    sp.wait_ge(yt_ready, START + BATCH * q + b + 1)
                    sp.dma_start(yT_d[bass.ds(q, 1), :, b * SEQ:(b + 1) * SEQ].rearrange("a p n -> p (a n)"),
                                 yts[:, b % 2, :]).then_inc(y_stored[b % 2], 16)

            load(0)
            for b in range(2):
                rows_of(b)
            with sp.Fori(0, QC - 1) as q:
                turn(q, False)
            turn(QC - 1, True)
            for u in range(2):
                sp.wait_ge(y_stored[u], START + 16 * QC * BATCH // 2)

        @block.gpsimd
        def _(pool):
            pool.memset(zero[:, :], 0.0).then_inc(zeroed, 1)
            pool.memset(upad[:, :, 0:KW - 1], 0.0).then_inc(zeroed, 1)

            def spread(out, src, mask):
                return pool.tensor_tensor(out.rearrange("p i (g t) -> p i g t", g=GRP),
                                          src.unsqueeze(2).broadcast_to([P, src.shape[1], GRP, CHUNK]),
                                          mask.unsqueeze(1).unsqueeze(3).broadcast_to([P, src.shape[1], GRP, CHUNK]),
                                          ALU.mult)

            with pool.Fori(0, QC) as q:
                wait_read(pool, q, ("Q", 4, len(groups) - 1))
                for j in range(2):
                    last = spread(tbd[:, j::2, :], qv[:, :, 0:CHUNK], head_of[:, GRP * j:GRP * (j + 1)])
                last.then_inc(v_spread, 1)
                wait_read(pool, q, ("O",))
                for j in range(2):
                    last = spread(obd[:, j::2, :], wo[:, :, :], head_of[:, GRP * j:GRP * (j + 1)])
                last.then_inc(o_spread, 1)
                wait_read(pool, q, ("R", 7))
                pool.wait_ge(tc_turned, START + q + 1)
                spread(tbd[:, :, :], tc_sb[:, :, :], group_of[:, :]).then_inc(t_spread, 1)

        @block.tensor
        def _(pe):
            pe.wait_ge(zeroed, START + 2)
            with pe.Fori(0, QC) as q:
                pe.wait_ge(loaded, START + 160 * q + 160)
                pe.wait_ge(first_ready, START + 2 * q + 2)
                pe.wait_ge(act_read, START + NA * q)
                pe.wait_ge(dve_read, START + ND * q)

                def begin(key):
                    n = number[key]
                    if n >= 6:
                        wait_read(pe, q, uses[n - 6])
                    return bank(key)

                def project(b):
                    pe.wait_ge(hb_loaded[b % 2], START + 16 * (BATCH // 2) * q + 16 * (b // 2 + 1))
                    if b >= 2:
                        pe.wait_ge(u_ready, START + BATCH * q + b - 1)
                    else:
                        pe.wait_ge(u_ready, START + BATCH * q)
                    for k in range(DC):
                        last = pe.matmul(ps[:, b % 2, :], win_sb[:, k, :], hb[:, b % 2, k, :],
                                         start=(k == 0), stop=(k == DC - 1))
                    last.then_inc(proj_full, 1)

                def square(level, g):
                    w = 2 ** level if level < 5 else 0
                    if level:
                        wait_read(pe, q, ("Q", level - 1, g))
                    for side in "PQ":
                        key = (side, level, g)
                        if key not in number:
                            continue
                        bk = begin(key)
                        for n, p in enumerate(groups[g]):
                            if side == "P":
                                stay, move = qv[:, p, CHUNK:], pw[:, p, 0:P + w]
                            else:
                                stay, move = pw[:, p, 0:P], qv[:, p, CHUNK - w:]
                            last = pe.matmul(ps[:, bk, n * (P + w):(n + 1) * (P + w)], stay, move,
                                             start=True, stop=True)
                        last.then_inc(ring_full, 1)

                steps = [(level, g) for level in range(5) for g in range(len(groups))]
                for b in range(BATCH):
                    project(b)
                    for level, g in steps[2 * b:2 * b + 2]:
                        square(level, g)
                wait_read(pe, q, ("Q", 4, len(groups) - 1))
                bk = begin(("O",))
                for p in range(NPAIR):
                    last = pe.matmul(ps[:, bk, p * CHUNK:(p + 1) * CHUNK], at[:, p, :], pw[:, p, P:],
                                     start=True, stop=True)
                last.then_inc(ring_full, 1)
                bk = begin(("K",))
                for p in range(NPAIR):
                    last = pe.matmul(ps[0:8, bk, p * CHUNK:(p + 1) * CHUNK], bb[:, p, :], pw[:, p, P:],
                                     start=True, stop=True)
                last.then_inc(ring_full, 1)
                pe.wait_ge(v_spread, START + q + 1)
                for n in range(8):
                    bk = begin(("R", n))
                    for i in range(4):
                        last = pe.transpose(ps[:, bk, i * P:(i + 1) * P], tbd[:, 4 * n + i, :], ident[:, :])
                    last.then_inc(ring_full, 1)
                pe.wait_ge(ut_ready, START + BATCH * (q + 1))
                per = NCH * BATCH
                for n in range(8):
                    if n == 0:
                        wait_read(pe, q, ("R", 7))
                    bk = begin(("S", n))
                    for m in range(2):
                        for j in range(2):
                            i = 2 * (2 * n + m) + j
                            last = pe.matmul(ps[:, bk, m * per:(m + 1) * per], rbd[:, i, :],
                                             ut[:, i, :, :].rearrange("p c b -> p (c b)"), start=(j == 0), stop=(j == 1))
                    last.then_inc(ring_full, 1)
                for s in range(4):
                    far = 2 ** s
                    for n in range(8):
                        wait_read(pe, q, ("X", s - 1, n) if s else ("S", n))
                        bk = begin(("X", s, n))
                        for m in range(2):
                            last = pe.matmul(ps[:, bk, m * per:m * per + (NCH - far) * BATCH], pw[:, 2 * n + m, 0:P],
                                             xs[:, 2 * n + m, 0:NCH - far, :].rearrange("p c b -> p (c b)"),
                                             start=True, stop=True)
                        last.then_inc(ring_full, 1)
                    if s < 3:
                        for g in range(len(groups)):
                            square(5 + s, g)
                        wait_read(pe, q, ("P", 5 + s, len(groups) - 1))
                pe.wait_ge(t_spread, START + q + 1)
                pe.wait_ge(o_spread, START + q + 1)
                wait_read(pe, q, ("X", 3, 7))
                for n in range(NPAIR):
                    bk = begin(("Y", n))
                    for j in range(2):
                        i = 2 * n + j
                        pe.matmul(ps[:, bk, j * per:(j + 1) * per], tbd[:, i, :],
                                  ut[:, i, :, :].rearrange("p c b -> p (c b)"), start=True, stop=False)
                        last = pe.matmul(ps[:, bk, j * per + BATCH:(j + 1) * per], obd[:, i, :],
                                         xs[:, n, 0:NCH - 1, :].rearrange("p c b -> p (c b)"), start=False, stop=True)
                    last.then_inc(ring_full, 1)

        def full(eng, q, key):
            eng.wait_ge(ring_full, START + NU * q + number[key] + 1)

        @block.scalar
        def _(act):
            with act.Fori(0, QC) as q:
                act.wait_ge(loaded, START + 160 * q + 160)
                act.wait_ge(o_spread, START + q)
                act.activation(pw[:, :, P], cb[:, 0, :], ACT.Copy).then_inc(first_ready, 1)
                act.activation(qv[:, :, CHUNK - 1], cb[:, 1, :], ACT.Copy).then_inc(first_ready, 1)
                act.wait_ge(k_stored, START + 32 * q)

                def take(b):
                    act.wait_ge(proj_full, START + BATCH * q + b + 1)
                    if b >= 2:
                        act.wait_ge(ut_ready, START + BATCH * q + b - 1)
                    act.activation(upad[:, b % 2, KW - 1:], ps[:, b % 2, :], ACT.Identity, bias=bias[:, 0:1])\
                       .then_inc(u_ready, 1)

                def squared(level, g):
                    w = 2 ** level if level < 5 else 0
                    a, z = groups[g][0], groups[g][-1] + 1
                    full(act, q, ("Q", level, g) if ("Q", level, g) in number else ("P", level, g))
                    for side in "PQ":
                        key = (side, level, g)
                        if key not in number:
                            continue
                        src = ps[:, bank(key), 0:(z - a) * (P + w)].rearrange("p (i n) -> p i n", n=P + w)
                        if side == "P":
                            if w:
                                act.activation(pw[:, a:z, P + w:P + 2 * w], src[:, :, P:], ACT.Copy)
                            last = act.activation(pw[:, a:z, 0:P], src[:, :, 0:P], ACT.Copy)
                        else:
                            if w:
                                act.activation(qv[:, a:z, CHUNK - 2 * w:CHUNK - w], src[:, :, 0:w], ACT.Copy)
                            last = act.activation(qv[:, a:z, CHUNK:], src[:, :, w:], ACT.Copy)
                        last.then_inc(act_read, 1)

                steps = [(level, g) for level in range(5) for g in range(len(groups))]
                for b in range(BATCH):
                    take(b)
                    for level, g in steps[2 * b:2 * b + 2]:
                        squared(level, g)
                full(act, q, ("O",))
                act.activation(wo[:, :, :].rearrange("p i n -> p (i n)"), ps[:, bank(("O",)), :], ACT.Copy)\
                   .then_inc(act_read, 1)
                full(act, q, ("K",))
                act.activation(k_sb[:, :, :].rearrange("p i n -> p (i n)"), ps[0:8, bank(("K",)), :], ACT.Copy)\
                   .then_inc(act_read, 1)
                for n in range(8):
                    full(act, q, ("R", n))
                    act.activation(rbd[:, 4 * n:4 * n + 4, :].rearrange("p i n -> p (i n)"), ps[:, bank(("R", n)), :],
                                   ACT.Copy).then_inc(act_read, 1)
                for n in range(8):
                    full(act, q, ("S", n))
                    act.activation(xs[:, 2 * n:2 * n + 2, :, :].rearrange("p i c b -> p (i c b)"),
                                   ps[:, bank(("S", n)), :], ACT.Copy).then_inc(act_read, 1)
                for s in range(3):
                    for g in range(len(groups)):
                        squared(5 + s, g)
                for n in range(1, NPAIR, 2):
                    full(act, q, ("Y", n))
                    act.activation(ut[:, 2 * n:2 * n + 2, :, :].rearrange("p i c b -> p (i c b)"),
                                   ps[:, bank(("Y", n)), :], ACT.Copy).then_inc(act_read, 1)

        @block.vector
        def _(dve):
            dve.wait_ge(zeroed, START + 2)
            with dve.Fori(0, QC) as q:
                dve.wait_ge(loaded, START + 160 * q + 160)
                for b in range(BATCH):
                    dve.wait_ge(u_ready, START + BATCH * q + b + 1)
                    dve.wait_ge(ut_ready, START + BATCH * q + b)
                    u = upad[:, b % 2, :]
                    dve.tensor_scalar(acc[:, :], u[:, KW - 1:], taps[:, KW - 1:KW], bias[:, 1:2], ALU.mult, ALU.add)\
                       .then_inc(conv_step, 1)
                    for k in range(1, KW):
                        dve.wait_ge(conv_step, START + KW * (BATCH * q + b) + k)
                        dve.scalar_tensor_tensor(out=acc[:, :], in0=u[:, KW - 1 - k:KW - 1 - k + SEQ],
                                                 scalar=taps[:, KW - 1 - k:KW - k], in1=acc[:, :],
                                                 op0=ALU.mult, op1=ALU.add).then_inc(conv_step, 1)
                    dve.wait_ge(conv_step, START + KW * (BATCH * q + b) + KW)
                    dve.transpose(ut[:, :, :, b].rearrange("p i c -> p c i"),
                                  acc[:, :].rearrange("p (c t) -> p c t", t=CHUNK)).then_inc(ut_ready, 1)
                dve.wait_ge(tc_loaded, START + 16 * GRP * (q + 1))
                dve.wait_ge(t_spread, START + q)
                apart(dve, c)
                dve.stream_shuffle(tc_sb[:, :, :].rearrange("p i t -> p (i t)"),
                                   tc_rev[:, :, :].rearrange("p i t -> p (i t)"),
                                   mask=[CHUNK - 1 - k for k in range(CHUNK)]).then_inc(tc_turned, 1)
                for s in range(4):
                    far = 2 ** s
                    n_cols = (NCH - far) * BATCH
                    for n in range(8):
                        full(dve, q, ("X", s, n))
                        src = ps[:, bank(("X", s, n)), :].rearrange("p (i n) -> p i n", i=2)[:, :, 0:n_cols]
                        dst = xs[:, 2 * n:2 * n + 2, far:, :].rearrange("p i c b -> p i (c b)")
                        dve.tensor_tensor(dst, src, dst, ALU.add).then_inc(dve_read, 1)
                for n in range(0, NPAIR, 2):
                    full(dve, q, ("Y", n))
                    dve.tensor_copy(ut[:, 2 * n:2 * n + 2, :, :].rearrange("p i c b -> p (i c b)"),
                                    ps[:, bank(("Y", n)), :]).then_inc(dve_read, 1)
                wait_read(dve, q, ("Y", NPAIR - 1))
                wait_read(dve, q, ("Y", NPAIR - 2))
                for b in range(BATCH):
                    if b >= 2:
                        dve.wait_ge(y_stored[b % 2], START + 16 * (BATCH // 2) * q + 16 * (b // 2))
                    else:
                        dve.wait_ge(y_stored[b % 2], START + 16 * (BATCH // 2) * q)
                    dve.transpose(yts[:, b % 2, :].rearrange("p (c t) -> p c t", t=CHUNK),
                                  ut[:, :, :, b].rearrange("p i c -> p c i")).then_inc(yt_ready, 1)
                dve.wait_ge(yt_ready, START + BATCH * (q + 1))


def project_out(nc, yT_d, wout, xr_rows, x3_rows):
    primed = []
    with ExitStack() as ctx:
        def sb(name, shape, dt=F32):
            return ctx.enter_context(nc.sbuf_tensor(f"o_{name}", shape, dt))

        def sem(name, software=False):
            s = ctx.enter_context(nc.semaphore(f"o_{name}"))
            primed.append((s, software))
            return s

        w = sb("w", [P, QC, D])
        yT = sb("yT", [P, 2, QC, SEQ])
        xr = sb("xr", [P, 2, TILES, D])
        x3 = sb("x3", [P, 2, TILES, D])
        ps = ctx.enter_context(nc.psum_tensor("o_ps", [P, 8, 512], F32))
        weights_in = sem("weights_in")
        loaded = [sem(f"loaded{u}") for u in range(2)]
        stored = [sem(f"stored{u}") for u in range(2)]
        full = sem("full")
        summed = sem("summed")
        prime(nc, primed)
        block = ctx.enter_context(nc.Block())
        xr_t = xr_rows.rearrange("(g t p) d -> g p t d", p=P, t=TILES)
        x3_t = x3_rows.rearrange("(g t p) d -> g p t d", p=P, t=TILES)
        y_t = yT_d.rearrange("q p (g n) -> g p q n", n=SEQ)

        @block.sync
        def _(sp):
            sp.dma_start(w[:, :, :], wout.rearrange("(q p) d -> p q d", p=P)).then_inc(weights_in, 16)

            def load(g, u):
                one = bass.ds(g, 1)
                sp.dma_start(yT[:, u], y_t[one].rearrange("a p q n -> p (a q) n")).then_inc(loaded[u], 16)
                sp.dma_start(xr[:, u], xr_t[one].rearrange("a p t d -> p (a t) d")).then_inc(loaded[u], 16)

            def store(g, u):
                sp.wait_ge(summed, START + TILES * (g + 1))
                sp.dma_start(x3_t[bass.ds(g, 1)].rearrange("a p t d -> p (a t) d"), x3[:, u]).then_inc(stored[u], 16)

            for u in range(2):
                load(u, u)
            with sp.Fori(0, BATCH // 2 - 1) as i:
                for u in range(2):
                    store(2 * i + u, u)
                    load(2 * i + u + 2, u)
            for u in range(2):
                store(BATCH - 2 + u, u)
            for u in range(2):
                sp.wait_ge(stored[u], START + 16 * BATCH // 2)

        @block.tensor
        def _(pe):
            pe.wait_ge(weights_in, START + 16)
            with pe.Fori(0, BATCH // 2) as i:
                for u in range(2):
                    pe.wait_ge(loaded[u], START + 32 * (i + 1))
                    pe.wait_ge(summed, START + TILES * 2 * i)
                    for t in range(TILES):
                        for k in range(QC):
                            last = pe.matmul(ps[:, TILES * u + t, 0:D], yT[:, u, k, t * P:(t + 1) * P], w[:, k, :],
                                             start=(k == 0), stop=(k == QC - 1))
                        last.then_inc(full, 1)

        @block.vector
        def _(dve):
            with dve.Fori(0, BATCH // 2) as i:
                for u in range(2):
                    dve.wait_ge(loaded[u], START + 32 * (i + 1))
                    dve.wait_ge(stored[u], START + 16 * i)
                    for t in range(TILES):
                        dve.wait_ge(full, START + TILES * (2 * i + u) + t + 1)
                        dve.tensor_tensor(x3[:, u, t, :], ps[:, TILES * u + t, 0:D], xr[:, u, t, :], ALU.add)\
                           .then_inc(summed, 1)


def copy_rows(nc, src, dst):
    with nc.semaphore("filled") as filled, nc.Block() as block:
        @block.sync
        def _(sp):
            sp.dma_start(dst, src).then_inc(filled, 16)
            sp.wait_ge(filled, 16)


def hybrid_block(nc, x, w_qkv, w_ky, w_proj, norm_w, win, b_in, conv_w, conv_b, a_bd, at_bd, b_bd, b_col, c_col,
                 wout, b_out, wg, bg, w1, b1, w2, b2, out):
    def dram(name, shape):
        return nc.dram_tensor(name, shape, F32, kind="Internal").ap()

    x1 = dram("x1", (NTOK, D))
    xr = dram("xr", (NTOK, D))
    x3 = dram("x3", (NTOK, D))
    rows = dram("rows", (NTOK, D))
    y = dram("y", (NTOK, D))
    hT = dram("hT", (P, DC, NTOK))
    yT = dram("yT", (QC, P, NTOK))
    with ExitStack() as ctx:
        def sb(name, shape, dt):
            return ctx.enter_context(nc.sbuf_tensor(name, shape, dt))

        c = constants(nc, sb)
        gates = sb("gates", [P, NTOK // P], F32)
        slots = sb("slots", [P, NTOK // P], U32)
        copy_rows(nc, x.rearrange("b s d -> (b s) d"), rows)
        attention(nc, c, x, w_qkv, w_ky, w_proj, x1)
        route(nc, c, "r1", x1, wg, bg, rows, gates, slots)
        experts(nc, c, "e1", rows, w1, b1, w2, b2, y)
        settle(nc, c, x1, y, gates, slots, norm_w, b_out, xr, hT)
        state_space(nc, c, hT, win, b_in, conv_w, conv_b, a_bd, at_bd, b_bd, b_col, c_col, yT)
        project_out(nc, yT, wout, xr, x3)
        route(nc, c, "r2", x3, wg, bg, rows, gates, slots)
        experts(nc, c, "e2", rows, w1, b1, w2, b2, y)
        combine_out(nc, c, x3, y, gates, slots, out)


def layouts(i):
    import numpy as np

    def groups(a):
        a = a.reshape(QC, GRP, NPAIR, 2, *a.shape[1:])
        return a.transpose(0, 2, 3, 1, *range(4, a.ndim)).reshape(QC, NPAIR, 8, *a.shape[4:])

    def diagonal(a):
        q, p, e, n, m = a.shape
        out = np.zeros((q, e, n, p, e, m), a.dtype)
        for k in range(e):
            out[:, k, :, :, k, :] = a[:, :, k].transpose(0, 2, 1, 3)
        return out.reshape(q, e * n, p, e * m)

    A = groups(i["L0_attn_b_A"])
    B = groups(i["L0_attn_b_Bm"])
    C = groups(i["L0_attn_b_Cm"].transpose(0, 2, 1))

    def column(a):
        return a.reshape(QC, NPAIR, P).transpose(0, 2, 1)

    return {
        "x": i["L0_attn_a_x"],
        "w_qkv": i["L0_attn_a_w_qkv"].T,
        "w_ky": i["L0_attn_a_w_ky"].T,
        "w_proj": i["L0_attn_a_w_proj"].T,
        "norm_w": i["L0_attn_b_norm_w"].reshape(DC, P).T,
        "win": i["L0_attn_b_Win"].reshape(DC, P, QC, P).transpose(2, 1, 0, 3),
        "b_in": i["L0_attn_b_b_in"].reshape(QC, P, 1),
        "conv_w": i["L0_attn_b_conv_w"].reshape(QC, P, KW),
        "conv_b": i["L0_attn_b_conv_b"].reshape(QC, P, 1),
        "a_bd": diagonal(A),
        "at_bd": diagonal(A.transpose(0, 1, 2, 4, 3)),
        "b_bd": diagonal(B),
        "b_col": column(B),
        "c_col": column(C),
        "wout": i["L0_attn_b_Wout"],
        "b_out": i["L0_attn_b_b_out"],
        "wg": i["L0_ffn_Wg"],
        "bg": i["L0_ffn_bg"],
        "w1": i["L0_ffn_W1"],
        "b1": i["L0_ffn_b1"].reshape(EXPERTS, HC, P).transpose(0, 2, 1),
        "w2": i["L0_ffn_W2"],
        "b2": i["L0_ffn_b2"],
    }


def kernel(**inputs):
    import numpy as np
    import concourse.bacc as bacc
    from concourse.bass_utils import run_bass_kernel_spmd

    nc = bacc.Bacc("TRN2", target_bir_lowering=False, num_devices=1)
    arrays, args = {}, {}
    for name, a in layouts({k: np.asarray(v) for k, v in inputs.items()}).items():
        a = np.ascontiguousarray(a)
        arrays[f"in_{name}"] = a
        args[name] = nc.dram_tensor(f"in_{name}", a.shape, mybir.dt.from_np(a.dtype), kind="ExternalInput").ap()
    out = nc.dram_tensor("out", (BATCH, SEQ, D), F32, kind="ExternalOutput").ap()
    hybrid_block(nc, out=out, **args)
    r = run_bass_kernel_spmd(nc, [arrays], core_ids=[0])
    return r.results[0]["out"]
```

```python
import concourse.bass as bass
from concourse import mybir
from contextlib import ExitStack

P = 128
F32 = mybir.dt.float32
F32R = mybir.dt.float32r
U32 = mybir.dt.uint32
I32 = mybir.dt.int32
ALU = mybir.AluOpType
ACT = mybir.ActivationFunctionType
AX = mybir.AxisListType

BATCH, SEQ, D = 16, 512, 256
NTOK = BATCH * SEQ
TILES = SEQ // P
DC = D // P
HEADS, HD = 16, 16
HPC = P // HD
VW = 32
EXPERTS, HID = 16, 1024
CAP = NTOK // EXPERTS
HC = HID // P
DIN = 512
NST = 16
CHUNK = 32
NCH = SEQ // CHUNK
QC = DIN // P
GRP = P // CHUNK
NPAIR = CHUNK // 2
KW = 4
COLS = TILES * (TILES + 1) // 2 * P
PLACE = {512: 0, 384: 512, 128: 896, 256: 1024}
START = 1
LN_EPS = 1e-5
EPS = 1e-6
LIMIT = 60.0


def constants(nc, sb):
    c = {
        "ident": sb("ident", [P, P], F32),
        "cap": sb("cap", [P, COLS], F32),
        "causal": sb("causal", [P, COLS], F32),
        "magnitude": sb("magnitude", [P, COLS], I32),
        "head_of": sb("head_of", [P, HPC], F32),
        "group_of": sb("group_of", [P, GRP], F32),
        "experts": sb("experts", [P, EXPERTS], F32),
        "experts_i": sb("experts_i", [P, EXPERTS], I32),
        "spare": sb("spare", [P, 2], F32),
        "power": sb("power", [P, TILES], F32),
    }
    with nc.semaphore("made") as made, nc.semaphore("bits") as bits, nc.Block() as block:
        @block.gpsimd
        def _(pool):
            pool.memset(c["ident"][:, :], 0.0)
            pool.memset(c["cap"][:, :], LIMIT)
            pool.memset(c["causal"][:, :], 1.0)
            pool.memset(c["head_of"][:, :], 1.0)
            pool.memset(c["group_of"][:, :], 1.0)
            pool.memset(c["power"][:, :], -0.5)
            pool.iota(c["experts_i"][:, :], [[1, EXPERTS]], base=0, channel_multiplier=0).then_inc(made, 1)
            pool.wait_ge(made, 1)
            pool.tensor_copy(c["experts"][:, :], c["experts_i"][:, :])
            pool.affine_select(out=c["ident"][:, :], in_=c["ident"][:, :], compare_op=ALU.not_equal, fill=1.0,
                               base=0, pattern=[[-1, P]], channel_multiplier=1)
            for t in range(TILES):
                n = (t + 1) * P
                v = c["cap"][:, PLACE[n]:PLACE[n] + n]
                pool.affine_select(out=v, in_=v, compare_op=ALU.is_ge, fill=-4e4, base=t * P,
                                   pattern=[[-1, n]], channel_multiplier=1)
                v = c["causal"][:, PLACE[n]:PLACE[n] + n]
                pool.affine_select(out=v, in_=v, compare_op=ALU.is_ge, fill=0.0, base=0,
                                   pattern=[[1, n]], channel_multiplier=-1)
            for name, width, n in (("head_of", HD, HPC), ("group_of", CHUNK, GRP)):
                m = c[name][:, :]
                pool.affine_select(out=m, in_=m, compare_op=ALU.is_ge, fill=0.0, base=0,
                                   pattern=[[-width, n]], channel_multiplier=1).then_inc(made, 1)
            pool.wait_ge(made, 3)
            for name, width, n in (("head_of", HD, HPC), ("group_of", CHUNK, GRP)):
                m = c[name][:, :]
                last = pool.affine_select(out=m, in_=m, compare_op=ALU.is_ge, fill=0.0, base=width - 1,
                                          pattern=[[width, n]], channel_multiplier=-1)
            last.then_inc(made, 1)
            pool.wait_ge(made, 4)

        @block.vector
        def _(dve):
            m = c["magnitude"][:, :]
            dve.wait_ge(made, 4)
            dve.tensor_copy(m, c["causal"][:, :]).then_inc(bits, 1)
            dve.wait_ge(bits, 1)
            dve.tensor_scalar(m, m, 31, 31, ALU.logical_shift_left, ALU.arith_shift_right).then_inc(bits, 1)
            dve.wait_ge(bits, 2)
            dve.tensor_scalar(m, m, 0x7FFFFFFF, None, ALU.bitwise_and).then_inc(bits, 1)
            dve.wait_ge(bits, 3)
    return c


def apart(eng, c):
    if eng.engine == mybir.EngineType.DVE:
        return eng.memset(c["spare"][:, 0:1], 0.0)
    return eng.tensor_tensor(c["spare"][:, 1:2], c["power"][:, 0:1], c["power"][:, 0:1], ALU.mult)


def prime(nc, semaphores):
    with nc.Block() as block:
        @block.sync
        def _(sp):
            for s, software in semaphores:
                sp.sem_clear(s)
                if not software:
                    sp.sem_inc(s, START)


def attention(nc, c, x, wqkv, wky, wproj, x1):
    ident, cap, causal, head_of = c["ident"], c["cap"], c["causal"], c["head_of"]
    ones = causal[:, P:2 * P]
    upper = causal[:, 0:P]
    primed = []
    STATS_AT, NORM_AT = 5, 9
    FACTORS_AT = 11
    XT, QK, V = (0, 1), (2, 3, 4, 5, 6, 7), (8, 9)
    RING = 8
    with ExitStack() as ctx:
        def sb(name, shape, dt=F32):
            return ctx.enter_context(nc.sbuf_tensor(name, shape, dt))

        def sem(name, software=False):
            s = ctx.enter_context(nc.semaphore(name))
            primed.append((s, software))
            return s

        w_sb = sb("a_w", [P, DC, 3 * D])
        wky_sb = sb("a_wky", [P, DC, D])
        wp_sb = sb("a_wp", [P, DC, D])
        x_in = sb("a_x", [P, TILES, D])
        x_res = sb("a_xres", [P, TILES, D])
        stats = sb("a_stats", [P, TILES, 6])
        mv = sb("a_mv", [P, TILES, 2])
        veps = sb("a_veps", [P, TILES])
        rstd = sb("a_rstd", [P, TILES])
        xn = sb("a_xn", [P, TILES, D])
        xnT = sb("a_xnT", [P, DC, SEQ])
        qT = sb("a_qT", [P, DC, SEQ])
        kT = sb("a_kT", [P, DC, SEQ])
        kyT = sb("a_kyT", [P, DC, SEQ])
        q2T = sb("a_q2T", [P, DC, SEQ])
        v = sb("a_v", [P, TILES, HEADS, VW])
        qm = sb("a_qm", [P, 4, SEQ])
        q2m = sb("a_q2m", [P, 4, SEQ])
        scored = sb("a_scored", [P, 2, COLS])
        agg = sb("a_agg", [P, TILES, HEADS])
        agg1 = sb("a_agg1", [P, TILES, HEADS])
        agg2 = sb("a_agg2", [P, TILES, HEADS])
        inv1 = sb("a_inv1", [P, TILES, HEADS])
        inv2 = sb("a_inv2", [P, TILES, HEADS])
        rx = sb("a_rx", [P, TILES, HEADS, HD])
        shift = sb("a_shift", [P, TILES, HEADS])
        weight = sb("a_weight", [P, RING, COLS])
        headT = sb("a_headT", [P, SEQ])
        av = sb("a_av", [P, TILES, HEADS, VW])
        t1 = sb("a_t1", [P, HEADS, HD + 1])
        t2 = sb("a_t2", [P, HEADS, HD + 1])
        den = sb("a_den", [P, HEADS])
        rden = sb("a_rden", [P, HEADS])
        o = sb("a_o", [P, TILES, D])
        oT = sb("a_oT", [P, DC, SEQ])
        ps = ctx.enter_context(nc.psum_tensor("a_ps", [P, 8, 512], F32))
        flat = ps[:, :, :].rearrange("p b n -> p (b n)")

        weights_in = sem("weights_in")
        x_loaded = sem("x_loaded")
        xres_loaded = sem("xres_loaded")
        x1_stored = sem("x1_stored")
        v_ones = sem("v_ones")
        ln_step = sem("ln_step")
        veps_ready = sem("veps_ready")
        rstd_ready = sem("rstd_ready")
        xn_ready = sem("xn_ready")
        misc_full = sem("misc_full")
        misc_read = sem("misc_read")
        qm_ready = sem("qm_ready")
        e_scores = sem("e_scores")
        clip_done = sem("clip_done")
        exp_done = sem("exp_done")
        agg_step = sem("agg_step")
        rx_ready = sem("rx_ready")
        shift_ready = sem("shift_ready")
        rT_full = sem("rT_full")
        q2_done = sem("q2_done")
        q2m_ready = sem("q2m_ready")
        w_scores = sem("w_scores")
        abs_done = sem("abs_done")
        ln_done = sem("ln_done")
        av_done = sem("av_done")
        headT_ready = sem("headT_ready")
        ot_full = sem("ot_full")
        av_read = sem("av_read")
        cv_full = sem("cv_full")
        norm_step = sem("norm_step")
        o_ready = sem("o_ready")
        oT_full = sem("oT_full")
        oT_ready = sem("oT_ready")
        proj_full = sem("proj_full")
        x1_ready = sem("x1_ready")
        prime(nc, primed)
        block = ctx.enter_context(nc.Block())

        x_t = x.rearrange("b (t p) d -> b p t d", p=P)
        x1_t = x1.rearrange("(b t p) d -> b p t d", p=P, t=TILES)

        def score_place(n):
            return slice(PLACE[n], PLACE[n] + n)

        @block.sync
        def _(sp):
            sp.dma_start(x_in[:, :, :], x_t[0]).then_inc(x_loaded, 16)
            sp.dma_start(w_sb[:, :, :], wqkv.rearrange("(c p) n -> p c n", p=P)).then_inc(weights_in, 16)
            sp.dma_start(wky_sb[:, :, :], wky.rearrange("(c p) n -> p c n", p=P)).then_inc(weights_in, 16)
            sp.dma_start(wp_sb[:, :, :], wproj.rearrange("(c p) n -> p c n", p=P)).then_inc(weights_in, 16)

            def turn(b, last):
                sp.wait_ge(x1_stored, START + 16 * b)
                sp.dma_start(x_res[:, :, :], x_t[bass.ds(b, 1)].rearrange("a p t d -> p (a t) d")
                             if not last else x_t[BATCH - 1]).then_inc(xres_loaded, 16)
                if not last:
                    sp.wait_ge(xn_ready, START + b + 1)
                    sp.dma_start(x_in[:, :, :], x_t[bass.ds(b + 1, 1)].rearrange("a p t d -> p (a t) d"))\
                      .then_inc(x_loaded, 16)
                sp.wait_ge(x1_ready, START + 2 * b + 2)
                sp.dma_start(x1_t[bass.ds(b, 1)].rearrange("a p t d -> p (a t) d") if not last
                             else x1_t[BATCH - 1], x_res[:, :, :]).then_inc(x1_stored, 16)

            with sp.Fori(0, BATCH - 1) as b:
                turn(b, False)
            turn(BATCH - 1, True)
            sp.wait_ge(x1_stored, START + 16 * BATCH)

        @block.gpsimd
        def _(pool):
            pool.memset(v[:, :, :, HD:VW], 0.0).then_inc(v_ones, 1)
            pool.wait_ge(v_ones, START + 1)
            pool.memset(v[:, :, :, HD:HD + 1], 1.0).then_inc(v_ones, 1)

            def rms(b):
                pool.wait_ge(veps_ready, START + b + 1)
                pool.tensor_tensor(rstd[:, :], veps[:, :], c["power"][:, :], ALU.pow).then_inc(rstd_ready, 1)

            def turn(b, last):
                pool.wait_ge(misc_read, START + 10 * b + 4)
                for h in range(HEADS):
                    if h >= 4:
                        pool.wait_ge(e_scores, START + HEADS * b + h - 3)
                    pool.tensor_tensor(qm[:, h % 4, :], qT[:, h // HPC, :],
                                       head_of[:, h % HPC:h % HPC + 1].broadcast_to([P, SEQ]), ALU.mult).then_inc(qm_ready, 1)
                for h in range(HEADS):
                    if h % HPC == 0:
                        pool.wait_ge(q2_done, START + 2 * b + 1 + h // HPC)
                    if h >= 4:
                        pool.wait_ge(w_scores, START + HEADS * b + h - 3)
                    pool.tensor_tensor(q2m[:, h % 4, :], q2T[:, h // HPC, :],
                                       head_of[:, h % HPC:h % HPC + 1].broadcast_to([P, SEQ]), ALU.mult).then_inc(q2m_ready, 1)
                    if h == NORM_AT and not last:
                        rms(b + 1)

            rms(0)
            with pool.Fori(0, BATCH - 1) as b:
                turn(b, False)
            turn(BATCH - 1, True)

        @block.tensor
        def _(pe):
            pe.wait_ge(weights_in, START + 48)
            pe.wait_ge(v_ones, START + 2)
            def turn_rows(b):
                pe.wait_ge(xn_ready, START + b + 1)
                pe.wait_ge(abs_done, START + HEADS * b)
                for k in range(DC):
                    for t in range(TILES):
                        last = pe.transpose(ps[:, 4 + k, t * P:(t + 1) * P], xn[:, t, k * P:(k + 1) * P], ident[:, :])
                    last.then_inc(misc_full, 1)

            def project(b, first, part):
                for m in part:
                    pe.wait_ge(misc_read, START + 10 * b + (2 if m == 2 else m - 1))
                    if m < 4 and not first:
                        if m == 2:
                            pe.wait_ge(headT_ready, START + 4 * b)
                        else:
                            pe.wait_ge(av_read, START + 4 * b)
                    bank = 6 + m % 2
                    if m < 8:
                        which, half = (m - 2) // 2, m % 2
                        w = wky_sb if which == 2 else w_sb
                        col = (D if which == 1 else 0) + half * P
                        for k in range(DC):
                            last = pe.matmul(ps[:, bank, :], w[:, k, col:col + P], xnT[:, k, :],
                                             start=(k == 0), stop=(k == DC - 1))
                    else:
                        for i in range(2):
                            t = 2 * (m - 8) + i
                            for k in range(DC):
                                last = pe.matmul(ps[:, bank, i * D:(i + 1) * D], xnT[:, k, t * P:(t + 1) * P],
                                                 w_sb[:, k, 2 * D:3 * D], start=(k == 0), stop=(k == DC - 1))
                    last.then_inc(misc_full, 1)

            def turn(b, last_turn):
                def turn_factors(k):
                    pe.wait_ge(rx_ready, START + 2 * b + k + 1)
                    pe.wait_ge(misc_read, START + 10 * b + 10)
                    for t in range(TILES):
                        last = pe.transpose(ps[:, 6 + k, t * P:(t + 1) * P],
                                            rx[:, t, k * HPC:(k + 1) * HPC, :].rearrange("p h d -> p (h d)"),
                                            ident[:, :])
                    last.then_inc(rT_full, 1)

                pe.wait_ge(misc_read, START + 10 * b + 8)
                for h in range(HEADS):
                    pe.wait_ge(qm_ready, START + HEADS * b + h + 1)
                    if h == 1:
                        pe.wait_ge(x1_ready, START + 2 * b)
                    if h >= 2:
                        pe.wait_ge(clip_done, START + HEADS * b + h - 1)
                    base = 3 * 512 * (h % 2)
                    for t in range(TILES):
                        n = (t + 1) * P
                        last = pe.matmul(flat[:, base + PLACE[n]:base + PLACE[n] + n],
                                         qm[:, h % 4, t * P:(t + 1) * P], kyT[:, h // HPC, 0:n],
                                         start=True, stop=True)
                    last.then_inc(e_scores, 1)
                    if h == FACTORS_AT + 1:
                        turn_factors(0)
                def scores(h):
                    if h < 2:
                        pe.wait_ge(clip_done, START + HEADS * b + HEADS - 1 + h)
                    else:
                        pe.wait_ge(abs_done, START + HEADS * b + h - 1)
                    pe.wait_ge(q2m_ready, START + HEADS * b + h + 1)
                    base = 3 * 512 * (h % 2)
                    for t in range(TILES):
                        n = SEQ - t * P
                        last = pe.matmul(flat[:, base + PLACE[n]:base + PLACE[n] + n],
                                         kT[:, h // HPC, t * P:(t + 1) * P], q2m[:, h % 4, t * P:SEQ],
                                         start=True, stop=True)
                    last.then_inc(w_scores, 1)

                def values(g):
                    pe.wait_ge(ln_done, START + HEADS * b + 4 * g + 4)
                    if g:
                        pe.wait_ge(headT_ready, START + 4 * b + g)
                    else:
                        pe.wait_ge(q2_done, START + 2 * b + 2)
                    for t in range(TILES):
                        for h in range(4 * g, 4 * g + 4):
                            r = VW * (h % 4)
                            last = pe.matmul(ps[r:r + VW, 6, t * P:SEQ], v[:, t, h, :],
                                             weight[:, h % RING, score_place(SEQ - t * P)],
                                             start=(t == 0), stop=(t == TILES - 1))
                    last.then_inc(av_done, 1)

                def turn_back(g):
                    pe.wait_ge(headT_ready, START + 4 * b + g + 1)
                    if g:
                        pe.wait_ge(av_read, START + 4 * b + g)
                    else:
                        pe.wait_ge(q2_done, START + 2 * b + 2)
                    for t in range(TILES):
                        last = pe.transpose(ps[:, 7, t * P:(t + 1) * P], headT[:, t * P:(t + 1) * P], ident[:, :])
                    last.then_inc(ot_full, 1)

                for h in range(HEADS + 2):
                    if h < HEADS:
                        scores(h)
                    if h == 2:
                        turn_factors(1)
                    if h >= 5 and h % 4 == 1:
                        values((h - 5) // 4)
                    if h >= 7 and h % 4 == 3:
                        turn_back((h - 7) // 4)
                if not last_turn:
                    turn_rows(b + 1)
                pe.wait_ge(abs_done, START + HEADS * b + HEADS)
                for t in range(TILES):
                    for s in range(t + 1):
                        last = pe.matmul(ps[:, t, 0:HEADS * (HD + 1)], upper if s == t else ones,
                                         v[:, s, :, 0:HD + 1], start=(s == 0), stop=(s == t))
                    last.then_inc(cv_full, 1)
                turn_back(3)
                if not last_turn:
                    project(b + 1, False, QK)
                for t in range(TILES):
                    pe.wait_ge(o_ready, START + TILES * b + t + 1)
                    for k in range(DC):
                        last = pe.transpose(ps[:, 4 + k, t * P:(t + 1) * P], o[:, t, k * P:(k + 1) * P],
                                            ident[:, :])
                last.then_inc(oT_full, 1)
                if not last_turn:
                    project(b + 1, False, V)
                pe.wait_ge(oT_ready, START + 2 * b + 2)
                for t in range(TILES):
                    for k in range(DC):
                        last = pe.matmul(ps[:, 4 + t // 2, (t % 2) * D:(t % 2 + 1) * D],
                                         oT[:, k, t * P:(t + 1) * P], wp_sb[:, k, :],
                                         start=(k == 0), stop=(k == DC - 1))
                    if t % 2:
                        last.then_inc(proj_full, 1)

            turn_rows(0)
            project(0, True, (*QK, *V))
            with pe.Fori(0, BATCH - 1) as b:
                turn(b, False)
            turn(BATCH - 1, True)

        @block.scalar
        def _(act):
            def project(b, part):
                for m in part:
                    act.wait_ge(misc_full, START + 10 * b + m + 1)
                    src = ps[:, (4 if m < 2 else 6) + m % 2, :]
                    if m == 2:
                        act.wait_ge(qm_ready, START + HEADS * b)
                        act.wait_ge(q2_done, START + 2 * b)
                    if m < 8:
                        dst = (xnT, qT, kT, kyT)[m // 2][:, m % 2, :]
                    else:
                        t = 2 * (m - 8)
                        dst = v[:, t:t + 2, :, 0:HD].rearrange("p t h d -> p (t h) d")
                        src = src.rearrange("p (t d) -> p t d", d=HD)
                    act.activation(dst, src, ACT.Copy).then_inc(misc_read, 1)

            def turn(b, last_turn):
                for h in range(HEADS):
                    act.wait_ge(clip_done, START + HEADS * b + h + 1)
                    if h == 0:
                        act.wait_ge(rx_ready, START + 2 * b)
                    for t in range(TILES):
                        n = (t + 1) * P
                        last = act.activation(scored[:, h % 2, score_place(n)], scored[:, h % 2, score_place(n)], ACT.Exp, scale=0.25,
                                              accum_out=agg[:, t, h:h + 1])
                    last.then_inc(exp_done, 1)

                def head_rows(g):
                    act.wait_ge(av_done, START + 4 * b + g + 1)
                    if g:
                        act.wait_ge(ot_full, START + 4 * b + g)
                    act.activation(headT[:, :], ps[:, 6, :], ACT.Copy).then_inc(headT_ready, 1)

                for h in range(HEADS):
                    act.wait_ge(abs_done, START + HEADS * b + h + 1)
                    if h >= RING:
                        act.wait_ge(av_done, START + 4 * b + (h - RING) // 4 + 1)
                    act.activation(weight[:, h % RING, :], scored[:, h % 2, :], ACT.Ln, bias=1.0).then_inc(ln_done, 1)
                    if h == 4:
                        act.wait_ge(rx_ready, START + 2 * b + 2)
                        act.activation(shift[:, :, :], inv1[:, :, :], ACT.Ln, scale=EPS, bias=1.0)\
                           .then_inc(shift_ready, 1)
                    if h >= 5 and h % 4 == 1:
                        head_rows((h - 5) // 4)
                head_rows(3)
                if not last_turn:
                    project(b + 1, (*XT, *QK))
                act.wait_ge(oT_full, START + b + 1)
                for k in range(DC):
                    act.activation(oT[:, k, :], ps[:, 4 + k, :], ACT.Copy).then_inc(oT_ready, 1)
                if not last_turn:
                    project(b + 1, V)

            project(0, (*XT, *QK, *V))
            with act.Fori(0, BATCH - 1) as b:
                turn(b, False)
            turn(BATCH - 1, True)

        @block.vector
        def _(dve):
            def statistics(b):
                dve.wait_ge(x_loaded, START + 16 * b + 16)
                for t in range(TILES):
                    last = dve.bn_stats(stats[:, t, :], x_in[:, t, :])
                last.then_inc(ln_step, 1)
                dve.wait_ge(ln_step, START + 2 * b + 1)
                apart(dve, c)
                for t in range(TILES):
                    last = dve.bn_aggr(mv[:, t, :], stats[:, t, :])
                last.then_inc(ln_step, 1)
                dve.wait_ge(ln_step, START + 2 * b + 2)
                dve.tensor_scalar(veps[:, :], mv[:, :, 1], LN_EPS, None, ALU.add).then_inc(veps_ready, 1)

            def normalise(b, first):
                dve.wait_ge(rstd_ready, START + b + 1)
                if not first:
                    dve.wait_ge(misc_full, START + 10 * b - 8)
                for t in range(TILES):
                    last = dve.tensor_scalar(xn[:, t, :], x_in[:, t, :], mv[:, t, 0:1], rstd[:, t:t + 1],
                                             ALU.subtract, ALU.mult)
                last.then_inc(xn_ready, 1)

            def turn(b, last_turn):
                def factors(k):
                    heads = slice(k * HPC, (k + 1) * HPC)
                    n = 6 * b + 3 * k
                    dve.wait_ge(exp_done, START + HEADS * b + (k + 1) * HPC)
                    dve.wait_ge(shift_ready, START + b)
                    dve.tensor_scalar(agg1[:, :, heads], agg[:, :, heads], EPS, None, ALU.add).then_inc(agg_step, 1)
                    dve.wait_ge(agg_step, START + n + 1)
                    dve.tensor_scalar(agg2[:, :, heads], agg1[:, :, heads], EPS, None, ALU.add).then_inc(agg_step, 1)
                    dve.reciprocal(inv1[:, :, heads], agg1[:, :, heads])
                    dve.wait_ge(agg_step, START + n + 2)
                    dve.reciprocal(inv2[:, :, heads], agg2[:, :, heads]).then_inc(agg_step, 1)
                    dve.wait_ge(agg_step, START + n + 3)
                    for t in range(TILES):
                        last = dve.tensor_scalar(rx[:, t, heads, :],
                                                 inv2[:, t, heads].unsqueeze(2).broadcast_to([P, HPC, HD]),
                                                 0.25, None, ALU.mult)
                    last.then_inc(rx_ready, 1)

                def scale_q(k):
                    dve.wait_ge(rT_full, START + 2 * b + k + 1)
                    dve.wait_ge(q2m_ready, START + HEADS * b)
                    dve.tensor_tensor(q2T[:, k, :], ps[:, 6 + k, :], qT[:, k, :], ALU.mult).then_inc(q2_done, 1)

                for h in range(HEADS):
                    dve.wait_ge(e_scores, START + HEADS * b + h + 1)
                    if h >= 2:
                        dve.wait_ge(exp_done, START + HEADS * b + h - 1)
                    elif h == 0:
                        dve.wait_ge(exp_done, START + HEADS * b)
                    base = 3 * 512 * (h % 2)
                    dve.scalar_tensor_tensor(out=scored[:, h % 2, :], in0=flat[:, base:base + COLS], scalar=-LIMIT,
                                             in1=cap[:, :], op0=ALU.max, op1=ALU.min).then_inc(clip_done, 1)
                    if h == FACTORS_AT:
                        factors(0)
                    if h == FACTORS_AT + 2:
                        scale_q(0)
                def sums(g):
                    dve.wait_ge(ot_full, START + 4 * b + g + 1)
                    dve.tensor_copy(av[:, :, 4 * g:4 * g + 4, :].rearrange("p t h d -> p t (h d)"),
                                    ps[:, 7, :].rearrange("p (t n) -> p t n", t=TILES)).then_inc(av_read, 1)

                for h in range(HEADS):
                    dve.wait_ge(w_scores, START + HEADS * b + h + 1)
                    if h >= 2:
                        dve.wait_ge(ln_done, START + HEADS * b + h - 1)
                    else:
                        dve.wait_ge(exp_done, START + HEADS * b + HEADS - 1 + h)
                    base = 3 * 512 * (h % 2)
                    dve.tensor_tensor(scored[:, h % 2, :].bitcast(I32), flat[:, base:base + COLS].bitcast(I32),
                                      c["magnitude"][:, :], ALU.bitwise_and).then_inc(abs_done, 1)
                    if h == 1:
                        factors(1)
                    if h == 2:
                        scale_q(1)
                    if h >= 8 and h % 4 == 0:
                        sums((h - 8) // 4)
                    if h == STATS_AT and not last_turn:
                        statistics(b + 1)
                    if h == NORM_AT and not last_turn:
                        normalise(b + 1, False)
                sums(2)
                sums(3)
                dve.wait_ge(shift_ready, START + b + 1)
                for t in range(TILES):
                    n = 4 * (TILES * b + t)
                    dve.wait_ge(cv_full, START + TILES * b + t + 1)
                    dve.tensor_tensor(t1[:, :, :], ps[:, t, 0:HEADS * (HD + 1)].rearrange("p (h d) -> p h d", h=HEADS),
                                      shift[:, t, :].unsqueeze(2).broadcast_to([P, HEADS, HD + 1]),
                                      ALU.mult).then_inc(norm_step, 1)
                    dve.wait_ge(norm_step, START + n + 1)
                    dve.tensor_tensor(t2[:, :, :], t1[:, :, :], av[:, t, :, 0:HD + 1], ALU.add).then_inc(norm_step, 1)
                    dve.wait_ge(norm_step, START + n + 2)
                    dve.tensor_scalar(den[:, :], t2[:, :, HD], EPS, None, ALU.add).then_inc(norm_step, 1)
                    dve.wait_ge(norm_step, START + n + 3)
                    dve.reciprocal(rden[:, :], den[:, :]).then_inc(norm_step, 1)
                    dve.wait_ge(norm_step, START + n + 4)
                    dve.tensor_tensor(o[:, t, :].rearrange("p (h d) -> p h d", h=HEADS), t2[:, :, 0:HD],
                                      rden[:, :].unsqueeze(2).broadcast_to([P, HEADS, HD]),
                                      ALU.mult).then_inc(o_ready, 1)
                dve.wait_ge(xres_loaded, START + 16 * b + 16)
                for k in range(2):
                    dve.wait_ge(proj_full, START + 2 * b + k + 1)
                    dve.tensor_tensor(x_res[:, 2 * k:2 * k + 2, :].rearrange("p t d -> p (t d)"), ps[:, 4 + k, :],
                                      x_res[:, 2 * k:2 * k + 2, :].rearrange("p t d -> p (t d)"),
                                      ALU.add).then_inc(x1_ready, 1)

            statistics(0)
            normalise(0, True)
            with dve.Fori(0, BATCH - 1) as b:
                turn(b, False)
            turn(BATCH - 1, True)


def route(nc, c, tag, x_rows, wg, bg, buf, gates, slots):
    ident, causal = c["ident"], c["causal"]
    ones, upper = causal[:, P:2 * P], causal[:, 0:P]
    groups = NTOK // (TILES * P)
    NT = NTOK // P
    ROWS = 4
    primed = []
    with ExitStack() as ctx:
        def sb(name, shape, dt=F32):
            return ctx.enter_context(nc.sbuf_tensor(f"{tag}_{name}", shape, dt))

        def sem(name, software=False):
            s = ctx.enter_context(nc.semaphore(f"{tag}_{name}"))
            primed.append((s, software))
            return s

        wg_sb = sb("wg", [P, DC, EXPERTS])
        bg_sb = sb("bg", [P, EXPERTS])
        x = sb("x", [P, 2, TILES, D])
        stats = sb("stats", [P, 2, TILES, 6])
        mv = sb("mv", [P, 2, TILES, 2])
        veps = sb("veps", [P, 2, TILES])
        rstd = sb("rstd", [P, 2, TILES])
        zg = sb("zg", [P, 2, TILES, D])
        z = sb("z", [P, NT, D])
        zT = sb("zT", [P, 2, DC, SEQ])
        logit = sb("logit", [P, NT, EXPERTS])
        best = sb("best", [P, NT])
        tied = sb("tied", [P, NT, EXPERTS])
        index = sb("index", [P, NT, EXPERTS])
        from_last = sb("from_last", [P, EXPERTS])
        expert = sb("expert", [P, NT])
        below = sb("below", [P, NT, EXPERTS])
        total = sb("total", [P, NT])
        gate = sb("gate", [P, NT])
        onehot = sb("onehot", [P, NT, EXPERTS])
        before = sb("before", [P, 2, NT + 1, EXPERTS])
        place = sb("place", [P, NT, EXPERTS])
        count = sb("count", [P, NT])
        kept = sb("kept", [P, NT])
        safe = sb("safe", [P, NT])
        slot = sb("slot", [P, NT])
        away = sb("away", [P, NT])
        target = sb("target", [P, NT])
        row = sb("row", [P, ROWS, TILES, D])
        row_target = sb("row_target", [P, ROWS, TILES], U32)
        ps = ctx.enter_context(nc.psum_tensor(f"{tag}_ps", [P, 8, 512], F32))

        weights_in = sem("weights_in")
        x_loaded = [sem(f"x_loaded{u}") for u in range(2)]
        ln_step = sem("ln_step")
        veps_ready = sem("veps_ready")
        rstd_ready = sem("rstd_ready")
        z_ready = sem("z_ready")
        z_kept = sem("z_kept")
        zT_full = sem("zT_full")
        zT_ready = sem("zT_ready")
        logits_full = sem("logits_full")
        logits_ready = sem("logits_ready")
        choice_step = sem("choice_step")
        below_ready = sem("below_ready")
        exp_ready = sem("exp_ready")
        onehot_ready = sem("onehot_ready")
        place_full = sem("place_full")
        row_ready = sem("row_ready")
        target_ready = sem("target_ready")
        row_free = [sem(f"row_free{u}") for u in range(ROWS)]
        spared = sem("spared")
        scattered = [sem(f"scattered{u}", software=True) for u in range(ROWS)]
        prime(nc, primed)
        block = ctx.enter_context(nc.Block())
        x_t = x_rows.rearrange("(g t p) d -> g p t d", p=P, t=TILES)

        @block.sync
        def _(sp):
            sp.dma_start(wg_sb[:, :, :], wg.rearrange("(c p) e -> p c e", p=P)).then_inc(weights_in, 16)
            sp.dma_start(bg_sb[:, :], bg.rearrange("(a e) -> a e", a=1).broadcast_to([P, EXPERTS])).then_inc(weights_in, 16)
            for u in range(2):
                sp.dma_start(x[:, u], x_t[u]).then_inc(x_loaded[u], 16)
            with sp.Fori(0, groups // 2 - 1) as i:
                for u in range(2):
                    sp.wait_ge(z_ready, START + 2 * i + u + 1)
                    sp.dma_start(x[:, u], x_t[bass.ds(2 * i + u + 2, 1)].rearrange("a p t d -> p (a t) d"))\
                      .then_inc(x_loaded[u], 16)

        @block.gpsimd
        def _(pool):
            with pool.Fori(0, groups // 2) as i:
                for u in range(2):
                    pool.wait_ge(veps_ready, START + 2 * i + u + 1)
                    pool.tensor_tensor(rstd[:, u, :], veps[:, u, :], c["power"][:, :], ALU.pow).then_inc(rstd_ready, 1)
                for u in range(2):
                    pool.wait_ge(z_ready, START + 2 * i + u + 1)
                    pool.tensor_copy(z[:, bass.ds((2 * i + u) * TILES, TILES), :].rearrange("p t d -> p (t d)"),
                                     zg[:, u, :, :].rearrange("p t d -> p (t d)")).then_inc(z_kept, 1)

            def sent(i, u):
                pool.wait_ge(scattered[u], 16 * TILES * (i + 1))
                pool.sem_inc(row_free[u], 1)

            with pool.Fori(0, groups // ROWS) as i:
                for u in range(ROWS):
                    pool.wait_ge(row_ready, START + ROWS * i + u + 1)
                    pool.wait_ge(target_ready, START + ROWS * i + u + 1)
                    pool.wait_ge(spared, START + ROWS * i + u)
                    apart(pool, c).then_inc(spared, 1)
                    for t in range(TILES):
                        pool.indirect_dma_start(buf, bass.IndirectOffsetOnAxis(row_target[:, u, t:t + 1], 0),
                                                row[:, u, t, :], None,
                                                bounds_check=NTOK - 1, oob_is_err=False).then_inc(scattered[u], 16)
                    if u:
                        sent(i, u - 1)
                sent(i, ROWS - 1)

        @block.tensor
        def _(pe):
            pe.wait_ge(weights_in, START + 32)
            with pe.Fori(0, groups // 2) as i:
                for u in range(2):
                    pe.wait_ge(z_ready, START + 2 * i + u + 1)
                    pe.wait_ge(zT_ready, START + DC * (2 * i))
                    for k in range(DC):
                        for t in range(TILES):
                            last = pe.transpose(ps[:, DC * u + k, t * P:(t + 1) * P],
                                                zg[:, u, t, k * P:(k + 1) * P], ident[:, :])
                    last.then_inc(zT_full, 1)
                    pe.wait_ge(zT_ready, START + DC * (2 * i + u + 1))
                    pe.wait_ge(logits_ready, START + 2 * i)
                    for t in range(TILES):
                        for k in range(DC):
                            last = pe.matmul(ps[:, 4 + u, t * EXPERTS:(t + 1) * EXPERTS], zT[:, u, k, t * P:(t + 1) * P],
                                             wg_sb[:, k, :], start=(k == 0), stop=(k == DC - 1))
                    last.then_inc(logits_full, 1)
            pe.wait_ge(onehot_ready, START + 1)
            for j, matrix in enumerate((upper, ones)):
                for h in range(2):
                    last = pe.matmul(ps[:, 2 * j + h, :], matrix,
                                     onehot[:, h * NT // 2:(h + 1) * NT // 2, :].rearrange("p t e -> p (t e)"),
                                     start=True, stop=True)
            last.then_inc(place_full, 1)

        @block.scalar
        def _(act):
            with act.Fori(0, groups // 2) as i:
                for u in range(2):
                    act.wait_ge(zT_full, START + 2 * i + u + 1)
                    act.wait_ge(logits_full, START + 2 * i)
                    for k in range(DC):
                        act.activation(zT[:, u, k, :], ps[:, DC * u + k, :], ACT.Copy).then_inc(zT_ready, 1)
                    act.wait_ge(logits_full, START + 2 * i + u + 1)
                    act.activation(logit[:, bass.ds((2 * i + u) * TILES, TILES), :].rearrange("p t e -> p (t e)"),
                                   ps[:, 4 + u, 0:TILES * EXPERTS], ACT.Copy).then_inc(logits_ready, 1)
            act.wait_ge(below_ready, START + 1)
            act.activation(below[:, :, :], below[:, :, :], ACT.Exp).then_inc(exp_ready, 1)
            act.wait_ge(z_kept, START + groups)
            with act.Fori(0, groups // ROWS) as i:
                for u in range(ROWS):
                    act.wait_ge(row_free[u], START + i)
                    act.activation(row[:, u, :, :].rearrange("p t d -> p (t d)"),
                                   z[:, bass.ds((ROWS * i + u) * TILES, TILES), :].rearrange("p t d -> p (t d)"),
                                   ACT.Copy).then_inc(row_ready, 1)

        @block.vector
        def _(dve):
            with dve.Fori(0, groups // 2) as i:
                for u in range(2):
                    dve.wait_ge(x_loaded[u], START + 16 * (i + 1))
                    for t in range(TILES):
                        last = dve.bn_stats(stats[:, u, t, :], x[:, u, t, :])
                    last.then_inc(ln_step, 1)
                    dve.wait_ge(ln_step, START + 4 * i + 2 * u + 1)
                    apart(dve, c)
                    for t in range(TILES):
                        last = dve.bn_aggr(mv[:, u, t, :], stats[:, u, t, :])
                    last.then_inc(ln_step, 1)
                    dve.wait_ge(ln_step, START + 4 * i + 2 * u + 2)
                    dve.tensor_scalar(veps[:, u, :], mv[:, u, :, 1], LN_EPS, None, ALU.add).then_inc(veps_ready, 1)
                for u in range(2):
                    dve.wait_ge(z_kept, START + 2 * i)
                    dve.wait_ge(zT_full, START + 2 * i)
                    dve.wait_ge(rstd_ready, START + 2 * i + u + 1)
                    for t in range(TILES):
                        last = dve.tensor_scalar(zg[:, u, t, :], x[:, u, t, :], mv[:, u, t, 0:1],
                                                 rstd[:, u, t:t + 1], ALU.subtract, ALU.mult)
                    last.then_inc(z_ready, 1)
            done = [0]

            def link(ins):
                done[0] += 1
                ins.then_inc(choice_step, 1)
                dve.wait_ge(choice_step, START + done[0])

            def over_experts(a):
                return a.unsqueeze(2).broadcast_to([P, NT, EXPERTS])

            def over_tiles(a):
                return a.unsqueeze(1).broadcast_to([P, NT, EXPERTS])

            dve.wait_ge(weights_in, START + 32)
            dve.wait_ge(logits_ready, START + groups)
            dve.tensor_scalar(from_last[:, :], c["experts"][:, :], float(EXPERTS), None, ALU.subtract)
            dve.memset(before[:, :, 0, :], 0.0)
            link(dve.tensor_tensor(logit[:, :, :], logit[:, :, :], over_tiles(bg_sb[:, :]), ALU.add))
            link(dve.tensor_reduce(best[:, :], logit[:, :, :], AX.X, ALU.max))
            dve.tensor_tensor(below[:, :, :], logit[:, :, :], over_experts(best[:, :]), ALU.subtract).then_inc(below_ready, 1)
            link(dve.tensor_tensor(tied[:, :, :], logit[:, :, :], over_experts(best[:, :]), ALU.is_equal))
            link(dve.tensor_tensor(index[:, :, :], tied[:, :, :], over_tiles(from_last[:, :]), ALU.mult))
            link(dve.tensor_reduce(safe[:, :], index[:, :, :], AX.X, ALU.min))
            link(dve.tensor_scalar(expert[:, :], safe[:, :], float(EXPERTS), None, ALU.add))
            dve.tensor_tensor(onehot[:, :, :], over_tiles(c["experts"][:, :]), over_experts(expert[:, :]), ALU.is_equal)\
               .then_inc(onehot_ready, 1)
            dve.wait_ge(exp_ready, START + 1)
            link(dve.tensor_reduce(total[:, :], below[:, :, :], AX.X, ALU.add))
            link(dve.reciprocal(gate[:, :], total[:, :]))
            dve.wait_ge(place_full, START + 1)
            link(dve.tensor_copy(before[:, 0, 1:, :].rearrange("p (h t) e -> p h (t e)", h=2), ps[:, 2:4, :]))
            far, src = 1, 0
            while far < NT:
                dve.tensor_copy(before[:, 1 - src, 1:far + 1, :], before[:, src, 1:far + 1, :])
                link(dve.tensor_tensor(before[:, 1 - src, far + 1:, :], before[:, src, far + 1:, :],
                                       before[:, src, 1:NT + 1 - far, :], ALU.add))
                far, src = 2 * far, 1 - src
            link(dve.tensor_tensor(place[:, :, :].rearrange("p (h t) e -> p h (t e)", h=2), ps[:, 0:2, :],
                                   before[:, src, 0:NT, :].rearrange("p (h t) e -> p h (t e)", h=2), ALU.add))
            link(dve.tensor_tensor(tied[:, :, :], place[:, :, :], onehot[:, :, :], ALU.mult))
            link(dve.tensor_reduce(count[:, :], tied[:, :, :], AX.X, ALU.add))
            dve.tensor_scalar(kept[:, :], count[:, :], float(CAP), None, ALU.is_le)
            dve.tensor_scalar(away[:, :], count[:, :], float(CAP), float(2 * NTOK), ALU.is_gt, ALU.mult)
            link(dve.tensor_scalar(safe[:, :], count[:, :], float(CAP), -1.0, ALU.min, ALU.add))
            dve.tensor_tensor(gates[:, :], gate[:, :], kept[:, :], ALU.mult)
            link(dve.scalar_tensor_tensor(out=slot[:, :], in0=expert[:, :], scalar=float(CAP), in1=safe[:, :],
                                          op0=ALU.mult, op1=ALU.add))
            dve.tensor_copy(slots[:, :], slot[:, :])
            link(dve.tensor_tensor(target[:, :], slot[:, :], away[:, :], ALU.add))
            with dve.Fori(0, groups // ROWS) as i:
                for u in range(ROWS):
                    dve.wait_ge(row_free[u], START + i)
                    dve.tensor_copy(row_target[:, u, :], target[:, bass.ds((ROWS * i + u) * TILES, TILES)])\
                       .then_inc(target_ready, 1)


def experts(nc, c, tag, buf, w1, b1, w2, b2, y_rows):
    ident = c["ident"]
    primed = []
    with ExitStack() as ctx:
        def sb(name, shape, dt=F32):
            return ctx.enter_context(nc.sbuf_tensor(f"{tag}_{name}", shape, dt))

        def sem(name, software=False):
            s = ctx.enter_context(nc.semaphore(f"{tag}_{name}"))
            primed.append((s, software))
            return s

        w1_sb = sb("w1", [P, 2, DC, HID])
        w2_sb = sb("w2", [P, 2, HC, D])
        b1_sb = sb("b1", [P, 2, HC])
        b2_sb = sb("b2", [P, 2, D])
        rows = sb("rows", [P, 2, TILES, D])
        rowsT = sb("rowsT", [P, 2, 2, DC, CAP], F32R)
        w1_halves = sb("w1_halves", [P, 2, 2, DC, HID], F32R)
        hT = sb("hT", [P, 2, HC, CAP])
        y = sb("y", [P, 2, TILES, D])
        ps = ctx.enter_context(nc.psum_tensor(f"{tag}_ps", [P, 8, 512], F32))
        loaded = [sem(f"loaded{u}") for u in range(2)]
        rowsT_full = sem("rowsT_full")
        rowsT_ready = sem("rowsT_ready")
        rowsT_low = sem("rowsT_low")
        w1_step = sem("w1_step")
        h_full = sem("h_full")
        h_ready = sem("h_ready")
        y_full = sem("y_full")
        y_ready = sem("y_ready")
        y_stored = [sem(f"y_stored{u}") for u in range(2)]
        prime(nc, primed)
        block = ctx.enter_context(nc.Block())
        buf_t = buf.rearrange("(e t p) d -> e p t d", p=P, t=TILES)
        y_t = y_rows.rearrange("(e t p) d -> e p t d", p=P, t=TILES)
        w1_t = w1.rearrange("e (c p) h -> e p c h", p=P)
        w2_t = w2.rearrange("e (j p) d -> e p j d", p=P)
        LOADS = 5

        @block.sync
        def _(sp):
            def load(e, u):
                for dst, src in ((rows[:, u], buf_t[bass.ds(e, 1)].rearrange("a p t d -> p (a t) d")),
                                 (w1_sb[:, u], w1_t[bass.ds(e, 1)].rearrange("a p c h -> p (a c) h")),
                                 (b1_sb[:, u], b1[bass.ds(e, 1)].rearrange("a p j -> p (a j)")),
                                 (w2_sb[:, u], w2_t[bass.ds(e, 1)].rearrange("a p j d -> p (a j) d")),
                                 (b2_sb[:, u], b2[bass.ds(e, 1), :].broadcast_to([P, D]))):
                    sp.dma_start(dst, src).then_inc(loaded[u], 16)

            def store(e, u):
                sp.wait_ge(y_ready, START + TILES * (e + 1))
                sp.dma_start(y_t[bass.ds(e, 1)].rearrange("a p t d -> p (a t) d"), y[:, u]).then_inc(y_stored[u], 16)

            for u in range(2):
                load(u, u)
            with sp.Fori(0, EXPERTS // 2 - 1) as i:
                for u in range(2):
                    store(2 * i + u, u)
                    load(2 * i + u + 2, u)
            for u in range(2):
                store(EXPERTS - 2 + u, u)
            for u in range(2):
                sp.wait_ge(y_stored[u], START + 16 * EXPERTS // 2)

        @block.gpsimd
        def _(pool):
            def split(e, u, n):
                pool.wait_ge(loaded[u], START + 16 * LOADS * n)
                apart(pool, c)
                whole = w1_sb[:, u].rearrange("p c h -> p (c h)")
                high, low = (w1_halves[:, u, half].rearrange("p c h -> p (c h)") for half in range(2))
                pool.tensor_copy(high, whole).then_inc(w1_step, 1)
                pool.wait_ge(w1_step, START + 2 * e + 1)
                pool.tensor_tensor(low, whole, high, ALU.subtract).then_inc(w1_step, 1)

            for u in range(2):
                split(u, u, 1)
            with pool.Fori(0, EXPERTS // 2 - 1) as i:
                for u in range(2):
                    pool.wait_ge(h_full, START + HC * (2 * i + u + 1))
                    split(2 * i + u + 2, u, i + 2)

        def experts_in_turn(eng, first, turn):
            first(0, 0, 1)
            with eng.Fori(0, EXPERTS // 2 - 1) as i:
                turn(2 * i, 0, i + 1, True)
                turn(2 * i + 1, 1, i + 1, True)
            turn(EXPERTS - 2, 0, EXPERTS // 2, True)
            turn(EXPERTS - 1, 1, EXPERTS // 2, False)

        @block.tensor
        def _(pe):
            def turn_rows(e, u, n):
                pe.wait_ge(loaded[u], START + 16 * LOADS * n)
                pe.wait_ge(rowsT_low, START + 2 * e)
                for k in range(DC):
                    for t in range(TILES):
                        last = pe.transpose(ps[:, k, t * P:(t + 1) * P], rows[:, u, t, k * P:(k + 1) * P], ident[:, :])
                last.then_inc(rowsT_full, 1)

            def turn(e, u, n, more):
                pe.wait_ge(rowsT_low, START + 2 * e + 2)
                pe.wait_ge(w1_step, START + 2 * e + 2)
                for j in range(HC):
                    if j < 4:
                        pe.wait_ge(h_ready, START + HC * e)
                    else:
                        pe.wait_ge(h_ready, START + HC * e + j - 3)
                    terms = [(a, b, k) for a, b in ((0, 0), (0, 1), (1, 0)) for k in range(DC)]
                    for a, b, k in terms:
                        last = pe.matmul(ps[:, 2 + j % 4, :], w1_halves[:, u, a, k, j * P:(j + 1) * P],
                                         rowsT[:, u, b, k, :], start=((a, b, k) == terms[0]), stop=((a, b, k) == terms[-1]))
                    last.then_inc(h_full, 1)
                if more:
                    turn_rows(e + 1, 1 - u, n + u)
                pe.wait_ge(h_ready, START + HC * (e + 1))
                for t in range(TILES):
                    if t < 2:
                        pe.wait_ge(y_ready, START + TILES * e)
                    else:
                        pe.wait_ge(y_ready, START + TILES * e + t - 1)
                    for j in range(HC):
                        last = pe.matmul(ps[:, 6 + t % 2, 0:D], hT[:, u, j, t * P:(t + 1) * P], w2_sb[:, u, j, :],
                                         start=(j == 0), stop=(j == HC - 1))
                    last.then_inc(y_full, 1)

            experts_in_turn(pe, turn_rows, turn)

        @block.scalar
        def _(act):
            def high_rows(e, u, n):
                act.wait_ge(rowsT_full, START + e + 1)
                for k in range(DC):
                    act.activation(rowsT[:, u, 0, k, :], ps[:, k, :], ACT.Copy).then_inc(rowsT_ready, 1)

            def turn(e, u, n, more):
                for j in range(HC):
                    act.wait_ge(h_full, START + HC * e + j + 1)
                    if j == 0:
                        act.wait_ge(loaded[u], START + 16 * LOADS * n)
                    act.activation(hT[:, u, j, :], ps[:, 2 + j % 4, :], ACT.Relu, bias=b1_sb[:, u, j:j + 1])\
                       .then_inc(h_ready, 1)
                if more:
                    high_rows(e + 1, 1 - u, n + u)

            experts_in_turn(act, high_rows, turn)

        @block.vector
        def _(dve):
            def low_rows(e, u, n):
                for k in range(DC):
                    dve.wait_ge(rowsT_ready, START + 2 * e + k + 1)
                    dve.tensor_tensor(rowsT[:, u, 1, k, :], ps[:, k, :], rowsT[:, u, 0, k, :], ALU.subtract)\
                       .then_inc(rowsT_low, 1)

            def turn(e, u, n, more):
                if more:
                    low_rows(e + 1, 1 - u, n + u)
                dve.wait_ge(loaded[u], START + 16 * LOADS * n)
                dve.wait_ge(y_stored[u], START + 16 * (n - 1))
                for t in range(TILES):
                    dve.wait_ge(y_full, START + TILES * e + t + 1)
                    dve.tensor_tensor(y[:, u, t, :], ps[:, 6 + t % 2, 0:D], b2_sb[:, u, :], ALU.add)\
                       .then_inc(y_ready, 1)

            experts_in_turn(dve, low_rows, turn)


def combine_out(nc, c, x_rows, y_rows, gates, slots, out):
    groups = NTOK // (TILES * P)
    primed = []
    with ExitStack() as ctx:
        def sb(name, shape, dt=F32):
            return ctx.enter_context(nc.sbuf_tensor(f"c_{name}", shape, dt))

        def sem(name, software=False):
            s = ctx.enter_context(nc.semaphore(f"c_{name}"))
            primed.append((s, software))
            return s

        x = sb("x", [P, 2, TILES, D])
        y = sb("y", [P, 2, TILES, D])
        s = sb("s", [P, 2, TILES, D])
        slot = sb("slot", [P, 2, TILES], U32)
        loaded = [sem(f"loaded{u}") for u in range(2)]
        gathered = [sem(f"gathered{u}", software=True) for u in range(2)]
        stored = [sem(f"stored{u}") for u in range(2)]
        slot_ready = sem("slot_ready")
        summed = sem("summed")
        spared = sem("spared")
        prime(nc, primed)
        block = ctx.enter_context(nc.Block())
        x_t = x_rows.rearrange("(g t p) d -> g p t d", p=P, t=TILES)
        out_t = out.rearrange("g (t p) d -> g p t d", p=P)

        @block.sync
        def _(sp):
            with sp.Fori(0, groups // 2) as i:
                for u in range(2):
                    sp.wait_ge(summed, START + 2 * i)
                    sp.dma_start(x[:, u], x_t[bass.ds(2 * i + u, 1)].rearrange("a p t d -> p (a t) d"))\
                      .then_inc(loaded[u], 16)

        @block.scalar
        def _(act):
            with act.Fori(0, groups // 2) as i:
                for u in range(2):
                    act.wait_ge(summed, START + 2 * i + u + 1)
                    act.dma_start(out_t[bass.ds(2 * i + u, 1)].rearrange("a p t d -> p (a t) d"), s[:, u])\
                       .then_inc(stored[u], 16)
            for u in range(2):
                act.wait_ge(stored[u], START + 16 * (groups // 2))

        @block.gpsimd
        def _(pool):
            with pool.Fori(0, groups // 2) as i:
                for u in range(2):
                    pool.wait_ge(summed, START + 2 * i)
                    pool.wait_ge(slot_ready, START + 2 * i + u + 1)
                    pool.wait_ge(spared, START + 2 * i + u)
                    apart(pool, c).then_inc(spared, 1)
                    for t in range(TILES):
                        pool.indirect_dma_start(y[:, u, t, :], None, y_rows,
                                                bass.IndirectOffsetOnAxis(slot[:, u, t:t + 1], 0),
                                                bounds_check=NTOK - 1, oob_is_err=False).then_inc(gathered[u], 16)

        @block.vector
        def _(dve):
            with dve.Fori(0, groups // 2) as i:
                for u in range(2):
                    dve.tensor_copy(slot[:, u, :], slots[:, bass.ds((2 * i + u) * TILES, TILES)]).then_inc(slot_ready, 1)
                for u in range(2):
                    dve.wait_ge(loaded[u], START + 16 * (i + 1))
                    dve.wait_ge(gathered[u], 16 * TILES * (i + 1))
                    dve.wait_ge(stored[u], START + 16 * i)
                    for t in range(TILES):
                        last = dve.scalar_tensor_tensor(out=s[:, u, t, :], in0=y[:, u, t, :],
                                                        scalar=gates[:, bass.ds((2 * i + u) * TILES + t, 1)],
                                                        in1=x[:, u, t, :], op0=ALU.mult, op1=ALU.add)
                    last.then_inc(summed, 1)


def settle(nc, c, x_rows, y_rows, gates, slots, norm_w, b_out, xr_rows, hT_d):
    ident = c["ident"]
    groups = NTOK // SEQ
    primed = []
    with ExitStack() as ctx:
        def sb(name, shape, dt=F32):
            return ctx.enter_context(nc.sbuf_tensor(f"n_{name}", shape, dt))

        def sem(name, software=False):
            s = ctx.enter_context(nc.semaphore(f"n_{name}"))
            primed.append((s, software))
            return s

        x = sb("x", [P, 2, TILES, D])
        y = sb("y", [P, 2, TILES, D])
        x2 = sb("x2", [P, TILES, D])
        res = sb("res", [P, TILES, D])
        h = sb("h", [P, TILES, D])
        hT = sb("hT", [P, DC, SEQ])
        xr = sb("xr", [P, TILES, D])
        xb = sb("xb", [P, TILES, D])
        nw = sb("nw", [P, DC])
        bo = sb("bo", [P, D])
        slot = sb("slot", [P, 2, TILES], U32)
        stats = sb("stats", [P, 2, TILES, 6])
        mv = sb("mv", [P, 2, TILES, 2])
        veps = sb("veps", [P, 2, TILES])
        square = sb("square", [P, TILES])
        meansq = sb("meansq", [P, TILES])
        rstd = sb("rstd", [P, 2, TILES])
        ps = ctx.enter_context(nc.psum_tensor("n_ps", [P, 2, 512], F32))
        weights_in = sem("weights_in")
        x_loaded = [sem(f"x_loaded{u}") for u in range(2)]
        slot_ready = sem("slot_ready")
        gathered = [sem(f"gathered{u}", software=True) for u in range(2)]
        dve_step = sem("dve_step")
        x2_ready = sem("x2_ready")
        veps_ready = sem("veps_ready")
        rstd_ready = sem("rstd_ready")
        h_ready = sem("h_ready")
        hT_full = sem("hT_full")
        hT_ready = sem("hT_ready")
        xr_ready = sem("xr_ready")
        xb_ready = sem("xb_ready")
        xb_stored = sem("xb_stored")
        hT_stored = sem("hT_stored")
        spared = sem("spared")
        prime(nc, primed)
        block = ctx.enter_context(nc.Block())
        x_t = x_rows.rearrange("(g t p) d -> g p t d", p=P, t=TILES)
        xr_t = xr_rows.rearrange("(g t p) d -> g p t d", p=P, t=TILES)

        @block.sync
        def _(sp):
            sp.dma_start(nw[:, :], norm_w).then_inc(weights_in, 16)
            sp.dma_start(bo[:, :], b_out.rearrange("(a e) -> a e", a=1).broadcast_to([P, D])).then_inc(weights_in, 16)

            def load(g, u):
                sp.dma_start(x[:, u], x_t[bass.ds(g, 1)].rearrange("a p t d -> p (a t) d")).then_inc(x_loaded[u], 16)

            def store(g):
                sp.wait_ge(xb_ready, START + g + 1)
                sp.dma_start(xr_t[bass.ds(g, 1)].rearrange("a p t d -> p (a t) d"), xb[:, :, :]).then_inc(xb_stored, 16)

            load(0, 0)
            load(1, 1)
            with sp.Fori(0, groups // 2 - 1) as i:
                for u in range(2):
                    sp.wait_ge(x2_ready, START + 2 * i + u + 1)
                    load(2 * i + u + 2, u)
                    store(2 * i + u)
            for u in range(2):
                store(groups - 2 + u)
            sp.wait_ge(xb_stored, START + 16 * groups)

        @block.gpsimd
        def _(pool):
            pool.wait_ge(weights_in, START + 32)

            def gather(g, u):
                pool.wait_ge(slot_ready, START + g + 1)
                pool.wait_ge(spared, START + g)
                apart(pool, c).then_inc(spared, 1)
                for t in range(TILES):
                    pool.indirect_dma_start(y[:, u, t, :], None, y_rows,
                                            bass.IndirectOffsetOnAxis(slot[:, u, t:t + 1], 0),
                                            bounds_check=NTOK - 1, oob_is_err=False).then_inc(gathered[u], 16)

            def turn(g, u, last):
                if not last:
                    gather(g + 1, 1 - u)
                for k in range(2):
                    pool.wait_ge(veps_ready, START + 2 * g + k + 1)
                    pool.tensor_tensor(rstd[:, k, :], veps[:, k, :], c["power"][:, :], ALU.pow).then_inc(rstd_ready, 1)
                pool.wait_ge(xr_ready, START + g + 1)
                pool.wait_ge(xb_stored, START + 16 * g)
                pool.tensor_tensor(xb[:, :, :], xr[:, :, :], bo[:, :].unsqueeze(1).broadcast_to([P, TILES, D]),
                                   ALU.add).then_inc(xb_ready, 1)

            gather(0, 0)
            with pool.Fori(0, groups // 2 - 1) as i:
                for u in range(2):
                    turn(2 * i + u, u, False)
            for u in range(2):
                turn(groups - 2 + u, u, u == 1)

        @block.tensor
        def _(pe):
            with pe.Fori(0, groups) as g:
                pe.wait_ge(h_ready, START + g + 1)
                pe.wait_ge(hT_ready, START + 2 * g)
                for k in range(DC):
                    for t in range(TILES):
                        last = pe.transpose(ps[:, k, t * P:(t + 1) * P], h[:, t, k * P:(k + 1) * P], ident[:, :])
                last.then_inc(hT_full, 1)

        @block.scalar
        def _(act):
            act.wait_ge(weights_in, START + 32)
            with act.Fori(0, groups) as g:
                act.wait_ge(hT_full, START + g + 1)
                act.wait_ge(hT_stored, START + 16 * g)
                for k in range(DC):
                    act.activation(hT[:, k, :], ps[:, k, :], ACT.Copy, scale=nw[:, k:k + 1]).then_inc(hT_ready, 1)
                act.wait_ge(hT_ready, START + 2 * g + 2)
                act.dma_start(hT_d[:, :, bass.ds(g * SEQ, SEQ)], hT[:, :, :]).then_inc(hT_stored, 16)
            act.wait_ge(hT_stored, START + 16 * groups)

        @block.vector
        def _(dve):
            steps = 6

            def take_slots(g, u):
                dve.tensor_copy(slot[:, u, :], slots[:, bass.ds(g * TILES, TILES)]).then_inc(slot_ready, 1)

            def turn(g, u, n, last_turn):
                done = [0]

                def link(ins, alone=False):
                    done[0] += 1
                    ins.then_inc(dve_step, 1)
                    dve.wait_ge(dve_step, START + steps * g + done[0])
                    if alone:
                        apart(dve, c)

                if not last_turn:
                    take_slots(g + 1, 1 - u)
                dve.wait_ge(h_ready, START + g)
                dve.wait_ge(x_loaded[u], START + 16 * n)
                dve.wait_ge(gathered[u], 16 * TILES * n)
                for t in range(TILES):
                    last = dve.scalar_tensor_tensor(out=x2[:, t, :], in0=y[:, u, t, :], scalar=gates[:, bass.ds(g * TILES + t, 1)],
                                                    in1=x[:, u, t, :], op0=ALU.mult, op1=ALU.add)
                last.then_inc(x2_ready, 1)
                dve.wait_ge(x2_ready, START + g + 1)
                for t in range(TILES):
                    last = dve.bn_stats(stats[:, 0, t, :], x2[:, t, :])
                link(last, alone=True)
                for t in range(TILES):
                    last = dve.bn_aggr(mv[:, 0, t, :], stats[:, 0, t, :])
                link(last)
                dve.tensor_scalar(veps[:, 0, :], mv[:, 0, :, 1], LN_EPS, None, ALU.add).then_inc(veps_ready, 1)
                dve.wait_ge(rstd_ready, START + 2 * g + 1)
                for t in range(TILES):
                    last = dve.tensor_scalar(res[:, t, :], x2[:, t, :], mv[:, 0, t, 0:1], rstd[:, 0, t:t + 1],
                                             ALU.subtract, ALU.mult)
                link(last)
                for t in range(TILES):
                    last = dve.bn_stats(stats[:, 1, t, :], res[:, t, :])
                link(last, alone=True)
                for t in range(TILES):
                    last = dve.bn_aggr(mv[:, 1, t, :], stats[:, 1, t, :])
                link(last)
                link(dve.tensor_tensor(square[:, :], mv[:, 1, :, 0], mv[:, 1, :, 0], ALU.mult))
                dve.scalar_tensor_tensor(out=veps[:, 1, :], in0=mv[:, 1, :, 1], scalar=EPS, in1=square[:, :],
                                         op0=ALU.add, op1=ALU.add).then_inc(veps_ready, 1)
                dve.wait_ge(xb_ready, START + g)
                dve.tensor_tensor(xr[:, :, :], x2[:, :, :], res[:, :, :], ALU.add).then_inc(xr_ready, 1)
                dve.wait_ge(rstd_ready, START + 2 * g + 2)
                dve.wait_ge(hT_full, START + g)
                for t in range(TILES):
                    last = dve.tensor_scalar(h[:, t, :], res[:, t, :], rstd[:, 1, t:t + 1], None, ALU.mult)
                last.then_inc(h_ready, 1)
                assert done[0] == steps, done

            take_slots(0, 0)
            with dve.Fori(0, groups // 2 - 1) as i:
                for u in range(2):
                    turn(2 * i + u, u, i + 1, False)
            for u in range(2):
                turn(groups - 2 + u, u, groups // 2, u == 1)


def state_space(nc, c, hT_d, win, b_in, conv_w, conv_b, a_bd, at_bd, b_bd, b_col, c_col, yT_d):
    ident, head_of, group_of = c["ident"], c["head_of"], c["group_of"]
    YB = 8
    primed = []
    with ExitStack() as ctx:
        def sb(name, shape, dt=F32):
            return ctx.enter_context(nc.sbuf_tensor(f"s_{name}", shape, dt))

        def sem(name, software=False):
            s = ctx.enter_context(nc.semaphore(f"s_{name}"))
            primed.append((s, software))
            return s

        win_sb = sb("win", [P, DC, P])
        bias = sb("bias", [P, 2])
        taps = sb("taps", [P, KW])
        pw = sb("pw", [P, NPAIR, P + CHUNK])
        qv = sb("qv", [P, NPAIR, CHUNK + P])
        cb = sb("cb", [P, 2, NPAIR])
        at = sb("at", [P, NPAIR, P])
        bb = sb("bb", [P, NPAIR, 8])
        wo = sb("wo", [P, NPAIR, CHUNK])
        k_sb = sb("k", [8, NPAIR, CHUNK])
        zero = sb("zero", [P, CHUNK])
        tc_rev = sb("tc_rev", [P, CHUNK, CHUNK])
        tc_sb = sb("tc", [P, CHUNK, CHUNK])
        tbd = sb("tbd", [P, CHUNK, P])
        obd = sb("obd", [P, CHUNK, P])
        rbd = sb("rbd", [P, CHUNK, P])
        hb = sb("hb", [P, 2, DC, SEQ])
        upad = sb("upad", [P, 2, KW - 1 + SEQ])
        acc = sb("acc", [P, SEQ])
        ut = sb("ut", [P, CHUNK, NCH, BATCH])
        xs = sb("xs", [P, NPAIR, NCH, BATCH])
        yts = sb("yts", [P, YB, SEQ])
        ps = ctx.enter_context(nc.psum_tensor("s_ps", [P, 8, 512], F32))
        kpad = nc.dram_tensor("s_kpad", (GRP, NPAIR, 2, 2 * CHUNK), F32, kind="Internal").ap()

        zeroed = sem("zeroed")
        kpad_zero = sem("kpad_zero")
        loaded = sem("loaded")
        hb_loaded = [sem(f"hb_loaded{u}") for u in range(2)]
        first_ready = sem("first_ready")
        proj_full = sem("proj_full")
        u_ready = sem("u_ready")
        conv_step = sem("conv_step")
        ut_ready = sem("ut_ready")
        ring_full = sem("ring_full")
        act_read = sem("act_read")
        dve_read = sem("dve_read")
        k_stored = sem("k_stored")
        tc_loaded = sem("tc_loaded")
        tc_turned = sem("tc_turned")
        v_spread = sem("v_spread")
        o_spread = sem("o_spread")
        t_spread = sem("t_spread")
        yt_ready = sem("yt_ready")
        y_stored = [sem(f"y_stored{u}") for u in range(YB)]
        prime(nc, primed)
        block = ctx.enter_context(nc.Block())

        groups = [range(3 * g, min(3 * g + 3, NPAIR)) for g in range((NPAIR + 2) // 3)]
        uses, reader = [], []

        def plan(key, who):
            uses.append(key)
            reader.append(who)

        for level in range(5):
            for g in range(len(groups)):
                plan(("P", level, g), "act")
                plan(("Q", level, g), "act")
        plan(("O",), "act")
        plan(("K",), "act")
        for n in range(8):
            plan(("R", n), "act")
        for n in range(8):
            plan(("S", n), "act")
        for s in range(4):
            for n in range(8):
                plan(("X", s, n), "dve")
            if s < 3:
                for g in range(len(groups)):
                    plan(("P", 5 + s, g), "act")
                    if s < 2:
                        plan(("Q", 5 + s, g), "act")
        for n in range(NPAIR):
            plan(("Y", n), "act" if n % 2 else "dve")
        NU = len(uses)
        number = {key: n for n, key in enumerate(uses)}
        read_by = [reader[:n + 1].count(reader[n]) for n in range(NU)]
        NA, ND = reader.count("act"), reader.count("dve")
        reads = {"act": (act_read, NA), "dve": (dve_read, ND)}

        def bank(key):
            return 2 + number[key] % 6

        def wait_read(eng, q, key):
            n = number[key]
            s, per = reads[reader[n]]
            eng.wait_ge(s, START + per * q + read_by[n])

        def spread(eng, out, src, mask):
            return eng.tensor_tensor(out.rearrange("p i (g t) -> p i g t", g=GRP),
                                     src.unsqueeze(2).broadcast_to([P, src.shape[1], GRP, CHUNK]),
                                     mask.unsqueeze(1).unsqueeze(3).broadcast_to([P, src.shape[1], GRP, CHUNK]),
                                     ALU.mult)

        @block.sync
        def _(sp):
            sp.wait_ge(zeroed, START + 2)
            rows = kpad.rearrange("g p j n -> (g p j) n")
            sp.dma_start(rows[:, 0:CHUNK], zero[:, :]).then_inc(kpad_zero, 16)
            sp.wait_ge(kpad_zero, START + 16)

            def load(q):
                one = bass.ds(q, 1)
                for dst, src in ((pw[:, :, 0:P], a_bd[one].rearrange("a p i n -> p (a i) n")),
                                 (qv[:, :, CHUNK:], at_bd[one].rearrange("a p i n -> p (a i) n")),
                                 (at[:, :, :], at_bd[one].rearrange("a p i n -> p (a i) n")),
                                 (cb[:, 0, :], c_col[one].rearrange("a p i -> p (a i)")),
                                 (cb[:, 1, :], b_col[one].rearrange("a p i -> p (a i)")),
                                 (bb[:, :, :], b_bd[one].rearrange("a p i n -> p (a i) n")),
                                 (win_sb[:, :, :], win[one].rearrange("a p c n -> p (a c) n")),
                                 (bias[:, 0:1], b_in[one].rearrange("a p n -> p (a n)")),
                                 (bias[:, 1:2], conv_b[one].rearrange("a p n -> p (a n)")),
                                 (taps[:, :], conv_w[one].rearrange("a p n -> p (a n)"))):
                    sp.dma_start(dst, src).then_inc(loaded, 16)

            def rows_of(b):
                sp.dma_start(hb[:, b % 2], hT_d[:, :, b * SEQ:(b + 1) * SEQ]).then_inc(hb_loaded[b % 2], 16)

            def turn(q, last):
                for b in range(2, BATCH):
                    sp.wait_ge(proj_full, START + BATCH * q + b - 1)
                    rows_of(b)
                wait_read(sp, q, ("K",))
                for j in range(2):
                    sp.dma_start(kpad[:, :, j, CHUNK:], k_sb[GRP * j:GRP * (j + 1)]).then_inc(k_stored, 16)
                sp.wait_ge(k_stored, START + 32 * q + 32)
                for g in range(GRP):
                    src = bass.AP(kpad.tensor, g * CHUNK * 2 * CHUNK + 1,
                                  [[1, CHUNK], [2 * CHUNK, CHUNK], [1, CHUNK]])
                    sp.dma_start(tc_rev[CHUNK * g:CHUNK * (g + 1)], src).then_inc(tc_loaded, 16)
                if not last:
                    sp.wait_ge(ring_full, START + NU * q + number[("X", 3, 7)] + 1)
                    for b in range(2):
                        rows_of(b)
                    load(q + 1)
                for b in range(BATCH):
                    sp.wait_ge(yt_ready, START + BATCH * q + b + 1)
                    sp.dma_start(yT_d[bass.ds(q, 1), :, b * SEQ:(b + 1) * SEQ].rearrange("a p n -> p (a n)"),
                                 yts[:, b % YB, :]).then_inc(y_stored[b % YB], 16)

            load(0)
            for b in range(2):
                rows_of(b)
            with sp.Fori(0, QC - 1) as q:
                turn(q, False)
            turn(QC - 1, True)
            for u in range(YB):
                sp.wait_ge(y_stored[u], START + 16 * QC * BATCH // YB)

        @block.gpsimd
        def _(pool):
            pool.memset(zero[:, :], 0.0).then_inc(zeroed, 1)
            pool.memset(upad[:, :, 0:KW - 1], 0.0).then_inc(zeroed, 1)

            with pool.Fori(0, QC) as q:
                wait_read(pool, q, ("Q", 4, len(groups) - 1))
                for j in range(2):
                    last = spread(pool, tbd[:, j::2, :], qv[:, :, 0:CHUNK], head_of[:, GRP * j:GRP * (j + 1)])
                last.then_inc(v_spread, 1)
                wait_read(pool, q, ("O",))
                for j in range(2):
                    last = spread(pool, obd[:, j::2, :], wo[:, :, :], head_of[:, GRP * j:GRP * (j + 1)])
                last.then_inc(o_spread, 1)
                wait_read(pool, q, ("R", 7))
                pool.wait_ge(tc_turned, START + q + 1)
                spread(pool, tbd[:, :, :], tc_sb[:, :, :], group_of[:, :]).then_inc(t_spread, 1)

        @block.tensor
        def _(pe):
            pe.wait_ge(zeroed, START + 2)
            with pe.Fori(0, QC) as q:
                pe.wait_ge(loaded, START + 160 * q + 160)
                pe.wait_ge(first_ready, START + 2 * q + 2)
                pe.wait_ge(act_read, START + NA * q)
                pe.wait_ge(dve_read, START + ND * q)

                def begin(key):
                    n = number[key]
                    if n >= 6:
                        wait_read(pe, q, uses[n - 6])
                    return bank(key)

                def project(b):
                    pe.wait_ge(hb_loaded[b % 2], START + 16 * (BATCH // 2) * q + 16 * (b // 2 + 1))
                    if b >= 2:
                        pe.wait_ge(u_ready, START + BATCH * q + b - 1)
                    else:
                        pe.wait_ge(u_ready, START + BATCH * q)
                    for k in range(DC):
                        last = pe.matmul(ps[:, b % 2, :], win_sb[:, k, :], hb[:, b % 2, k, :],
                                         start=(k == 0), stop=(k == DC - 1))
                    last.then_inc(proj_full, 1)

                def square(level, g):
                    w = 2 ** level if level < 5 else 0
                    if level:
                        wait_read(pe, q, ("Q", level - 1, g))
                    for side in "PQ":
                        key = (side, level, g)
                        if key not in number:
                            continue
                        bk = begin(key)
                        for n, p in enumerate(groups[g]):
                            if side == "P":
                                stay, move = qv[:, p, CHUNK:], pw[:, p, 0:P + w]
                            else:
                                stay, move = pw[:, p, 0:P], qv[:, p, CHUNK - w:]
                            last = pe.matmul(ps[:, bk, n * (P + w):(n + 1) * (P + w)], stay, move,
                                             start=True, stop=True)
                        last.then_inc(ring_full, 1)

                steps = [(level, g) for level in range(5) for g in range(len(groups))]
                for b in range(BATCH):
                    project(b)
                    for level, g in steps[2 * b:2 * b + 2]:
                        square(level, g)
                wait_read(pe, q, ("Q", 4, len(groups) - 1))
                bk = begin(("O",))
                for p in range(NPAIR):
                    last = pe.matmul(ps[:, bk, p * CHUNK:(p + 1) * CHUNK], at[:, p, :], pw[:, p, P:],
                                     start=True, stop=True)
                last.then_inc(ring_full, 1)
                bk = begin(("K",))
                for p in range(NPAIR):
                    last = pe.matmul(ps[0:8, bk, p * CHUNK:(p + 1) * CHUNK], bb[:, p, :], pw[:, p, P:],
                                     start=True, stop=True)
                last.then_inc(ring_full, 1)
                pe.wait_ge(v_spread, START + q + 1)
                for n in range(8):
                    bk = begin(("R", n))
                    for i in range(4):
                        last = pe.transpose(ps[:, bk, i * P:(i + 1) * P], tbd[:, 4 * n + i, :], ident[:, :])
                    last.then_inc(ring_full, 1)
                pe.wait_ge(ut_ready, START + BATCH * (q + 1))
                per = NCH * BATCH
                for n in range(8):
                    if n == 0:
                        wait_read(pe, q, ("R", 7))
                    bk = begin(("S", n))
                    for m in range(2):
                        for j in range(2):
                            i = 2 * (2 * n + m) + j
                            last = pe.matmul(ps[:, bk, m * per:(m + 1) * per], rbd[:, i, :],
                                             ut[:, i, :, :].rearrange("p c b -> p (c b)"), start=(j == 0), stop=(j == 1))
                    last.then_inc(ring_full, 1)
                for s in range(4):
                    far = 2 ** s
                    for n in range(8):
                        wait_read(pe, q, ("X", s - 1, n) if s else ("S", n))
                        bk = begin(("X", s, n))
                        for m in range(2):
                            last = pe.matmul(ps[:, bk, m * per:m * per + (NCH - far) * BATCH], pw[:, 2 * n + m, 0:P],
                                             xs[:, 2 * n + m, 0:NCH - far, :].rearrange("p c b -> p (c b)"),
                                             start=True, stop=True)
                        last.then_inc(ring_full, 1)
                    if s < 3:
                        for g in range(len(groups)):
                            square(5 + s, g)
                        wait_read(pe, q, ("P", 5 + s, len(groups) - 1))
                pe.wait_ge(t_spread, START + q + 1)
                pe.wait_ge(o_spread, START + q + 1)
                wait_read(pe, q, ("X", 3, 7))
                for n in range(NPAIR):
                    bk = begin(("Y", n))
                    for j in range(2):
                        i = 2 * n + j
                        pe.matmul(ps[:, bk, j * per:(j + 1) * per], tbd[:, i, :],
                                  ut[:, i, :, :].rearrange("p c b -> p (c b)"), start=True, stop=False)
                        last = pe.matmul(ps[:, bk, j * per + BATCH:(j + 1) * per], obd[:, i, :],
                                         xs[:, n, 0:NCH - 1, :].rearrange("p c b -> p (c b)"), start=False, stop=True)
                    last.then_inc(ring_full, 1)

        def full(eng, q, key):
            eng.wait_ge(ring_full, START + NU * q + number[key] + 1)

        @block.scalar
        def _(act):
            with act.Fori(0, QC) as q:
                act.wait_ge(loaded, START + 160 * q + 160)
                act.wait_ge(o_spread, START + q)
                act.activation(pw[:, :, P], cb[:, 0, :], ACT.Copy).then_inc(first_ready, 1)
                act.activation(qv[:, :, CHUNK - 1], cb[:, 1, :], ACT.Copy).then_inc(first_ready, 1)
                act.wait_ge(k_stored, START + 32 * q)

                def take(b):
                    act.wait_ge(proj_full, START + BATCH * q + b + 1)
                    if b >= 2:
                        act.wait_ge(ut_ready, START + BATCH * q + b - 1)
                    act.activation(upad[:, b % 2, KW - 1:], ps[:, b % 2, :], ACT.Identity, bias=bias[:, 0:1])\
                       .then_inc(u_ready, 1)

                def squared(level, g):
                    w = 2 ** level if level < 5 else 0
                    a, z = groups[g][0], groups[g][-1] + 1
                    full(act, q, ("Q", level, g) if ("Q", level, g) in number else ("P", level, g))
                    for side in "PQ":
                        key = (side, level, g)
                        if key not in number:
                            continue
                        src = ps[:, bank(key), 0:(z - a) * (P + w)].rearrange("p (i n) -> p i n", n=P + w)
                        if side == "P":
                            if w:
                                act.activation(pw[:, a:z, P + w:P + 2 * w], src[:, :, P:], ACT.Copy)
                            last = act.activation(pw[:, a:z, 0:P], src[:, :, 0:P], ACT.Copy)
                        else:
                            if w:
                                act.activation(qv[:, a:z, CHUNK - 2 * w:CHUNK - w], src[:, :, 0:w], ACT.Copy)
                            last = act.activation(qv[:, a:z, CHUNK:], src[:, :, w:], ACT.Copy)
                        last.then_inc(act_read, 1)

                steps = [(level, g) for level in range(5) for g in range(len(groups))]
                for b in range(BATCH):
                    take(b)
                    for level, g in steps[2 * b:2 * b + 2]:
                        squared(level, g)
                full(act, q, ("O",))
                act.activation(wo[:, :, :].rearrange("p i n -> p (i n)"), ps[:, bank(("O",)), :], ACT.Copy)\
                   .then_inc(act_read, 1)
                full(act, q, ("K",))
                act.activation(k_sb[:, :, :].rearrange("p i n -> p (i n)"), ps[0:8, bank(("K",)), :], ACT.Copy)\
                   .then_inc(act_read, 1)
                for n in range(8):
                    full(act, q, ("R", n))
                    act.activation(rbd[:, 4 * n:4 * n + 4, :].rearrange("p i n -> p (i n)"), ps[:, bank(("R", n)), :],
                                   ACT.Copy).then_inc(act_read, 1)
                for n in range(8):
                    full(act, q, ("S", n))
                    act.activation(xs[:, 2 * n:2 * n + 2, :, :].rearrange("p i c b -> p (i c b)"),
                                   ps[:, bank(("S", n)), :], ACT.Copy).then_inc(act_read, 1)
                for s in range(3):
                    for g in range(len(groups)):
                        squared(5 + s, g)
                for n in range(1, NPAIR, 2):
                    full(act, q, ("Y", n))
                    act.activation(ut[:, 2 * n:2 * n + 2, :, :].rearrange("p i c b -> p (i c b)"),
                                   ps[:, bank(("Y", n)), :], ACT.Copy).then_inc(act_read, 1)

        @block.vector
        def _(dve):
            dve.wait_ge(zeroed, START + 2)
            with dve.Fori(0, QC) as q:
                dve.wait_ge(loaded, START + 160 * q + 160)
                for b in range(BATCH):
                    dve.wait_ge(u_ready, START + BATCH * q + b + 1)
                    dve.wait_ge(ut_ready, START + BATCH * q + b)
                    u = upad[:, b % 2, :]
                    dve.tensor_scalar(acc[:, :], u[:, KW - 1:], taps[:, KW - 1:KW], bias[:, 1:2], ALU.mult, ALU.add)\
                       .then_inc(conv_step, 1)
                    for k in range(1, KW):
                        dve.wait_ge(conv_step, START + KW * (BATCH * q + b) + k)
                        dve.scalar_tensor_tensor(out=acc[:, :], in0=u[:, KW - 1 - k:KW - 1 - k + SEQ],
                                                 scalar=taps[:, KW - 1 - k:KW - k], in1=acc[:, :],
                                                 op0=ALU.mult, op1=ALU.add).then_inc(conv_step, 1)
                    dve.wait_ge(conv_step, START + KW * (BATCH * q + b) + KW)
                    dve.transpose(ut[:, :, :, b].rearrange("p i c -> p c i"),
                                  acc[:, :].rearrange("p (c t) -> p c t", t=CHUNK)).then_inc(ut_ready, 1)
                dve.wait_ge(tc_loaded, START + 16 * GRP * (q + 1))
                dve.wait_ge(t_spread, START + q)
                apart(dve, c)
                dve.stream_shuffle(tc_sb[:, :, :].rearrange("p i t -> p (i t)"),
                                   tc_rev[:, :, :].rearrange("p i t -> p (i t)"),
                                   mask=[CHUNK - 1 - k for k in range(CHUNK)]).then_inc(tc_turned, 1)
                for s in range(4):
                    far = 2 ** s
                    n_cols = (NCH - far) * BATCH
                    for n in range(8):
                        full(dve, q, ("X", s, n))
                        src = ps[:, bank(("X", s, n)), :].rearrange("p (i n) -> p i n", i=2)[:, :, 0:n_cols]
                        dst = xs[:, 2 * n:2 * n + 2, far:, :].rearrange("p i c b -> p i (c b)")
                        dve.tensor_tensor(dst, src, dst, ALU.add).then_inc(dve_read, 1)
                for n in range(0, NPAIR, 2):
                    full(dve, q, ("Y", n))
                    dve.tensor_copy(ut[:, 2 * n:2 * n + 2, :, :].rearrange("p i c b -> p (i c b)"),
                                    ps[:, bank(("Y", n)), :]).then_inc(dve_read, 1)
                wait_read(dve, q, ("Y", NPAIR - 1))
                wait_read(dve, q, ("Y", NPAIR - 2))
                for b in range(BATCH):
                    dve.wait_ge(y_stored[b % YB], START + 16 * (BATCH // YB) * q + 16 * (b // YB))
                    dve.transpose(yts[:, b % YB, :].rearrange("p (c t) -> p c t", t=CHUNK),
                                  ut[:, :, :, b].rearrange("p i c -> p c i")).then_inc(yt_ready, 1)
                dve.wait_ge(yt_ready, START + BATCH * (q + 1))


def project_out(nc, yT_d, wout, xr_rows, x3_rows):
    primed = []
    with ExitStack() as ctx:
        def sb(name, shape, dt=F32):
            return ctx.enter_context(nc.sbuf_tensor(f"o_{name}", shape, dt))

        def sem(name, software=False):
            s = ctx.enter_context(nc.semaphore(f"o_{name}"))
            primed.append((s, software))
            return s

        w = sb("w", [P, QC, D])
        yT = sb("yT", [P, 2, QC, SEQ])
        xr = sb("xr", [P, 2, TILES, D])
        x3 = sb("x3", [P, 2, TILES, D])
        ps = ctx.enter_context(nc.psum_tensor("o_ps", [P, 8, 512], F32))
        weights_in = sem("weights_in")
        loaded = [sem(f"loaded{u}") for u in range(2)]
        stored = [sem(f"stored{u}") for u in range(2)]
        full = sem("full")
        summed = sem("summed")
        prime(nc, primed)
        block = ctx.enter_context(nc.Block())
        xr_t = xr_rows.rearrange("(g t p) d -> g p t d", p=P, t=TILES)
        x3_t = x3_rows.rearrange("(g t p) d -> g p t d", p=P, t=TILES)
        y_t = yT_d.rearrange("q p (g n) -> g p q n", n=SEQ)

        @block.sync
        def _(sp):
            sp.dma_start(w[:, :, :], wout.rearrange("(q p) d -> p q d", p=P)).then_inc(weights_in, 16)

            def load(g, u):
                one = bass.ds(g, 1)
                sp.dma_start(yT[:, u], y_t[one].rearrange("a p q n -> p (a q) n")).then_inc(loaded[u], 16)
                sp.dma_start(xr[:, u], xr_t[one].rearrange("a p t d -> p (a t) d")).then_inc(loaded[u], 16)

            def store(g, u):
                sp.wait_ge(summed, START + TILES * (g + 1))
                sp.dma_start(x3_t[bass.ds(g, 1)].rearrange("a p t d -> p (a t) d"), x3[:, u]).then_inc(stored[u], 16)

            for u in range(2):
                load(u, u)
            with sp.Fori(0, BATCH // 2 - 1) as i:
                for u in range(2):
                    store(2 * i + u, u)
                    load(2 * i + u + 2, u)
            for u in range(2):
                store(BATCH - 2 + u, u)
            for u in range(2):
                sp.wait_ge(stored[u], START + 16 * BATCH // 2)

        @block.tensor
        def _(pe):
            pe.wait_ge(weights_in, START + 16)
            with pe.Fori(0, BATCH // 2) as i:
                for u in range(2):
                    pe.wait_ge(loaded[u], START + 32 * (i + 1))
                    pe.wait_ge(summed, START + TILES * 2 * i)
                    for t in range(TILES):
                        for k in range(QC):
                            last = pe.matmul(ps[:, TILES * u + t, 0:D], yT[:, u, k, t * P:(t + 1) * P], w[:, k, :],
                                             start=(k == 0), stop=(k == QC - 1))
                        last.then_inc(full, 1)

        @block.vector
        def _(dve):
            with dve.Fori(0, BATCH // 2) as i:
                for u in range(2):
                    dve.wait_ge(loaded[u], START + 32 * (i + 1))
                    dve.wait_ge(stored[u], START + 16 * i)
                    for t in range(TILES):
                        dve.wait_ge(full, START + TILES * (2 * i + u) + t + 1)
                        dve.tensor_tensor(x3[:, u, t, :], ps[:, TILES * u + t, 0:D], xr[:, u, t, :], ALU.add)\
                           .then_inc(summed, 1)


def copy_rows(nc, src, dst):
    with nc.semaphore("filled") as filled, nc.Block() as block:
        @block.sync
        def _(sp):
            sp.dma_start(dst, src).then_inc(filled, 16)
            sp.wait_ge(filled, 16)


def hybrid_block(nc, x, w_qkv, w_ky, w_proj, norm_w, win, b_in, conv_w, conv_b, a_bd, at_bd, b_bd, b_col, c_col,
                 wout, b_out, wg, bg, w1, b1, w2, b2, out):
    def dram(name, shape):
        return nc.dram_tensor(name, shape, F32, kind="Internal").ap()

    x1 = dram("x1", (NTOK, D))
    xr = dram("xr", (NTOK, D))
    x3 = dram("x3", (NTOK, D))
    rows = dram("rows", (NTOK, D))
    y = dram("y", (NTOK, D))
    hT = dram("hT", (P, DC, NTOK))
    yT = dram("yT", (QC, P, NTOK))
    with ExitStack() as ctx:
        def sb(name, shape, dt):
            return ctx.enter_context(nc.sbuf_tensor(name, shape, dt))

        c = constants(nc, sb)
        gates = sb("gates", [P, NTOK // P], F32)
        slots = sb("slots", [P, NTOK // P], U32)
        copy_rows(nc, x.rearrange("b s d -> (b s) d"), rows)
        attention(nc, c, x, w_qkv, w_ky, w_proj, x1)
        route(nc, c, "r1", x1, wg, bg, rows, gates, slots)
        experts(nc, c, "e1", rows, w1, b1, w2, b2, y)
        settle(nc, c, x1, y, gates, slots, norm_w, b_out, xr, hT)
        state_space(nc, c, hT, win, b_in, conv_w, conv_b, a_bd, at_bd, b_bd, b_col, c_col, yT)
        project_out(nc, yT, wout, xr, x3)
        route(nc, c, "r2", x3, wg, bg, rows, gates, slots)
        experts(nc, c, "e2", rows, w1, b1, w2, b2, y)
        combine_out(nc, c, x3, y, gates, slots, out)


def layouts(i):
    import numpy as np

    def groups(a):
        a = a.reshape(QC, GRP, NPAIR, 2, *a.shape[1:])
        return a.transpose(0, 2, 3, 1, *range(4, a.ndim)).reshape(QC, NPAIR, 8, *a.shape[4:])

    def diagonal(a):
        q, p, e, n, m = a.shape
        out = np.zeros((q, e, n, p, e, m), a.dtype)
        for k in range(e):
            out[:, k, :, :, k, :] = a[:, :, k].transpose(0, 2, 1, 3)
        return out.reshape(q, e * n, p, e * m)

    A = groups(i["L0_attn_b_A"])
    B = groups(i["L0_attn_b_Bm"])
    C = groups(i["L0_attn_b_Cm"].transpose(0, 2, 1))

    def column(a):
        return a.reshape(QC, NPAIR, P).transpose(0, 2, 1)

    return {
        "x": i["L0_attn_a_x"],
        "w_qkv": i["L0_attn_a_w_qkv"].T,
        "w_ky": i["L0_attn_a_w_ky"].T,
        "w_proj": i["L0_attn_a_w_proj"].T,
        "norm_w": i["L0_attn_b_norm_w"].reshape(DC, P).T,
        "win": i["L0_attn_b_Win"].reshape(DC, P, QC, P).transpose(2, 1, 0, 3),
        "b_in": i["L0_attn_b_b_in"].reshape(QC, P, 1),
        "conv_w": i["L0_attn_b_conv_w"].reshape(QC, P, KW),
        "conv_b": i["L0_attn_b_conv_b"].reshape(QC, P, 1),
        "a_bd": diagonal(A),
        "at_bd": diagonal(A.transpose(0, 1, 2, 4, 3)),
        "b_bd": diagonal(B),
        "b_col": column(B),
        "c_col": column(C),
        "wout": i["L0_attn_b_Wout"],
        "b_out": i["L0_attn_b_b_out"],
        "wg": i["L0_ffn_Wg"],
        "bg": i["L0_ffn_bg"],
        "w1": i["L0_ffn_W1"],
        "b1": i["L0_ffn_b1"].reshape(EXPERTS, HC, P).transpose(0, 2, 1),
        "w2": i["L0_ffn_W2"],
        "b2": i["L0_ffn_b2"],
    }


def kernel(**inputs):
    import numpy as np
    import concourse.bacc as bacc
    from concourse.bass_utils import run_bass_kernel_spmd

    nc = bacc.Bacc("TRN2", target_bir_lowering=False, num_devices=1)
    arrays, args = {}, {}
    for name, a in layouts({k: np.asarray(v) for k, v in inputs.items()}).items():
        a = np.ascontiguousarray(a)
        arrays[f"in_{name}"] = a
        args[name] = nc.dram_tensor(f"in_{name}", a.shape, mybir.dt.from_np(a.dtype), kind="ExternalInput").ap()
    out = nc.dram_tensor("out", (BATCH, SEQ, D), F32, kind="ExternalOutput").ap()
    hybrid_block(nc, out=out, **args)
    r = run_bass_kernel_spmd(nc, [arrays], core_ids=[0])
    return r.results[0]["out"]
```
